# Optimizing a Trainium2 kernel written in Bass

```python
import numpy as np
import jax
import jax.numpy as jnp

def _softmax(x, axis=-1):
    return jax.nn.softmax(x, axis=axis)

def _gelu(x):
    return jax.nn.gelu(x, approximate=True)

def _silu(x):
    return jax.nn.silu(x)

def _sigmoid(x):
    return jax.nn.sigmoid(x)

def _layernorm(x, axis=-1, eps=1e-05):
    m = jnp.mean(x, axis=axis, keepdims=True)
    v = jnp.var(x, axis=axis, keepdims=True)
    return (x - m) / jnp.sqrt(v + eps)

def _scatter_add(tgt, idx, src, axis=0):
    return tgt.at[idx].add(src)

def _segment_sum(src, seg, n):
    return jax.ops.segment_sum(src, seg, n)
kernel_name = 'mk_conv_preact_d4_conv_nchw128_r4_27c86f'

def setup_inputs(seed: int=0):
    np.random.seed(seed)
    _w = jnp.asarray

    def _rec_inputs():
        import jax
        import jax.numpy as jnp
        _gk = jax.random.key(seed)
        x = -0.0003929 + 0.9999 * jax.random.normal(jax.random.fold_in(_gk, 1), (2, 32, 64, 64), jnp.float32)
        return x
    x = _rec_inputs()

    def _L0_conv_setup():
        import jax, jax.numpy as jnp
        import numpy as np
        C = 32
        Y_ANCHORS = 16
        X_ANCHORS = 16
        H = 64
        W = 64

        def _cubic(t):
            a = -0.75
            at = jnp.abs(t)
            near = ((a + 2.0) * at - (a + 3.0)) * at * at + 1.0
            far = (((at - 5.0) * at + 8.0) * at - 4.0) * a
            return jnp.where(at <= 1.0, near, jnp.where(at < 2.0, far, 0.0))

        def _bicubic_weight_matrix(out_size, in_size):
            scale = in_size / out_size
            src = (jnp.arange(out_size, dtype=jnp.float32) + 0.5) * scale - 0.5
            i0 = jnp.floor(src)
            t = src - i0
            offs = jnp.arange(-1, 3)
            w = _cubic(t[:, None] - offs[None, :].astype(jnp.float32))
            idx = jnp.clip(i0[:, None].astype(jnp.int32) + offs[None, :], 0, in_size - 1)
            Wm = jnp.zeros((out_size, in_size), jnp.float32)
            return Wm.at[jnp.arange(out_size)[:, None], idx].add(w)
        key = jax.random.key(seed)
        k1, k2, k3 = jax.random.split(key, 3)
        x = jax.random.normal(k1, (2, C, H, W), jnp.float32)
        mean_table = jax.random.normal(k2, (Y_ANCHORS, X_ANCHORS, C), jnp.float32)
        std_table = jax.random.uniform(k3, (Y_ANCHORS, X_ANCHORS, C), jnp.float32) + 0.5
        weight = jnp.ones((1, C, 1, 1), jnp.float32)
        bias = jnp.zeros((1, C, 1, 1), jnp.float32)
        return {'x': x, 'mean_table': mean_table, 'std_table': std_table, 'weight': weight, 'bias': bias, 'y_anchor': 4, 'x_anchor': 5, 'pre_y1_anchor': 5, 'pre_x1_anchor': 6}
    _L0_conv_all = _L0_conv_setup()
    _L0_conv_in = {k: v for k, v in _L0_conv_all.items() if k in ('mean_table', 'std_table', 'weight', 'bias')}
    del _L0_conv_all

    def _L1_conv_setup():
        import jax, jax.numpy as jnp
        import numpy as np
        from jax import lax
        EPS_NORM = 1e-12
        KS = 3
        K2 = KS * KS
        MIN_CONN, MAX_CONN = (1, 8)
        NUM_GROUPS = 16
        GN_EPS = 1e-05

        def _unfold3x3_reflect(x):
            B, C, H, W = x.shape
            p = jnp.pad(x, ((0, 0), (0, 0), (1, 1), (1, 1)), mode='reflect')
            pats = [p[:, :, dy:dy + H, dx:dx + W] for dy in range(KS) for dx in range(KS)]
            return jnp.stack(pats, axis=2)

        def _df_counts(x):
            B = x.shape[0]
            avg = jnp.mean(x, axis=1, keepdims=True)
            kern = jnp.array([[0.0, -1.0, 0.0], [-1.0, 4.0, -1.0], [0.0, -1.0, 0.0]], dtype=x.dtype).reshape(1, 1, 3, 3)
            df = jnp.abs(lax.conv_general_dilated(avg, kern, window_strides=(1, 1), padding=((1, 1), (1, 1)), dimension_numbers=('NCHW', 'OIHW', 'NCHW')))
            dmin = df.reshape(B, -1).min(axis=1).reshape(B, 1, 1, 1)
            dmax = df.reshape(B, -1).max(axis=1).reshape(B, 1, 1, 1)
            dn = (df - dmin) / (dmax - dmin + 1e-08)
            return MIN_CONN + jnp.round(dn * (MAX_CONN - MIN_CONN))

        def _group_norm(x, w, b):
            B, C, H, W = x.shape
            g = x.reshape(B, NUM_GROUPS, -1)
            mu = g.mean(-1, keepdims=True)
            var = g.var(-1, keepdims=True)
            g = (g - mu) * lax.rsqrt(var + GN_EPS)
            return g.reshape(B, C, H, W) * w[None, :, None, None] + b[None, :, None, None]
        key = jax.random.key(seed)
        ks = jax.random.split(key, 7)
        B, C, H, W = (8, 32, 24, 24)
        return {'x': jax.random.normal(ks[0], (B, C, H, W), jnp.float32), 'gn_weight': jax.random.uniform(ks[1], (C,), jnp.float32, 0.5, 1.5), 'gn_bias': jax.random.normal(ks[2], (C,), jnp.float32) * 0.1, 'w1': jax.random.normal(ks[3], (2 * C, C), jnp.float32) * 0.02, 'b1': jax.random.normal(ks[4], (2 * C,), jnp.float32) * 0.02, 'w2': jax.random.normal(ks[5], (C, 2 * C), jnp.float32) * 0.02, 'b2': jax.random.normal(ks[6], (C,), jnp.float32) * 0.02}
    _L1_conv_all = _L1_conv_setup()
    _L1_conv_in = {k: v for k, v in _L1_conv_all.items() if k in ('gn_weight', 'gn_bias', 'w1', 'b1', 'w2', 'b2')}
    del _L1_conv_all

    def _L2_conv_setup():
        import jax, jax.numpy as jnp
        import numpy as np
        DIM, D_STATE, D_CONV, EXPAND = (32, 16, 4, 2)
        D_INNER = EXPAND * DIM
        DT_RANK = (DIM + 15) // 16

        def _mamba(xn, W_in, conv_w, conv_b, W_xproj, W_dt, b_dt, A_log, D, W_out):
            Bsz, L, _ = xn.shape
            d_inner, d_conv = conv_w.shape
            d_state = A_log.shape[1]
            dt_rank = W_dt.shape[1]
            xz = xn @ W_in.T
            xin, z = jnp.split(xz, 2, axis=-1)
            xc = jnp.swapaxes(xin, 1, 2)
            xc = jax.lax.conv_general_dilated(xc, conv_w[:, None, :], window_strides=(1,), padding=[(d_conv - 1, 0)], feature_group_count=d_inner)
            xc = xc + conv_b[None, :, None]
            u = jax.nn.silu(jnp.swapaxes(xc, 1, 2))
            x_dbl = u @ W_xproj.T
            dt, Bm, Cm = jnp.split(x_dbl, [dt_rank, dt_rank + d_state], axis=-1)
            delta = jax.nn.softplus(dt @ W_dt.T + b_dt)
            A = -jnp.exp(A_log)

            def step(h, xs):
                d_t, B_t, C_t, u_t = xs
                dA = jnp.exp(d_t[..., None] * A)
                h = dA * h + (d_t * u_t)[..., None] * B_t[:, None, :]
                y = jnp.einsum('bdn,bn->bd', h, C_t)
                return (h, y)
            xs = (jnp.swapaxes(delta, 0, 1), jnp.swapaxes(Bm, 0, 1), jnp.swapaxes(Cm, 0, 1), jnp.swapaxes(u, 0, 1))
            h0 = jnp.zeros((Bsz, d_inner, d_state), delta.dtype)
            _, ys = jax.lax.scan(step, h0, xs)
            y = jnp.swapaxes(ys, 0, 1) + u * D
            y = y * jax.nn.silu(z)
            return y @ W_out.T
        key = jax.random.key(seed)
        ks = jax.random.split(key, 8)
        B, H, W = (4, 32, 32)
        x = jax.random.normal(ks[0], (B, DIM, H, W), dtype=jnp.float32)
        W_in = jax.random.normal(ks[1], (2 * D_INNER, DIM)) / np.sqrt(DIM)
        conv_w = jax.random.normal(ks[2], (D_INNER, D_CONV)) / np.sqrt(D_CONV)
        conv_b = jnp.zeros((D_INNER,), jnp.float32)
        W_xproj = jax.random.normal(ks[3], (DT_RANK + 2 * D_STATE, D_INNER)) / np.sqrt(D_INNER)
        W_dt = jax.random.normal(ks[4], (D_INNER, DT_RANK)) / np.sqrt(DT_RANK)
        b_dt = jax.random.normal(ks[5], (D_INNER,)) * 0.1
        A_log = jnp.log(jnp.tile(jnp.arange(1, D_STATE + 1, dtype=jnp.float32), (D_INNER, 1)))
        Dskip = jnp.ones((D_INNER,), jnp.float32)
        W_out = jax.random.normal(ks[6], (DIM, D_INNER)) / np.sqrt(D_INNER)
        return {'x': x, 'ln_w': jnp.ones((DIM,), jnp.float32), 'ln_b': jnp.zeros((DIM,), jnp.float32), 'W_in': W_in, 'conv_w': conv_w, 'conv_b': conv_b, 'W_xproj': W_xproj, 'W_dt': W_dt, 'b_dt': b_dt, 'A_log': A_log, 'D': Dskip, 'W_out': W_out}
    _L2_conv_all = _L2_conv_setup()
    _L2_conv_in = {k: v for k, v in _L2_conv_all.items() if k in ('ln_w', 'ln_b', 'W_in', 'conv_w', 'conv_b', 'W_xproj', 'W_dt', 'b_dt', 'A_log', 'D', 'W_out')}
    del _L2_conv_all

    def _L3_conv_setup():
        import jax, jax.numpy as jnp
        import numpy as np
        KH, KW = (3, 3)
        SH, SW = (1, 1)
        PH, PW = (1, 1)
        DH, DW = (1, 1)
        DG = 1

        def _conv(x, w):
            return jax.lax.conv_general_dilated(x, w, window_strides=(SH, SW), padding=((PH, PH), (PW, PW)), rhs_dilation=(DH, DW), dimension_numbers=('NCHW', 'OIHW', 'NCHW'))

        def _deform_im2col(data_im, offset, mask):
            B, C, H, W = data_im.shape
            K = KH * KW
            Ho, Wo = (offset.shape[2], offset.shape[3])
            Cg = C // DG
            off = offset.reshape(B, DG, K, 2, Ho, Wo)
            off_y, off_x = (off[:, :, :, 0], off[:, :, :, 1])
            msk = mask.reshape(B, DG, 1, K, Ho, Wo)
            gi = jnp.repeat(jnp.arange(KH), KW)
            gj = jnp.tile(jnp.arange(KW), KH)
            base_y = (jnp.arange(Ho) * SH - PH)[None, :] + (gi * DH)[:, None]
            base_x = (jnp.arange(Wo) * SW - PW)[None, :] + (gj * DW)[:, None]
            y = base_y[None, None, :, :, None].astype(off_y.dtype) + off_y
            x = base_x[None, None, :, None, :].astype(off_x.dtype) + off_x
            y0 = jnp.floor(y)
            x0 = jnp.floor(x)
            ly = y - y0
            lx = x - x0
            y0i = y0.astype(jnp.int32)
            x0i = x0.astype(jnp.int32)
            y1i = y0i + 1
            x1i = x0i + 1
            flat = data_im.reshape(B, DG, Cg, H * W)

            def gather(yi, xi):
                valid = (yi >= 0) & (yi < H) & (xi >= 0) & (xi < W)
                idx = jnp.clip(yi, 0, H - 1) * W + jnp.clip(xi, 0, W - 1)
                idxf = idx.reshape(B, DG, 1, -1)
                g = jnp.take_along_axis(flat, jnp.broadcast_to(idxf, (B, DG, Cg, idxf.shape[-1])), axis=-1)
                g = g.reshape(B, DG, Cg, K, Ho, Wo)
                return g * valid[:, :, None].astype(g.dtype)
            w00 = ((1 - ly) * (1 - lx))[:, :, None]
            w01 = ((1 - ly) * lx)[:, :, None]
            w10 = (ly * (1 - lx))[:, :, None]
            w11 = (ly * lx)[:, :, None]
            val = w00 * gather(y0i, x0i) + w01 * gather(y0i, x1i) + w10 * gather(y1i, x0i) + w11 * gather(y1i, x1i)
            val = val * msk
            return val.reshape(B, C * K, Ho, Wo)
        key = jax.random.key(seed)
        k1, k2, k3, k4 = jax.random.split(key, 4)
        B, C, H, W = (8, 32, 16, 16)
        Cout = 32
        data_im = jax.random.normal(k1, (B, C, H, W), dtype=jnp.float32)
        weight = jax.random.normal(k2, (Cout, C * KH * KW), dtype=jnp.float32) * (2.0 / (C * KH * KW)) ** 0.5
        offset_w = jax.random.normal(k3, (2 * DG * KH * KW, C, KH, KW), dtype=jnp.float32) * 0.1
        mask_w = jax.random.normal(k4, (DG * KH * KW, C, KH, KW), dtype=jnp.float32) * 0.1
        return {'data_im': data_im, 'weight': weight, 'offset_w': offset_w, 'mask_w': mask_w}
    _L3_conv_all = _L3_conv_setup()
    _L3_conv_in = {k: v for k, v in _L3_conv_all.items() if k in ('weight', 'offset_w', 'mask_w')}
    del _L3_conv_all
    return {'x': x, 'L0_conv_mean_table': _L0_conv_in['mean_table'], 'L0_conv_std_table': _L0_conv_in['std_table'], 'L0_conv_weight': _L0_conv_in['weight'], 'L0_conv_bias': _L0_conv_in['bias'], 'L1_conv_gn_weight': _L1_conv_in['gn_weight'], 'L1_conv_gn_bias': _L1_conv_in['gn_bias'], 'L1_conv_w1': _L1_conv_in['w1'], 'L1_conv_b1': _L1_conv_in['b1'], 'L1_conv_w2': _L1_conv_in['w2'], 'L1_conv_b2': _L1_conv_in['b2'], 'L2_conv_ln_w': _L2_conv_in['ln_w'], 'L2_conv_ln_b': _L2_conv_in['ln_b'], 'L2_conv_W_in': _L2_conv_in['W_in'], 'L2_conv_conv_w': _L2_conv_in['conv_w'], 'L2_conv_conv_b': _L2_conv_in['conv_b'], 'L2_conv_W_xproj': _L2_conv_in['W_xproj'], 'L2_conv_W_dt': _L2_conv_in['W_dt'], 'L2_conv_b_dt': _L2_conv_in['b_dt'], 'L2_conv_A_log': _L2_conv_in['A_log'], 'L2_conv_D': _L2_conv_in['D'], 'L2_conv_W_out': _L2_conv_in['W_out'], 'L3_conv_weight': _L3_conv_in['weight'], 'L3_conv_offset_w': _L3_conv_in['offset_w'], 'L3_conv_mask_w': _L3_conv_in['mask_w']}

def reference(x, L0_conv_mean_table, L0_conv_std_table, L0_conv_weight, L0_conv_bias, L1_conv_gn_weight, L1_conv_gn_bias, L1_conv_w1, L1_conv_b1, L1_conv_w2, L1_conv_b2, L2_conv_ln_w, L2_conv_ln_b, L2_conv_W_in, L2_conv_conv_w, L2_conv_conv_b, L2_conv_W_xproj, L2_conv_W_dt, L2_conv_b_dt, L2_conv_A_log, L2_conv_D, L2_conv_W_out, L3_conv_weight, L3_conv_offset_w, L3_conv_mask_w):
    import jax
    import jax.numpy as jnp

    def _L0_conv_ref(x, mean_table, std_table, weight, bias, y_anchor, x_anchor, pre_y1_anchor, pre_x1_anchor):
        import jax, jax.numpy as jnp
        import numpy as np
        C = 32
        Y_ANCHORS = 16
        X_ANCHORS = 16
        H = 64
        W = 64

        def _cubic(t):
            a = -0.75
            at = jnp.abs(t)
            near = ((a + 2.0) * at - (a + 3.0)) * at * at + 1.0
            far = (((at - 5.0) * at + 8.0) * at - 4.0) * a
            return jnp.where(at <= 1.0, near, jnp.where(at < 2.0, far, 0.0))

        def _bicubic_weight_matrix(out_size, in_size):
            scale = in_size / out_size
            src = (jnp.arange(out_size, dtype=jnp.float32) + 0.5) * scale - 0.5
            i0 = jnp.floor(src)
            t = src - i0
            offs = jnp.arange(-1, 3)
            w = _cubic(t[:, None] - offs[None, :].astype(jnp.float32))
            idx = jnp.clip(i0[:, None].astype(jnp.int32) + offs[None, :], 0, in_size - 1)
            Wm = jnp.zeros((out_size, in_size), jnp.float32)
            return Wm.at[jnp.arange(out_size)[:, None], idx].add(w)
        real_x, pre_x = jnp.split(x, 2, axis=0)
        h, w = (real_x.shape[2], real_x.shape[3])
        n = h * w
        pre_mean = jnp.mean(pre_x, axis=(2, 3))
        pre_var = jnp.sum((pre_x - pre_mean[:, :, None, None]) ** 2, axis=(2, 3)) / (n - 1)
        pre_std = jnp.sqrt(pre_var)
        mean_table = mean_table.at[pre_y1_anchor, pre_x1_anchor].set(pre_mean[0])
        std_table = std_table.at[pre_y1_anchor, pre_x1_anchor].set(pre_std[0])
        pm = jnp.pad(mean_table, ((1, 2), (1, 2), (0, 0)), mode='edge')
        ps = jnp.pad(std_table, ((1, 2), (1, 2), (0, 0)), mode='edge')
        mean_patch = jax.lax.dynamic_slice(pm, (y_anchor, x_anchor, 0), (4, 4, C))
        std_patch = jax.lax.dynamic_slice(ps, (y_anchor, x_anchor, 0), (4, 4, C))
        Wy = _bicubic_weight_matrix(3 * h, 4)[h // 2:h // 2 + h]
        Wx = _bicubic_weight_matrix(3 * w, 4)[w // 2:w // 2 + w]
        mean_map = jnp.einsum('oy,yxc,px->cop', Wy, mean_patch, Wx)[None]
        stdinv_map = jnp.einsum('oy,yxc,px->cop', Wy, 1.0 / std_patch, Wx)[None]
        real = (real_x - mean_map) * stdinv_map * weight + bias
        pre = (pre_x - pre_mean[:, :, None, None]) / pre_std[:, :, None, None] * weight + bias
        return jnp.concatenate([real, pre], axis=0)

    def _L1_conv_ref(x, gn_weight, gn_bias, w1, b1, w2, b2):
        import jax, jax.numpy as jnp
        import numpy as np
        from jax import lax
        EPS_NORM = 1e-12
        KS = 3
        K2 = KS * KS
        MIN_CONN, MAX_CONN = (1, 8)
        NUM_GROUPS = 16
        GN_EPS = 1e-05

        def _unfold3x3_reflect(x):
            B, C, H, W = x.shape
            p = jnp.pad(x, ((0, 0), (0, 0), (1, 1), (1, 1)), mode='reflect')
            pats = [p[:, :, dy:dy + H, dx:dx + W] for dy in range(KS) for dx in range(KS)]
            return jnp.stack(pats, axis=2)

        def _df_counts(x):
            B = x.shape[0]
            avg = jnp.mean(x, axis=1, keepdims=True)
            kern = jnp.array([[0.0, -1.0, 0.0], [-1.0, 4.0, -1.0], [0.0, -1.0, 0.0]], dtype=x.dtype).reshape(1, 1, 3, 3)
            df = jnp.abs(lax.conv_general_dilated(avg, kern, window_strides=(1, 1), padding=((1, 1), (1, 1)), dimension_numbers=('NCHW', 'OIHW', 'NCHW')))
            dmin = df.reshape(B, -1).min(axis=1).reshape(B, 1, 1, 1)
            dmax = df.reshape(B, -1).max(axis=1).reshape(B, 1, 1, 1)
            dn = (df - dmin) / (dmax - dmin + 1e-08)
            return MIN_CONN + jnp.round(dn * (MAX_CONN - MIN_CONN))

        def _group_norm(x, w, b):
            B, C, H, W = x.shape
            g = x.reshape(B, NUM_GROUPS, -1)
            mu = g.mean(-1, keepdims=True)
            var = g.var(-1, keepdims=True)
            g = (g - mu) * lax.rsqrt(var + GN_EPS)
            return g.reshape(B, C, H, W) * w[None, :, None, None] + b[None, :, None, None]
        B, C, H, W = x.shape
        P = H * W
        counts = lax.stop_gradient(_df_counts(x))
        kvals = jnp.minimum(counts, K2).astype(jnp.int32).reshape(B, 1, P)
        patches = _unfold3x3_reflect(x).reshape(B, C, K2, P)
        xc = x.reshape(B, C, P)
        cn = xc / jnp.maximum(jnp.linalg.norm(xc, axis=1, keepdims=True), EPS_NORM)
        pn = patches / jnp.maximum(jnp.linalg.norm(patches, axis=1, keepdims=True), EPS_NORM)
        sim = jnp.einsum('bcp,bckp->bkp', cn, pn)
        order = jnp.argsort(-sim, axis=1)
        top_sim = jnp.take_along_axis(sim, order, axis=1)
        mask = jnp.arange(K2)[None, :, None] < kvals
        wts = jnp.exp(top_sim) * mask
        wts = wts / jnp.sum(wts, axis=1, keepdims=True)
        pat_sorted = jnp.take_along_axis(patches, order[:, None, :, :], axis=2)
        out = jnp.einsum('bckp,bkp->bcp', pat_sorted, wts).reshape(B, C, H, W)
        enhanced = out + _group_norm(x, gn_weight, gn_bias)
        h = jax.nn.relu(jnp.einsum('oi,bihw->bohw', w1, enhanced) + b1[None, :, None, None])
        ffn = jnp.einsum('oi,bihw->bohw', w2, h) + b2[None, :, None, None]
        return enhanced + ffn

    def _L2_conv_ref(x, ln_w, ln_b, W_in, conv_w, conv_b, W_xproj, W_dt, b_dt, A_log, D, W_out):
        import jax, jax.numpy as jnp
        import numpy as np
        DIM, D_STATE, D_CONV, EXPAND = (32, 16, 4, 2)
        D_INNER = EXPAND * DIM
        DT_RANK = (DIM + 15) // 16

        def _mamba(xn, W_in, conv_w, conv_b, W_xproj, W_dt, b_dt, A_log, D, W_out):
            Bsz, L, _ = xn.shape
            d_inner, d_conv = conv_w.shape
            d_state = A_log.shape[1]
            dt_rank = W_dt.shape[1]
            xz = xn @ W_in.T
            xin, z = jnp.split(xz, 2, axis=-1)
            xc = jnp.swapaxes(xin, 1, 2)
            xc = jax.lax.conv_general_dilated(xc, conv_w[:, None, :], window_strides=(1,), padding=[(d_conv - 1, 0)], feature_group_count=d_inner)
            xc = xc + conv_b[None, :, None]
            u = jax.nn.silu(jnp.swapaxes(xc, 1, 2))
            x_dbl = u @ W_xproj.T
            dt, Bm, Cm = jnp.split(x_dbl, [dt_rank, dt_rank + d_state], axis=-1)
            delta = jax.nn.softplus(dt @ W_dt.T + b_dt)
            A = -jnp.exp(A_log)

            def step(h, xs):
                d_t, B_t, C_t, u_t = xs
                dA = jnp.exp(d_t[..., None] * A)
                h = dA * h + (d_t * u_t)[..., None] * B_t[:, None, :]
                y = jnp.einsum('bdn,bn->bd', h, C_t)
                return (h, y)
            xs = (jnp.swapaxes(delta, 0, 1), jnp.swapaxes(Bm, 0, 1), jnp.swapaxes(Cm, 0, 1), jnp.swapaxes(u, 0, 1))
            h0 = jnp.zeros((Bsz, d_inner, d_state), delta.dtype)
            _, ys = jax.lax.scan(step, h0, xs)
            y = jnp.swapaxes(ys, 0, 1) + u * D
            y = y * jax.nn.silu(z)
            return y @ W_out.T
        Bsz, d_model = x.shape[:2]
        img_dims = x.shape[2:]
        L = int(np.prod(img_dims))
        xf = jnp.swapaxes(x.reshape(Bsz, d_model, L), 1, 2)
        mu = jnp.mean(xf, axis=-1, keepdims=True)
        var = jnp.mean(jnp.square(xf - mu), axis=-1, keepdims=True)
        xn = (xf - mu) * jax.lax.rsqrt(var + 1e-05) * ln_w + ln_b
        y = _mamba(xn, W_in, conv_w, conv_b, W_xproj, W_dt, b_dt, A_log, D, W_out)
        return jnp.swapaxes(y, 1, 2).reshape(x.shape)

    def _L3_conv_ref(data_im, weight, offset_w, mask_w):
        import jax, jax.numpy as jnp
        import numpy as np
        KH, KW = (3, 3)
        SH, SW = (1, 1)
        PH, PW = (1, 1)
        DH, DW = (1, 1)
        DG = 1

        def _conv(x, w):
            return jax.lax.conv_general_dilated(x, w, window_strides=(SH, SW), padding=((PH, PH), (PW, PW)), rhs_dilation=(DH, DW), dimension_numbers=('NCHW', 'OIHW', 'NCHW'))

        def _deform_im2col(data_im, offset, mask):
            B, C, H, W = data_im.shape
            K = KH * KW
            Ho, Wo = (offset.shape[2], offset.shape[3])
            Cg = C // DG
            off = offset.reshape(B, DG, K, 2, Ho, Wo)
            off_y, off_x = (off[:, :, :, 0], off[:, :, :, 1])
            msk = mask.reshape(B, DG, 1, K, Ho, Wo)
            gi = jnp.repeat(jnp.arange(KH), KW)
            gj = jnp.tile(jnp.arange(KW), KH)
            base_y = (jnp.arange(Ho) * SH - PH)[None, :] + (gi * DH)[:, None]
            base_x = (jnp.arange(Wo) * SW - PW)[None, :] + (gj * DW)[:, None]
            y = base_y[None, None, :, :, None].astype(off_y.dtype) + off_y
            x = base_x[None, None, :, None, :].astype(off_x.dtype) + off_x
            y0 = jnp.floor(y)
            x0 = jnp.floor(x)
            ly = y - y0
            lx = x - x0
            y0i = y0.astype(jnp.int32)
            x0i = x0.astype(jnp.int32)
            y1i = y0i + 1
            x1i = x0i + 1
            flat = data_im.reshape(B, DG, Cg, H * W)

            def gather(yi, xi):
                valid = (yi >= 0) & (yi < H) & (xi >= 0) & (xi < W)
                idx = jnp.clip(yi, 0, H - 1) * W + jnp.clip(xi, 0, W - 1)
                idxf = idx.reshape(B, DG, 1, -1)
                g = jnp.take_along_axis(flat, jnp.broadcast_to(idxf, (B, DG, Cg, idxf.shape[-1])), axis=-1)
                g = g.reshape(B, DG, Cg, K, Ho, Wo)
                return g * valid[:, :, None].astype(g.dtype)
            w00 = ((1 - ly) * (1 - lx))[:, :, None]
            w01 = ((1 - ly) * lx)[:, :, None]
            w10 = (ly * (1 - lx))[:, :, None]
            w11 = (ly * lx)[:, :, None]
            val = w00 * gather(y0i, x0i) + w01 * gather(y0i, x1i) + w10 * gather(y1i, x0i) + w11 * gather(y1i, x1i)
            val = val * msk
            return val.reshape(B, C * K, Ho, Wo)
        offset = _conv(data_im, offset_w)
        mask = jax.nn.sigmoid(_conv(data_im, mask_w))
        col = _deform_im2col(data_im, offset, mask)
        out = jnp.einsum('op,bphw->bohw', weight, col)
        return out

    def _gn(v, G=32, eps=1e-05):
        B_, C_, H_, W_ = v.shape
        g = v.reshape(B_, G, C_ // G, H_, W_)
        m = jnp.mean(g, axis=(2, 3, 4), keepdims=True)
        s = jnp.var(g, axis=(2, 3, 4), keepdims=True)
        return ((g - m) / jnp.sqrt(s + eps)).reshape(v.shape)

    def _ln_c(v, eps=1e-06):
        m = jnp.mean(v, axis=1, keepdims=True)
        s = jnp.var(v, axis=1, keepdims=True)
        return (v - m) / jnp.sqrt(s + eps)

    def _ln_t(v, eps=1e-05):
        m = jnp.mean(v, axis=-1, keepdims=True)
        s = jnp.var(v, axis=-1, keepdims=True)
        return (v - m) / jnp.sqrt(s + eps)

    def _to_tokens(v):
        B_, C_, H_, W_ = v.shape
        return v.reshape(B_, C_, H_ * W_).transpose(0, 2, 1)

    def _from_tokens(t, like):
        B_, C_, H_, W_ = like.shape
        return t.transpose(0, 2, 1).reshape(B_, C_, H_, W_)
    x = x + _L0_conv_ref(_gn(x), L0_conv_mean_table, L0_conv_std_table, L0_conv_weight, L0_conv_bias, 4, 5, 5, 6)
    x = x + _L1_conv_ref(_gn(x), L1_conv_gn_weight, L1_conv_gn_bias, L1_conv_w1, L1_conv_b1, L1_conv_w2, L1_conv_b2)
    x = x + _L2_conv_ref(_gn(x), L2_conv_ln_w, L2_conv_ln_b, L2_conv_W_in, L2_conv_conv_w, L2_conv_conv_b, L2_conv_W_xproj, L2_conv_W_dt, L2_conv_b_dt, L2_conv_A_log, L2_conv_D, L2_conv_W_out)
    x = x + _L3_conv_ref(_gn(x), L3_conv_weight, L3_conv_offset_w, L3_conv_mask_w)
    return x

_drawn_inputs = setup_inputs


def setup_inputs(seed=0):
    import zlib

    import numpy as np

    out = dict(_drawn_inputs(seed))
    spreads = {'L0_conv_weight': (1.0, 0.2),
     'L0_conv_bias': (0.0, 0.301),
     'L2_conv_ln_w': (1.0, 0.2),
     'L2_conv_ln_b': (0.0, 0.1),
     'L2_conv_conv_b': (0.0, 0.1),
     'L2_conv_D': (1.0, 0.562)}
    factors = {'L1_conv_w1': 8.0,
     'L1_conv_b1': 8.0,
     'L1_conv_w2': 8.0,
     'L1_conv_b2': 8.0,
     'L2_conv_b_dt': 4.416}
    for name, (base, spread) in spreads.items():
        noise = np.random.default_rng([zlib.crc32(name.encode()), seed]).standard_normal(out[name].shape)
        drawn = base * np.exp(spread * noise) if base else spread * noise
        out[name] = jnp.asarray(drawn.astype(out[name].dtype))
    for name, factor in factors.items():
        out[name] = (out[name] * factor).astype(out[name].dtype)
    return out
```

```python
import concourse.bass as bass
import numpy as np
from concourse import mybir
from contextlib import ExitStack

F32 = mybir.dt.float32
BF16 = mybir.dt.bfloat16
U32 = mybir.dt.uint32
ALU = mybir.AluOpType
ACT = mybir.ActivationFunctionType
AX = mybir.AxisListType

P = 128
B, C, H, W = 2, 32, 64, 64
L = H * W
HALF = L // 2
BANK = 512
WP = W + 2
DI = 64
DS = 16
PAIRS = DS // 2
CHUNK = 1024
NCHUNK = L // CHUNK
TAPS = 9
GROUPS = L // P
GN_EPS = 1e-5
ROUND = 12582912.0

(M_IDENT, M_OWN, M_PRE, M_PAIR, M_CENTER, M_MEAN, M_LAP, M_DOWN, M_UPR, M_UP, M_UP0, M_PICKB) = range(12)
NMAT = 12
(V_W0, V_B0, V_GNW, V_GNB, V_B1, V_B2, V_LNW, V_LNB, V_CB, V_BDT, V_D) = range(11)
V_A = 11
V_M3 = V_A + PAIRS
V_HALF = V_M3 + 3
V_EPS = V_HALF + 2
NV = V_EPS + 1
W_ONE = 0
W_TWO = W_ONE + 128
W_INX = W_TWO + 64
W_CONV = W_INX + 128
W_INZ = W_CONV + 128
W_BC = W_INZ + 64
W_DTA = W_BC + 96
W_DTB = W_DTA + 64
W_OUT = W_DTB + 128
W_SUM = W_OUT + 32
W_OFF = W_SUM + 64
W_L3 = W_OFF + 3 * 27
NW = W_L3 + TAPS * 32


class Chain:

    def __init__(self, sem):
        self.sem, self.n, self.loop = sem, 0, 0

    def __call__(self, engine, ins):
        ins.then_inc(self.sem, 1)
        self.n += 1
        engine.wait_ge(self.sem, self.loop + self.n)

    def enter(self, i, per_turn):
        self.start, self.per_turn, self.loop = self.n, per_turn, i * per_turn

    def leave(self, turns):
        assert self.n == self.start + self.per_turn, (self.n - self.start, self.per_turn)
        self.n, self.loop = self.start + self.per_turn * turns, 0
def build(nc, x, mats, vecs, wts, bic, anchors, base, sel, out):
    ctx = ExitStack()
    with ctx:
        def sb(name, shape, dt=F32):
            return ctx.enter_context(nc.sbuf_tensor(name, shape, dt))

        def sem(name):
            return ctx.enter_context(nc.semaphore(name))

        X = sb("X", [P, HALF])
        mat = sb("mat", [P, NMAT, P])
        vec = sb("vec", [P, NV])
        wt = sb("wt", [P, NW])
        PS = ctx.enter_context(nc.psum_tensor("PS", [P, 8, BANK], F32))

        def M(k, rows=slice(0, P), cols=slice(0, P)):
            return mat[rows, k, cols]

        def V(k, n=1, rows=slice(0, P)):
            return vec[rows, k:k + n]

        ident = M(M_IDENT)
        x_half = x.rearrange("b c (h y) w -> b h c (y w)", h=2)
        out_half = out.rearrange("b c (h y) w -> b h c (y w)", h=2)
        vchain, achain, pchain, gchain = Chain(sem("dve_own")), Chain(sem("act_own")), Chain(sem("pe_own")), Chain(sem("pool_own"))

        def banks(first, n, rows=slice(0, P)):
            return PS[rows, first:first + n, :].rearrange("p b n -> p (b n)")

        def tell(engine, ins, signal, n=1):
            ins.then_inc(signal, 1)
            engine.wait_ge(signal, n)

        st6 = sb("st6", [P, 4, 6])
        mv = sb("mv", [P, 2])
        S2 = sb("S2", [P, 2])
        tot = sb("tot", [P, 4])
        var = sb("var", [P, 2])
        std = sb("std", [P, 2])
        rstd = sb("rstd", [P, 2])
        mrs = sb("mrs", [P, 2])
        nmrs = sb("nmrs", [P, 1])

        def gn_partition_stats(v, rows=slice(0, P)):
            for q in range(4):
                vchain(v, nc.vector.bn_stats(st6[rows, q, :], X[rows, q * BANK:(q + 1) * BANK]))
            vchain(v, nc.vector.bn_aggr(mv[rows, :], st6[rows, :, :].rearrange("p a b -> p (a b)")))
            vchain(v, nc.vector.tensor_copy(S2[rows, 0:1], mv[rows, 0:1]))
            return nc.vector.scalar_tensor_tensor(S2[rows, 1:2], mv[rows, 0:1], mv[rows, 0:1], mv[rows, 1:2],
                                                  ALU.mult, ALU.add)

        def variance(v, n, eps, rows=slice(0, P)):
            pairs = tot[rows, 0:2 * n].rearrange("p (n s) -> p n s", s=2)
            vchain(v, nc.vector.tensor_tensor(var[rows, 0:n], pairs[:, :, 0], pairs[:, :, 0], ALU.mult))
            vchain(v, nc.vector.tensor_tensor(var[rows, 0:n], pairs[:, :, 1], var[rows, 0:n], ALU.subtract))
            return nc.vector.tensor_scalar(std[rows, 0:n], var[rows, 0:n], eps, None, ALU.add)

        with ExitStack() as stage:
            bicubic = stage.enter_context(nc.sbuf_tensor("bicubic", [64, HALF], F32))
            patch = stage.enter_context(nc.sbuf_tensor("patch", [64, 2, 32], F32))
            LMS = stage.enter_context(nc.sbuf_tensor("LMS", [64, 2, P], F32))
            D = stage.enter_context(nc.sbuf_tensor("D", [P, 2, 3], F32))
            t1 = stage.enter_context(nc.sbuf_tensor("t1", [P, HALF], F32))
            xb = stage.enter_context(nc.sbuf_tensor("xb", [P, HALF], F32))
            pv = stage.enter_context(nc.sbuf_tensor("pv", [P, 3], F32))
            x_in, mat_in, vec_in, bic_in, rest_in = (sem(n) for n in ("x_in", "mat_in", "vec_in", "bic_in", "rest_in"))
            stats0, totals0, sqrt0_go, sqrt0_done, d_ready, dt_done, l_ready, maps_done, xb_done = (
                sem(n) for n in ("stats0", "totals0", "sqrt0_go", "sqrt0_done", "d_ready", "dt_done", "l_ready",
                                 "maps_done", "xb_done"))
            with nc.Block() as block:
                @block.sync
                def _(sp):
                    for b in range(B):
                        for h in range(2):
                            q = 2 * b + h
                            sp.dma_start(X[32 * q:32 * q + 32, :], x_half[b, h]).then_inc(x_in, 16)
                    sp.dma_start(bicubic[:, :], bic).then_inc(bic_in, 16)
                    sp.dma_start(wt[:, :], wts).then_inc(rest_in, 16)
                    sp.wait_ge(rest_in, 16)

                @block.scalar
                def _(act):
                    act.dma_start(vec[:, :], vecs).then_inc(vec_in, 16)
                    act.dma_start(mat[:, :, :], mats).then_inc(mat_in, 16)
                    act.dma_start(patch[32:64, :, :], anchors).then_inc(vec_in, 16)
                    act.wait_ge(x_in, 64)
                    act.wait_ge(vec_in, 32)
                    nc.scalar.activation(xb[:, :], X[:, :], ACT.Identity, bias=V(V_B0)).then_inc(xb_done, 1)
                    act.wait_ge(sqrt0_go, 1)
                    nc.scalar.activation(std[:, :], std[:, :], ACT.Sqrt).then_inc(sqrt0_done, 1)
                    act.wait_ge(sqrt0_go, 2)
                    nc.scalar.activation(pv[:, 1:2], pv[:, 0:1], ACT.Sqrt).then_inc(sqrt0_done, 1)

                @block.tensor
                def _(pe):
                    pe.wait_ge(mat_in, 16)
                    pe.wait_ge(stats0, 1)
                    nc.tensor.matmul(PS[:, 0, 0:2], M(M_OWN), S2[:, :], start=True, stop=True)
                    nc.tensor.matmul(PS[:, 0, 2:4], M(M_PRE), S2[:, :], start=True, stop=True).then_inc(totals0, 1)
                    pe.wait_ge(d_ready, 1)
                    for s in range(2):
                        last = nc.tensor.transpose(PS[0:3, 1, s * P:s * P + P], D[:, s, :], ident)
                    last.then_inc(dt_done, 1)
                    pe.wait_ge(bic_in, 16)
                    pe.wait_ge(l_ready, 1)
                    for s in range(2):
                        for n in range(4):
                            last = nc.tensor.matmul(PS[:, 4 * s + n, :], LMS[:, s, :], bicubic[:, n * BANK:(n + 1) * BANK],
                                                    start=True, stop=True)
                    last.then_inc(maps_done, 1)

                @block.vector
                def _(v):
                    vchain(v, nc.vector.memset(LMS[:, :, :], 0.0))
                    v.wait_ge(vec_in, 32)
                    vchain(v, nc.vector.reciprocal(patch[32:64, 1, :], patch[32:64, 1, :]))
                    for s in range(2):
                        for h in range(2):
                            vchain(v, nc.vector.tensor_scalar(LMS[32:64, s, 32 * h:32 * h + 32], patch[32:64, s, :],
                                                              vec[32:64, V_HALF + h:V_HALF + h + 1], None, ALU.mult))
                    v.wait_ge(x_in, 64)
                    gn_partition_stats(v).then_inc(stats0, 1)
                    v.wait_ge(totals0, 1)
                    vchain(v, nc.vector.tensor_copy(tot[:, :], PS[:, 0, 0:4]))
                    variance(v, 2, GN_EPS).then_inc(sqrt0_go, 1)
                    v.wait_ge(sqrt0_done, 1)
                    vchain(v, nc.vector.reciprocal(rstd[:, :], std[:, :]))
                    vchain(v, nc.vector.tensor_tensor(mrs[:, :], tot[:, 0:4:2], rstd[:, :], ALU.mult))
                    vchain(v, nc.vector.tensor_tensor(pv[:, 0:1], rstd[:, 1:2], rstd[:, 1:2], ALU.mult))
                    tell(v, nc.vector.tensor_scalar(pv[:, 0:1], pv[:, 0:1], var[:, 1:2], float(L) / (L - 1), ALU.mult, ALU.mult), sqrt0_go, 2)
                    vchain(v, nc.vector.tensor_scalar(pv[:, 2:3], tot[:, 2:3], rstd[:, 1:2], mrs[:, 1:2], ALU.mult, ALU.subtract))
                    v.wait_ge(sqrt0_done, 2)
                    vchain(v, nc.vector.reciprocal(pv[:, 1:2], pv[:, 1:2]))
                    vchain(v, nc.vector.tensor_scalar(D[:, 0, :], V(V_M3, 3), pv[:, 2:3], None, ALU.mult))
                    vchain(v, nc.vector.tensor_scalar(D[:, 1, :], V(V_M3, 3), pv[:, 1:2], None, ALU.mult))
                    nc.vector.tensor_tensor(D[:, 0, 2:3], D[:, 0, 2:3], mrs[:, 0:1], ALU.add).then_inc(d_ready, 1)
                    v.wait_ge(dt_done, 1)
                    nc.vector.tensor_copy(LMS[0:3, :, :], PS[0:3, 1, 0:2 * P].rearrange("p (s n) -> p s n", s=2)).then_inc(l_ready, 1)
                    v.wait_ge(maps_done, 1)
                    vchain(v, nc.vector.scalar_tensor_tensor(t1[:, :], X[:, :], rstd[:, 0:1], banks(0, 4), ALU.mult, ALU.subtract))
                    vchain(v, nc.vector.tensor_tensor(t1[:, :], t1[:, :], banks(4, 4), ALU.mult))
                    v.wait_ge(xb_done, 1)
                    vchain(v, nc.vector.scalar_tensor_tensor(X[:, :], t1[:, :], V(V_W0), xb[:, :], ALU.mult, ALU.add))

        with ExitStack() as stage:
            def tile(name, shape, dt=F32):
                return stage.enter_context(nc.sbuf_tensor(name, shape, dt))

            G = tile("G", [P, HALF])
            GR = tile("GR", [P, WP, C])
            GD = tile("GD", [P, WP, C])
            GU = tile("GU", [P, WP, C])
            NPROD = 4
            prod = tile("prod", [P, NPROD, WP, C])
            avg = tile("avg", [P, WP])
            df = tile("df", [P, 2, W])
            mm = tile("mm", [P, 2])
            mmT = tile("mmT", [2, B])
            mmB = tile("mmB", [B, 2])
            rng = tile("rng", [P, 4])
            kval = tile("kval", [P, W])
            n2 = tile("n2", [P, 2, W])
            rn = tile("rn", [P, 3, WP])
            ER = tile("ER", [P, WP])
            VD = tile("VD", [P, 3, WP])
            sim = tile("sim", [P, TAPS, W])
            cmp = tile("cmp", [P, TAPS, W])
            rank = tile("rank", [P, TAPS, W])
            wk = tile("wk", [P, TAPS, W])
            wsum = tile("wsum", [P, 2, W])
            gn2 = tile("gn2", [P, 8])
            enh = tile("enh", [P, HALF])
            hid = tile("hid", [P, 2, HALF])
            names = ("stats1", "totals1", "sqrt1_go", "sqrt1_done", "g_done", "gn_stats", "gn_totals", "gr_ready",
                     "shift_done", "gd_ready", "lap_in", "lap_done", "mm_ready", "mmT_done", "mmT_ready", "mmB_done",
                     "mmB_ready", "rng_done", "norm2_ready", "norm_done", "rn_ready", "rn_shift_done", "vd_ready", "dm_done",
                     "sim_ready", "exp_done", "w_ready", "prod_ready", "prod_free", "agg_done", "enh_ready", "h_psum",
                     "h_ready", "f_psum", "pool_prod")
            S = {n: sem("s1_" + n) for n in names}
            with nc.Block() as block:
                @block.vector
                def _(v):
                    gn_partition_stats(v).then_inc(S["stats1"], 1)
                    v.wait_ge(S["totals1"], 1)
                    vchain(v, nc.vector.tensor_copy(tot[:, 0:2], PS[:, 0, 0:2]))
                    variance(v, 1, GN_EPS).then_inc(S["sqrt1_go"], 1)
                    v.wait_ge(S["sqrt1_done"], 1)
                    vchain(v, nc.vector.reciprocal(rstd[:, 0:1], std[:, 0:1]))
                    vchain(v, nc.vector.scalar_tensor_tensor(nmrs[:, :], tot[:, 0:1], -1.0, rstd[:, 0:1], ALU.mult, ALU.mult))
                    vchain(v, nc.vector.tensor_scalar(G[:, :], X[:, :], rstd[:, 0:1], nmrs[:, :], ALU.mult, ALU.add))
                    vchain(v, nc.vector.tensor_scalar(gn2[:, 0:1], tot[:, 0:1], rstd[:, 0:1], nmrs[:, :], ALU.mult, ALU.add))
                    vchain(v, nc.vector.tensor_tensor(gn2[:, 2:3], rstd[:, 0:1], rstd[:, 0:1], ALU.mult))
                    vchain(v, nc.vector.tensor_scalar(gn2[:, 2:3], gn2[:, 2:3], var[:, 0:1], None, ALU.mult))
                    nc.vector.scalar_tensor_tensor(gn2[:, 1:2], gn2[:, 0:1], gn2[:, 0:1], gn2[:, 2:3],
                                                   ALU.mult, ALU.add).then_inc(S["gn_stats"], 1)
                    vchain(v, nc.vector.transpose(GR[:, 1:W + 1, :], G[:, :].rearrange("p (y x) -> p x y", x=W)))
                    tell(v, nc.vector.tensor_copy(GR[:, 0:WP:W + 1, :], GR[:, 2:W:W - 3, :]), S["gr_ready"])
                    v.wait_ge(S["gn_totals"], 1)
                    vchain(v, nc.vector.tensor_copy(tot[:, 0:2], PS[:, 7, 0:2]))
                    variance(v, 1, GN_EPS).then_inc(S["sqrt1_go"], 1)
                    v.wait_ge(S["sqrt1_done"], 2)
                    vchain(v, nc.vector.reciprocal(gn2[:, 4:5], std[:, 0:1]))
                    vchain(v, nc.vector.tensor_tensor(gn2[:, 4:5], gn2[:, 4:5], V(V_GNW), ALU.mult))
                    vchain(v, nc.vector.tensor_tensor(gn2[:, 5:6], tot[:, 0:1], gn2[:, 4:5], ALU.mult))
                    vchain(v, nc.vector.tensor_tensor(gn2[:, 5:6], V(V_GNB), gn2[:, 5:6], ALU.subtract))
                    vchain(v, nc.vector.memset(avg[:, :], 0.0))
                    vchain(v, nc.vector.tensor_reduce(avg[:, 1:W + 1], GR[:, 1:W + 1, :], AX.X, ALU.add))
                    tell(v, nc.vector.tensor_scalar(avg[:, 1:W + 1], avg[:, 1:W + 1], 1.0 / C, None, ALU.mult), S["lap_in"])
                    vchain(v, nc.vector.tensor_tensor(prod[:, 0, 0:W, :], GR[:, 1:W + 1, :], GR[:, 1:W + 1, :], ALU.mult))
                    tell(v, nc.vector.tensor_reduce(n2[:, 0, :], prod[:, 0, 0:W, :], AX.X, ALU.add), S["norm2_ready"])
                    vchain(v, nc.vector.tensor_tensor(prod[:, 0, 0:W + 1, :], GR[:, 0:W + 1, :], GR[:, 1:W + 2, :], ALU.mult))
                    vchain(v, nc.vector.tensor_reduce(ER[:, 0:W + 1], prod[:, 0, 0:W + 1, :], AX.X, ALU.add))
                    v.wait_ge(S["norm_done"], 1)
                    vchain(v, nc.vector.tensor_scalar(n2[:, 1, :], n2[:, 1, :], 1e-12, None, ALU.max))
                    vchain(v, nc.vector.reciprocal(rn[:, 1, 1:W + 1], n2[:, 1, :]))
                    tell(v, nc.vector.tensor_copy(rn[:, 1, 0:WP:W + 1], rn[:, 1, 2:W:W - 3]), S["rn_ready"])
                    v.wait_ge(S["gd_ready"], 1)
                    for j, (lo, hi, dx) in enumerate(((1, WP, -1), (1, W + 1, 0), (0, W + 1, 1))):
                        vchain(v, nc.vector.tensor_tensor(prod[:, j, lo:hi, :], GR[:, lo:hi, :], GD[:, lo + dx:hi + dx, :], ALU.mult))
                        tell(v, nc.vector.tensor_reduce(VD[:, j, lo:hi], prod[:, j, lo:hi, :], AX.X, ALU.add), S["vd_ready"], j + 1)
                    v.wait_ge(S["lap_done"], 1)
                    vchain(v, nc.vector.tensor_tensor(df[:, 0, :], PS[:, 6, 0:W], avg[:, 0:W], ALU.subtract))
                    vchain(v, nc.vector.tensor_tensor(df[:, 0, :], df[:, 0, :], avg[:, 2:W + 2], ALU.subtract))
                    vchain(v, nc.vector.tensor_scalar(df[:, 1, :], df[:, 0, :], -1.0, None, ALU.mult))
                    vchain(v, nc.vector.tensor_tensor(df[:, 0, :], df[:, 0, :], df[:, 1, :], ALU.max))
                    vchain(v, nc.vector.tensor_scalar(df[:, 1, :], df[:, 0, :], -1.0, None, ALU.mult))
                    tell(v, nc.vector.tensor_reduce(mm[:, :], df[:, :, :], AX.X, ALU.max), S["mm_ready"])
                    v.wait_ge(S["mmT_done"], 1)
                    tell(v, nc.vector.tensor_reduce(mmT[:, :], PS[0:2, 7, 0:P].rearrange("s (b y) -> s b y", b=B), AX.X, ALU.max), S["mmT_ready"])
                    v.wait_ge(S["mmB_done"], 1)
                    tell(v, nc.vector.tensor_copy(mmB[:, :], PS[0:B, 7, 0:2]), S["mmB_ready"])
                    v.wait_ge(S["rng_done"], 1)
                    vchain(v, nc.vector.tensor_copy(rng[:, 0:2], PS[:, 7, 0:2]))
                    vchain(v, nc.vector.tensor_tensor(rng[:, 2:3], rng[:, 0:1], rng[:, 1:2], ALU.add))
                    vchain(v, nc.vector.tensor_scalar(rng[:, 2:3], rng[:, 2:3], 1e-8, None, ALU.add))
                    vchain(v, nc.vector.reciprocal(rng[:, 3:4], rng[:, 2:3]))
                    vchain(v, nc.vector.tensor_scalar(kval[:, :], df[:, 0, :], rng[:, 1:2], rng[:, 3:4], ALU.add, ALU.mult))
                    vchain(v, nc.vector.tensor_scalar(kval[:, :], kval[:, :], 7.0, ROUND, ALU.mult, ALU.add))
                    vchain(v, nc.vector.tensor_scalar(kval[:, :], kval[:, :], ROUND - 1.0, 9.0, ALU.subtract, ALU.min))
                    v.wait_ge(S["rn_shift_done"], 1)
                    vchain(v, nc.vector.tensor_copy(rn[:, 0:3:2, :], PS[:, 6, 0:2 * WP].rearrange("p (s x) -> p s x", s=2)))
                    for dx in (-1, 0, 1):
                        lo, hi = 1 + dx, W + 1 + dx
                        vchain(v, nc.vector.tensor_tensor(sim[:, 7 + dx, :], VD[:, 1 + dx, 1:W + 1], rn[:, 2, lo:hi], ALU.mult))
                    vchain(v, nc.vector.tensor_tensor(sim[:, 3, :], ER[:, 0:W], rn[:, 1, 0:W], ALU.mult))
                    vchain(v, nc.vector.tensor_tensor(sim[:, 4, :], n2[:, 0, :], rn[:, 1, 1:W + 1], ALU.mult))
                    vchain(v, nc.vector.tensor_tensor(sim[:, 5, :], ER[:, 1:W + 1], rn[:, 1, 2:W + 2], ALU.mult))
                    v.wait_ge(S["dm_done"], 1)
                    for dx in (-1, 0, 1):
                        lo, hi = 1 + dx, W + 1 + dx
                        vchain(v, nc.vector.tensor_tensor(sim[:, 1 + dx, :], PS[:, 5, (1 + dx) * W:(2 + dx) * W], rn[:, 0, lo:hi], ALU.mult))
                    tell(v, nc.vector.tensor_tensor(sim[:, :, :], sim[:, :, :],
                                                      rn[:, 1, 1:W + 1].unsqueeze(1).to_broadcast([P, TAPS, W]), ALU.mult), S["sim_ready"])
                    for k in range(TAPS):
                        last = nc.vector.memset(rank[:, k, :], float(TAPS - 1 - k))
                    vchain(v, last)
                    for d in range(1, TAPS):
                        n = TAPS - d
                        vchain(v, nc.vector.tensor_tensor(cmp[:, 0:n, :], sim[:, 0:n, :], sim[:, d:TAPS, :], ALU.is_ge))
                        vchain(v, nc.vector.tensor_tensor(rank[:, d:TAPS, :], rank[:, d:TAPS, :], cmp[:, 0:n, :], ALU.add))
                        vchain(v, nc.vector.tensor_tensor(rank[:, 0:n, :], rank[:, 0:n, :], cmp[:, 0:n, :], ALU.subtract))
                    vchain(v, nc.vector.tensor_tensor(cmp[:, :, :], rank[:, :, :],
                                                      kval[:, :].unsqueeze(1).to_broadcast([P, TAPS, W]), ALU.is_lt))
                    v.wait_ge(S["exp_done"], 1)
                    vchain(v, nc.vector.tensor_tensor(wk[:, :, :], wk[:, :, :], cmp[:, :, :], ALU.mult))
                    vchain(v, nc.vector.tensor_reduce(wsum[:, 0, :], wk[:, :, :].rearrange("p k x -> p x k"), AX.X, ALU.add))
                    vchain(v, nc.vector.reciprocal(wsum[:, 1, :], wsum[:, 0, :]))
                    tell(v, nc.vector.tensor_tensor(wk[:, :, :], wk[:, :, :],
                                                      wsum[:, 1, :].unsqueeze(1).to_broadcast([P, TAPS, W]), ALU.mult), S["w_ready"])
                    for k in range(TAPS):
                        src = (GU, GR, GD)[k // 3]
                        if k >= NPROD:
                            v.wait_ge(S["prod_free"], k - NPROD + 1)
                        nc.vector.tensor_tensor(prod[:, k % NPROD, 0:W, :], src[:, k % 3:k % 3 + W, :],
                                                wk[:, k, :].unsqueeze(2).to_broadcast([P, W, C]),
                                                ALU.mult).then_inc(S["prod_ready"], 1)
                    v.wait_ge(S["agg_done"], 1)
                    vchain(v, nc.vector.transpose(enh[:, :].rearrange("p (y x) -> p x y", x=W),
                                                  banks(0, 4).rearrange("p (x c) -> p x c", c=C)))
                    vchain(v, nc.vector.scalar_tensor_tensor(enh[:, :], G[:, :], gn2[:, 4:5], enh[:, :], ALU.mult, ALU.add))
                    tell(v, nc.vector.tensor_scalar(enh[:, :], enh[:, :], gn2[:, 5:6], None, ALU.add), S["enh_ready"])
                    vchain(v, nc.vector.tensor_tensor(X[:, :], X[:, :], enh[:, :], ALU.add))
                    for n in range(4):
                        v.wait_ge(S["f_psum"], n + 1)
                        vchain(v, nc.vector.scalar_tensor_tensor(X[:, n * BANK:(n + 1) * BANK], PS[:, n, :], V(V_B2),
                                                                 X[:, n * BANK:(n + 1) * BANK], ALU.add, ALU.add))

                @block.scalar
                def _(act):
                    act.wait_ge(S["sqrt1_go"], 1)
                    nc.scalar.activation(std[:, 0:1], std[:, 0:1], ACT.Sqrt).then_inc(S["sqrt1_done"], 1)
                    act.wait_ge(S["sqrt1_go"], 2)
                    nc.scalar.activation(std[:, 0:1], std[:, 0:1], ACT.Sqrt).then_inc(S["sqrt1_done"], 1)
                    act.wait_ge(S["norm2_ready"], 1)
                    nc.scalar.activation(n2[:, 1, :], n2[:, 0, :], ACT.Sqrt).then_inc(S["norm_done"], 1)
                    for j, dst in enumerate((GD, GU)):
                        act.wait_ge(S["shift_done"], j + 1)
                        nc.scalar.activation(dst[:, :, :].rearrange("p x c -> p (x c)"), banks(0, 5)[:, 0:WP * C],
                                             ACT.Copy).then_inc(S["gd_ready"], 1)
                    act.wait_ge(S["sim_ready"], 1)
                    nc.scalar.activation(wk[:, :, :], sim[:, :, :], ACT.Exp).then_inc(S["exp_done"], 1)
                    for m in range(8):
                        act.wait_ge(S["h_psum"], m + 1)
                        nc.scalar.activation(hid[:, m % 2, (m // 2) * BANK:(m // 2 + 1) * BANK], PS[:, 4 + m % 4, :],
                                             ACT.Relu, bias=V(V_B1)).then_inc(S["h_ready"], 1)

                @block.tensor
                def _(pe):
                    pe.wait_ge(S["stats1"], 1)
                    nc.tensor.matmul(PS[:, 0, 0:2], M(M_OWN), S2[:, :], start=True, stop=True).then_inc(S["totals1"], 1)
                    pe.wait_ge(S["gn_stats"], 1)
                    nc.tensor.matmul(PS[:, 7, 0:2], M(M_PAIR), gn2[:, 0:2], start=True, stop=True).then_inc(S["gn_totals"], 1)
                    pe.wait_ge(S["gr_ready"], 1)
                    flat = GR[:, :, :].rearrange("p x c -> p (x c)")

                    def shift_rows(k):
                        for n in range(5):
                            hi = min((n + 1) * BANK, WP * C)
                            last = nc.tensor.matmul(PS[:, n, 0:hi - n * BANK], M(k), flat[:, n * BANK:hi], start=True, stop=True)
                        last.then_inc(S["shift_done"], 1)

                    shift_rows(M_DOWN)
                    pe.wait_ge(S["lap_in"], 1)
                    nc.tensor.matmul(PS[:, 6, 0:W], M(M_LAP), avg[:, 1:W + 1], start=True, stop=True).then_inc(S["lap_done"], 1)
                    pe.wait_ge(S["gd_ready"], 1)
                    shift_rows(M_UPR)
                    pe.wait_ge(S["vd_ready"], 3)
                    for dx in (-1, 0, 1):
                        o = PS[:, 5, (1 + dx) * W:(2 + dx) * W]
                        nc.tensor.matmul(o, M(M_UP), VD[:, 1 - dx, 1 + dx:1 + dx + W], start=True, stop=False)
                        last = nc.tensor.matmul(o, M(M_UP0), VD[:, 1 + dx, 1:W + 1], start=False, stop=True)
                    last.then_inc(S["dm_done"], 1)
                    pe.wait_ge(S["mm_ready"], 1)
                    nc.tensor.transpose(PS[0:2, 7, 0:P], mm[:, :], ident).then_inc(S["mmT_done"], 1)
                    pe.wait_ge(S["rn_ready"], 1)
                    nc.tensor.matmul(PS[:, 6, 0:WP], M(M_UPR), rn[:, 1, :], start=True, stop=True)
                    nc.tensor.matmul(PS[:, 6, WP:2 * WP], M(M_DOWN), rn[:, 1, :], start=True, stop=True).then_inc(S["rn_shift_done"], 1)
                    pe.wait_ge(S["mmT_ready"], 1)
                    nc.tensor.transpose(PS[0:2, 7, 0:2], mmT[:, :], M(M_IDENT, slice(0, 2), slice(0, 2))).then_inc(S["mmB_done"], 1)
                    pe.wait_ge(S["mmB_ready"], 1)
                    nc.tensor.matmul(PS[:, 7, 0:2], M(M_PICKB, slice(0, B)), mmB[:, :], start=True, stop=True).then_inc(S["rng_done"], 1)
                    pe.wait_ge(S["gd_ready"], 2)
                    for k in range(TAPS):
                        pe.wait_ge(S["prod_ready"], k + 1)
                        for n in range(4):
                            last = nc.tensor.matmul(PS[:, n, :], ident,
                                                    prod[:, k % NPROD, 0:W, :].rearrange("p x c -> p (x c)")[:, n * BANK:(n + 1) * BANK],
                                                    start=(k == 0), stop=(k == TAPS - 1))
                        last.then_inc(S["prod_free"] if k < TAPS - 1 else S["agg_done"], 1)
                    pe.wait_ge(S["enh_ready"], 1)

                    def ffn_out(m):
                        n, r = m // 2, m % 2
                        pe.wait_ge(S["h_ready"], m + 1)
                        last = nc.tensor.matmul(PS[64 * r:64 * r + 64, n, :], wt[:, W_TWO:W_TWO + 64],
                                                hid[:, r, n * BANK:(n + 1) * BANK], start=True, stop=True)
                        if r == 1:
                            last.then_inc(S["f_psum"], 1)

                    for m in range(8):
                        n, r = m // 2, m % 2
                        if m >= 4:
                            pe.wait_ge(S["h_ready"], m - 3)
                        rows = slice(64 * r, 64 * r + 64)
                        nc.tensor.matmul(PS[:, 4 + m % 4, :], wt[rows, W_ONE:W_ONE + 128], enh[rows, n * BANK:(n + 1) * BANK],
                                         start=True, stop=True).then_inc(S["h_psum"], 1)
                        if m:
                            ffn_out(m - 1)
                    ffn_out(7)

        XN = sb("XN", [P, B, L])
        UZ = sb("UZ", [P, 2 * L])
        u = UZ[:, 0:L]
        zy = UZ[0:DI, L:2 * L]
        wx = sb("wx", [P, P])
        wdt = sb("wdt", [DI, P])
        negA = sb("negA", [P, PAIRS])
        selb = sb("selb", [96, 2, PAIRS, P], BF16)

        with ExitStack() as stage:
            g = stage.enter_context(nc.sbuf_tensor("ln_g", [P, HALF], F32))
            sq = stage.enter_context(nc.sbuf_tensor("ln_sq", [P, HALF], F32))
            selw = stage.enter_context(nc.sbuf_tensor("selw", [96, 2 * PAIRS * P], F32))
            names = ("sel_in", "stats", "totals", "sqrt_go", "sqrt_done", "g_ready", "centered", "squared", "var_done",
                     "std_done", "xn_ready", "zeroed", "xn_in", "dt_psum", "expA_done", "w_done")
            S = {n: sem("s2_" + n) for n in names}
            with nc.Block() as block:
                @block.sync
                def _(sp):
                    sp.dma_start(selw[:, :], sel).then_inc(S["sel_in"], 16)
                    sp.wait_ge(S["zeroed"], 1)
                    sp.wait_ge(S["xn_ready"], 1)
                    for b in range(B):
                        for h in range(2):
                            q = 2 * b + h
                            for j in range(4):
                                first = h * HALF + 3 - j
                                n = min(HALF, L - first)
                                sp.dma_start(XN[32 * j:32 * j + 32, b, first:first + n],
                                             g[32 * q:32 * q + 32, 0:n]).then_inc(S["xn_in"], 16)
                    sp.wait_ge(S["xn_in"], 16 * 16)

                @block.tensor
                def _(pe):
                    nc.tensor.matmul(PS[0:DI, 4, 0:P], wt[0:2, W_DTA:W_DTA + DI], wt[0:2, W_DTB:W_DTB + P],
                                     start=True, stop=True).then_inc(S["dt_psum"], 1)
                    pe.wait_ge(S["stats"], 1)
                    nc.tensor.matmul(PS[:, 0, 0:2], M(M_OWN), S2[:, :], start=True, stop=True).then_inc(S["totals"], 1)
                    pe.wait_ge(S["g_ready"], 1)
                    for n in range(4):
                        last = nc.tensor.matmul(PS[:, n, :], M(M_CENTER), g[:, n * BANK:(n + 1) * BANK], start=True, stop=True)
                    last.then_inc(S["centered"], 1)
                    pe.wait_ge(S["squared"], 1)
                    pe.wait_ge(S["w_done"], 1)
                    for n in range(4):
                        last = nc.tensor.matmul(PS[:, 4 + n, :], M(M_MEAN), sq[:, n * BANK:(n + 1) * BANK], start=True, stop=True)
                    last.then_inc(S["var_done"], 1)

                @block.scalar
                def _(act):
                    nc.scalar.activation(negA[:, :], V(V_A, PAIRS), ACT.Exp).then_inc(S["expA_done"], 1)
                    act.wait_ge(S["sqrt_go"], 1)
                    nc.scalar.activation(std[:, 0:1], std[:, 0:1], ACT.Sqrt).then_inc(S["sqrt_done"], 1)
                    act.wait_ge(S["centered"], 1)
                    nc.scalar.activation(sq[:, :], banks(0, 4), ACT.Square).then_inc(S["squared"], 1)
                    act.wait_ge(S["var_done"], 1)
                    nc.scalar.activation(sq[:, :], banks(4, 4), ACT.Sqrt, bias=V(V_EPS)).then_inc(S["std_done"], 1)

                @block.vector
                def _(v):
                    gn_partition_stats(v).then_inc(S["stats"], 1)
                    v.wait_ge(S["totals"], 1)
                    vchain(v, nc.vector.tensor_copy(tot[:, 0:2], PS[:, 0, 0:2]))
                    variance(v, 1, GN_EPS).then_inc(S["sqrt_go"], 1)
                    v.wait_ge(S["sqrt_done"], 1)
                    vchain(v, nc.vector.reciprocal(rstd[:, 0:1], std[:, 0:1]))
                    vchain(v, nc.vector.scalar_tensor_tensor(nmrs[:, :], tot[:, 0:1], -1.0, rstd[:, 0:1], ALU.mult, ALU.mult))
                    tell(v, nc.vector.tensor_scalar(g[:, :], X[:, :], rstd[:, 0:1], nmrs[:, :], ALU.mult, ALU.add), S["g_ready"])
                    tell(v, nc.vector.memset(XN[0:96, :, 0:3], 0.0), S["zeroed"])
                    vchain(v, nc.vector.tensor_tensor(wx[:, :], wt[:, W_INX:W_INX + P], wt[:, W_CONV:W_CONV + P], ALU.mult))
                    v.wait_ge(S["expA_done"], 1)
                    vchain(v, nc.vector.tensor_scalar(negA[:, :], negA[:, :], -1.0, None, ALU.mult))
                    v.wait_ge(S["sel_in"], 16)
                    vchain(v, nc.vector.tensor_copy(selb[:, :, :, :].rearrange("p a b c -> p (a b c)"), selw[:, :]))
                    v.wait_ge(S["dt_psum"], 1)
                    tell(v, nc.vector.tensor_copy(wdt[:, :], PS[0:DI, 4, 0:P]), S["w_done"])
                    v.wait_ge(S["std_done"], 1)
                    vchain(v, nc.vector.reciprocal(sq[:, :], sq[:, :]))
                    vchain(v, nc.vector.tensor_tensor(g[:, :], banks(0, 4), sq[:, :], ALU.mult))
                    tell(v, nc.vector.tensor_scalar(g[:, :], g[:, :], V(V_LNW), V(V_LNB), ALU.mult, ALU.add), S["xn_ready"])

        scratch = sb("scratch", [P, 9 * CHUNK])

        def chunk_buffer(k, n=1):
            return scratch[:, k * CHUNK:(k + n) * CHUNK]

        dl = chunk_buffer(0)
        du = chunk_buffer(1)
        sp_tmp = chunk_buffer(2)
        resid = chunk_buffer(3)
        dA = chunk_buffer(4, 2).rearrange("p (s n) -> p s n", s=2)
        dBC = chunk_buffer(6, 2).rearrange("p (s n) -> p s n", s=2)
        hs = chunk_buffer(8)
        parts = sb("parts", [96, CHUNK], BF16)
        prime = sb("prime", [P, 8])
        carry = sb("carry", [P, PAIRS])

        pr = {n: sem("proj_" + n) for n in ("xc_psum", "z_psum", "u_done", "z_done")}

        def project(b):
            with nc.Block() as block:
                @block.tensor
                def _(pe):
                    for n in range(8):
                        k = 8 * b + n
                        cols = slice(n * BANK, (n + 1) * BANK)
                        if n >= 4:
                            pe.wait_ge(pr["z_done"], k - 3)
                        nc.tensor.matmul(PS[:, n % 4, :], wx[:, :], XN[:, b, cols], start=True, stop=True).then_inc(pr["xc_psum"], 1)
                        nc.tensor.matmul(PS[0:DI, 4 + n % 4, :], wt[:, W_INZ:W_INZ + DI], XN[:, b, cols],
                                         start=True, stop=True).then_inc(pr["z_psum"], 1)

                @block.scalar
                def _(act):
                    for n in range(8):
                        k = 8 * b + n
                        cols = slice(n * BANK, (n + 1) * BANK)
                        act.wait_ge(pr["xc_psum"], k + 1)
                        nc.scalar.activation(u[:, cols], PS[:, n % 4, :], ACT.Silu, bias=V(V_CB)).then_inc(pr["u_done"], 1)
                        act.wait_ge(pr["z_psum"], k + 1)
                        nc.scalar.activation(zy[:, cols], PS[0:DI, 4 + n % 4, :], ACT.Silu).then_inc(pr["z_done"], 1)

        sc = {n: sem("scan_" + n) for n in ("pre_psum", "hi_done", "abs_done", "log_done", "parts_ready", "pre_used",
                                            "delta_ready", "b_psum", "c_psum", "b_used", "exp_done", "h_done", "hc_done",
                                            "y_done", "y_used", "resid_done")}

        def scan_tensor(pe, b, i, c):
            tok = lambda n: bass.ds(i * CHUNK + n * BANK, BANK)
            pe.wait_ge(sc["hc_done"], c * PAIRS + 1)
            for n in range(2):
                nc.tensor.matmul(PS[:, n, :], wdt[:, :], u[0:DI, tok(n)], start=True, stop=True)
            for n in range(2):
                last = nc.tensor.matmul(PS[0:96, 2 + n, :], wt[0:DI, W_BC:W_BC + 96], u[0:DI, tok(n)], start=True, stop=True)
            last.then_inc(sc["pre_psum"], 1)

            def add_states(j):
                s = c * PAIRS + j
                pe.wait_ge(sc["hc_done"], s + 2)
                if j == 0:
                    pe.wait_ge(sc["y_used"], c + 1)
                for n in range(2):
                    last = nc.tensor.matmul(PS[0:DI, 4 + n, :], wt[:, W_SUM:W_SUM + DI], dBC[:, j % 2, n * BANK:(n + 1) * BANK],
                                            start=(j == 0), stop=(j == PAIRS - 1))
                last.then_inc(sc["y_done"], 1)

            pe.wait_ge(sc["parts_ready"], c + 1)
            pe.wait_ge(sc["pre_used"], c + 1)
            for j in range(PAIRS):
                s = c * PAIRS + j
                if j:
                    pe.wait_ge(sc["b_used"], s)
                for n in range(2):
                    last = nc.tensor.matmul(PS[:, n, :], selb[:, 0, j, :], parts[:, n * BANK:(n + 1) * BANK], start=True, stop=True)
                last.then_inc(sc["b_psum"], 1)
                if j:
                    pe.wait_ge(sc["hc_done"], s + 1)
                for n in range(2):
                    last = nc.tensor.matmul(PS[:, 2 + n, :], selb[:, 1, j, :], parts[:, n * BANK:(n + 1) * BANK], start=True, stop=True)
                last.then_inc(sc["c_psum"], 1)
                if j:
                    add_states(j - 1)
            add_states(PAIRS - 1)

        def scan_scalar(act, b, i, c):
            act.wait_ge(sc["pre_psum"], c + 1)
            nc.scalar.activation(parts[:, :], banks(2, 2, slice(0, 96)), ACT.Copy).then_inc(sc["hi_done"], 1)
            act.wait_ge(sc["y_used"], c + 1)
            nc.scalar.activation(sp_tmp, banks(0, 2), ACT.Abs, bias=V(V_BDT)).then_inc(sc["abs_done"], 1)
            act.wait_ge(sc["abs_done"], c + 1)
            achain(act, nc.scalar.activation(sp_tmp, sp_tmp, ACT.Exp, scale=-1.0))
            nc.scalar.activation(sp_tmp, sp_tmp, ACT.Ln, bias=1.0).then_inc(sc["log_done"], 1)
            act.wait_ge(sc["delta_ready"], c + 1)
            for j in range(PAIRS):
                s = c * PAIRS + j
                act.wait_ge(sc["h_done"], s + 1)
                nc.scalar.activation(dA[:, j % 2, :], dl, ACT.Exp, scale=negA[:, j:j + 1]).then_inc(sc["exp_done"], 1)

        def scan_vector(v, b, i, c):
            tok = bass.ds(i * CHUNK, CHUNK)
            v.wait_ge(sc["hi_done"], c + 1)
            vchain(v, nc.vector.tensor_tensor(resid[0:DI, :], banks(2, 2, slice(0, DI)), parts[0:DI, :], ALU.subtract))
            vchain(v, nc.vector.tensor_copy(parts[0:DI, :], resid[0:DI, :]))
            nc.vector.tensor_tensor(parts[0:32, :], resid[0:32, :], parts[0:32, :], ALU.subtract).then_inc(sc["parts_ready"], 1)
            v.wait_ge(sc["abs_done"], c + 1)
            nc.vector.tensor_scalar(dl, banks(0, 2), V(V_BDT), 0.0, ALU.add, ALU.max).then_inc(sc["pre_used"], 1)
            v.wait_ge(sc["pre_used"], c + 1)
            v.wait_ge(sc["log_done"], c + 1)
            tell(v, nc.vector.tensor_tensor(dl, dl, sp_tmp, ALU.add), sc["delta_ready"], c + 1)
            vchain(v, nc.vector.tensor_tensor(du, dl, u[:, tok], ALU.mult))
            for j in range(PAIRS):
                s = c * PAIRS + j
                slot = dBC[:, j % 2, :]
                v.wait_ge(sc["b_psum"], s + 1)
                v.wait_ge(sc["y_done"], s + 1)
                tell(v, nc.vector.tensor_tensor(slot, du, banks(0, 2), ALU.mult), sc["b_used"], s + 1)
                v.wait_ge(sc["exp_done"], s + 1)
                v.wait_ge(sc["hc_done"], s + 1)
                tell(v, nc.vector.tensor_tensor_scan(hs, dA[:, j % 2, :], slot, carry[:, j:j + 1], ALU.mult, ALU.add),
                     sc["h_done"], s + 3)
                nc.vector.tensor_copy(carry[:, j:j + 1], hs[:, CHUNK - 1:CHUNK])
                v.wait_ge(sc["c_psum"], s + 1)
                nc.vector.tensor_tensor(slot, hs, banks(2, 2), ALU.mult).then_inc(sc["hc_done"], 1)
            v.wait_ge(sc["y_done"], c * PAIRS + PAIRS + 2)
            vchain(v, nc.vector.scalar_tensor_tensor(sp_tmp[0:DI, :], u[0:DI, tok], V(V_D, rows=slice(0, DI)),
                                                     banks(4, 2, slice(0, DI)), ALU.mult, ALU.add))
            tell(v, nc.vector.tensor_tensor(zy[:, tok], sp_tmp[0:DI, :], zy[:, tok], ALU.mult), sc["y_used"], c + 2)

        def scan(b):
            with nc.Block() as block:
                @block.tensor
                def _(pe):
                    with nc.tensor.Fori(0, NCHUNK) as i:
                        scan_tensor(pe, b, i, i + NCHUNK * b)

                @block.scalar
                def _(act):
                    with nc.scalar.Fori(0, NCHUNK) as i:
                        achain.enter(i, 1)
                        scan_scalar(act, b, i, i + NCHUNK * b)
                    achain.leave(NCHUNK)

                @block.vector
                def _(v):
                    vchain(v, nc.vector.memset(carry[:, :], 0.0))
                    if b == 0:
                        nc.vector.memset(prime[:, 0:1], 0.0).then_inc(sc["h_done"], 2)
                        nc.vector.memset(prime[:, 1:2], 0.0).then_inc(sc["hc_done"], 1)
                        nc.vector.memset(prime[:, 2:3], 0.0).then_inc(sc["y_done"], 2)
                        nc.vector.memset(prime[:, 3:4], 0.0).then_inc(sc["y_used"], 1)
                        v.wait_ge(sc["y_used"], 1)
                    with nc.vector.Fori(0, NCHUNK) as i:
                        vchain.enter(i, 4)
                        scan_vector(v, b, i, i + NCHUNK * b)
                    vchain.leave(NCHUNK)

        o_psum = sem("o_psum")

        def output_projection(b):
            with nc.Block() as block:
                @block.tensor
                def _(pe):
                    for n in range(4):
                        for h in range(2):
                            q = 2 * b + h
                            last = nc.tensor.matmul(PS[32 * q:32 * q + 32, n, :], wt[0:DI, W_OUT:W_OUT + C],
                                                    zy[:, h * HALF + n * BANK:h * HALF + (n + 1) * BANK], start=True, stop=True)
                    last.then_inc(o_psum, 1)

                @block.vector
                def _(v):
                    rows = slice(64 * b, 64 * b + 64)
                    v.wait_ge(o_psum, b + 1)
                    vchain(v, nc.vector.tensor_tensor(X[rows, :], X[rows, :], banks(0, 4, rows), ALU.add))

        SETS, SET = 4, 8
        SLOTS = 4
        GLEN = (H + 2) * W
        G3s = [sb("G3", [96, GLEN])[:, :], UZ[0:96, 0:GLEN]]
        tab = XN[:, :, :].rearrange("p b n -> p (b n)").rearrange("p (x k c) -> p x k c", k=4, c=C)
        idx_all = sb("idx_all", [P, (GROUPS + SET) * TAPS], U32)
        idx_set = sb("idx_set", [P, 2, SET * TAPS], U32)
        coef = sb("coef", [P, GROUPS, TAPS, 4])
        tables = [nc.dram_tensor(f"corner_table_{b}", (L, 4 * C), F32, kind="Internal").ap() for b in range(B)]
        l3 = {n: sem("l3_" + n) for n in (
            "stats", "totals", "sqrt_go", "sqrt_done", "g_ready", "corner_ready", "shift_done", "below_ready", "table_in",
            "zeroed", "g3_in", "g3_ready", "off_psum", "mask_in", "mask_exp", "base_in", "resid_in",
            "idx_ready", "prod_done", "t_psum", "t_read", "o_psum", "o_read", "out_dma")}
        gathered = [sem(f"gathered{k}") for k in range(SLOTS)]

        def prepare_gather(b):
            rows = slice(64 * b, 64 * b + 64)
            G3 = G3s[b]
            n = GROUPS * TAPS

            def temp(first, count):
                return scratch[:, first:first + count]

            g4 = temp(0, HALF)
            bases, yx, corner0 = (temp(HALF + 2 * n * k, 2 * n).rearrange("p (g k) -> p g k", k=2 * TAPS) for k in range(3))
            hat = temp(HALF + 6 * n, 4 * n).rearrange("p (r g k) -> p r g k", r=2, k=2 * TAPS)
            msk = temp(HALF + 10 * n, n).rearrange("p (g k) -> p g k", k=TAPS)
            cm = temp(HALF + 11 * n, 2 * n).rearrange("p (r g k) -> p r g k", r=2, k=TAPS)
            if True:
                with nc.Block() as block:
                    @block.sync
                    def _(sp):
                        sp.dma_start(bases[:, :, :].rearrange("p g k -> p (g k)"), base).then_inc(l3["base_in"], 16)
                        sp.wait_ge(l3["zeroed"], b + 1)
                        sp.wait_ge(l3["g_ready"], b + 1)
                        for h in range(2):
                            for j in range(3):
                                first = W + h * HALF - (j - 1)
                                sp.dma_start(G3[32 * j:32 * j + 32, first:first + HALF],
                                             g4[64 * b + 32 * h:64 * b + 32 * h + 32, :]).then_inc(l3["g3_in"], 16)
                        sp.wait_ge(l3["corner_ready"], b + 1)
                        sp.wait_ge(l3["below_ready"], b + 1)
                        sp.dma_start(tables[b].rearrange("(y x) n -> y (x n)", y=H),
                                     tab[rows, :, :, :].rearrange("p x k c -> p (x k c)")).then_inc(l3["table_in"], 16)
                        sp.wait_ge(l3["table_in"], 16 * (b + 1))

                    @block.tensor
                    def _(pe):
                        pe.wait_ge(l3["stats"], b + 1)
                        nc.tensor.matmul(PS[rows, 0, 0:2], M(M_OWN, rows, rows), S2[rows, :], start=True, stop=True).then_inc(l3["totals"], 1)
                        pe.wait_ge(l3["corner_ready"], b + 1)
                        for n in range(4):
                            last = nc.tensor.matmul(PS[rows, n, :], M(M_DOWN, rows, rows), tab[rows, 16 * n:16 * n + 16, 0, :],
                                                    start=True, stop=True)
                        last.then_inc(l3["shift_done"], 1)
                        pe.wait_ge(l3["g3_ready"], b + 1)
                        for q in range(GROUPS):
                            o = PS[:, 4 + q // 16, 32 * (q % 16):32 * (q % 16) + 27]
                            for dy in range(3):
                                last = nc.tensor.matmul(o, G3[:, (2 * q + dy) * W:(2 * q + dy) * W + P],
                                                        wt[0:96, W_OFF + 27 * dy:W_OFF + 27 * dy + 27], start=(dy == 0), stop=(dy == 2))
                        last.then_inc(l3["off_psum"], 1)

                    @block.scalar
                    def _(act):
                        act.wait_ge(l3["sqrt_go"], b + 1)
                        nc.scalar.activation(std[rows, 0:1], std[rows, 0:1], ACT.Sqrt).then_inc(l3["sqrt_done"], 1)
                        act.wait_ge(l3["shift_done"], b + 1)
                        below = banks(0, 4, rows).rearrange("p (x c) -> p x c", c=C)
                        nc.scalar.activation(tab[rows, :, 2, :], below, ACT.Copy)
                        nc.scalar.activation(tab[rows, 0:W - 1, 3, :], below[:, 1:W, :], ACT.Copy).then_inc(l3["below_ready"], 1)
                        act.wait_ge(l3["mask_in"], b + 1)
                        nc.scalar.activation(msk[:, :, :], msk[:, :, :], ACT.Exp, scale=-1.0).then_inc(l3["mask_exp"], 1)

                    @block.vector
                    def _(v):
                        vchain(v, nc.vector.memset(G3[:, 0:W], 0.0))
                        tell(v, nc.vector.memset(G3[:, GLEN - W:GLEN], 0.0), l3["zeroed"], b + 1)
                        if b == 0:
                            vchain(v, nc.vector.memset(idx_all[:, GROUPS * TAPS:], 0))
                        gn_partition_stats(v, rows).then_inc(l3["stats"], 1)
                        v.wait_ge(l3["totals"], b + 1)
                        vchain(v, nc.vector.tensor_copy(tot[rows, 0:2], PS[rows, 0, 0:2]))
                        variance(v, 1, GN_EPS, rows).then_inc(l3["sqrt_go"], 1)
                        v.wait_ge(l3["sqrt_done"], b + 1)
                        vchain(v, nc.vector.reciprocal(rstd[rows, 0:1], std[rows, 0:1]))
                        vchain(v, nc.vector.scalar_tensor_tensor(nmrs[rows, :], tot[rows, 0:1], -1.0, rstd[rows, 0:1], ALU.mult, ALU.mult))
                        tell(v, nc.vector.tensor_scalar(g4[rows, :], X[rows, :], rstd[rows, 0:1], nmrs[rows, :], ALU.mult, ALU.add),
                             l3["g_ready"], b + 1)
                        vchain(v, nc.vector.memset(tab[rows, W - 1, 1::2, :], 0.0))
                        vchain(v, nc.vector.transpose(tab[rows, :, 0, :], g4[rows, :].rearrange("p (y x) -> p x y", x=W)))
                        tell(v, nc.vector.tensor_copy(tab[rows, 0:W - 1, 1, :], tab[rows, 1:W, 0, :]), l3["corner_ready"], b + 1)
                        cols = G3[:, :].rearrange("p (y x) -> p y x", x=W)
                        v.wait_ge(l3["g3_in"], 96 * (b + 1))
                        vchain(v, nc.vector.memset(cols[0:32, :, 0], 0.0))
                        tell(v, nc.vector.memset(cols[64:96, :, W - 1], 0.0), l3["g3_ready"], b + 1)
                        v.wait_ge(l3["base_in"], 16 * (b + 1))
                        v.wait_ge(l3["off_psum"], b + 1)
                        om = banks(4, 2).rearrange("p (g k) -> p g k", k=32)
                        vchain(v, nc.vector.tensor_tensor(yx[:, :, :], om[:, :, 0:18], bases[:, :, :], ALU.add))
                        tell(v, nc.vector.tensor_copy(msk[:, :, :], om[:, :, 18:27]), l3["mask_in"], b + 1)
                        vchain(v, nc.vector.tensor_scalar(corner0[:, :, :], yx[:, :, :], 0.5, 0.0, ALU.subtract, ALU.max))
                        vchain(v, nc.vector.tensor_scalar(corner0[:, :, :], corner0[:, :, :], float(H - 2), ROUND, ALU.min, ALU.add))
                        vchain(v, nc.vector.tensor_scalar(corner0[:, :, :], corner0[:, :, :], ROUND, None, ALU.subtract))
                        vchain(v, nc.vector.tensor_tensor(hat[:, 0, :, :], yx[:, :, :], corner0[:, :, :], ALU.subtract))
                        vchain(v, nc.vector.tensor_scalar(hat[:, 1, :, :], hat[:, 0, :, :], 1.0, None, ALU.subtract))
                        flat = hat[:, :, :, :].rearrange("p r g k -> p (r g k)")
                        vchain(v, nc.vector.scalar_tensor_tensor(flat, flat, -1.0, flat, ALU.mult, ALU.min))
                        vchain(v, nc.vector.tensor_scalar(flat, flat, 1.0, 0.0, ALU.add, ALU.max))
                        vchain(v, nc.vector.scalar_tensor_tensor(
                            idx_all[:, 0:GROUPS * TAPS].rearrange("p (g k) -> p g k", k=TAPS),
                            corner0[:, :, 0::2], float(W), corner0[:, :, 1::2], ALU.mult, ALU.add))
                        v.wait_ge(l3["mask_exp"], b + 1)
                        vchain(v, nc.vector.tensor_scalar(msk[:, :, :], msk[:, :, :], 1.0, None, ALU.add))
                        vchain(v, nc.vector.reciprocal(msk[:, :, :], msk[:, :, :]))
                        for r in range(2):
                            vchain(v, nc.vector.tensor_tensor(cm[:, r, :, :], hat[:, r, :, 0::2], msk[:, :, :], ALU.mult))
                            for s in range(2):
                                vchain(v, nc.vector.tensor_tensor(coef[:, :, :, 2 * r + s], cm[:, r, :, :], hat[:, s, :, 1::2], ALU.mult))

        got = sb("got", [P, SLOTS, TAPS, 4, C])
        prodg = sb("prodg", [P, TAPS, 4, C])
        colT = sb("colT", [P, TAPS, P])


        def gather_pool(pool, b, i):
            for half in range(2):
                pool.wait_ge(l3["idx_ready"], i * 2 + (5 * b + half + 1))
                for k in range(SET):
                    n = 8 * half + k
                    pool.wait_ge(l3["prod_done"], i * 16 + (32 * b + n + 1))
                    pool.nop(nofuse=True)
                    for tap in range(TAPS):
                        pool.indirect_dma_start(got[:, n % SLOTS, tap, :, :].rearrange("p k c -> p (k c)"), None, tables[b],
                                                bass.IndirectOffsetOnAxis(ap=idx_set[:, half, TAPS * k + tap:TAPS * k + tap + 1], axis=0)
                                                ).then_inc(gathered[n % SLOTS], 16)

        def gather_vector(v, b, i):
            xr = G3s[b][0:C, 0:L]
            for half in range(2):
                nc.vector.tensor_copy(idx_set[:, 1 - half, :], idx_all[:, bass.ds(i * (2 * SET * TAPS) + (half + 1) * SET * TAPS, SET * TAPS)]
                                      ).then_inc(l3["idx_ready"], 1)
                for k in range(SET):
                    n = 8 * half + k
                    v.wait_ge(gathered[n % SLOTS], i * (4 * 16 * TAPS) + 16 * TAPS * (8 * b + n // SLOTS + 1))
                    nc.vector.tensor_tensor(prodg[:, :, :, :].rearrange("p t k c -> p (t k) c"),
                                            got[:, n % SLOTS, :, :, :].rearrange("p t k c -> p (t k) c"),
                                            coef[:, bass.ds(i * 16 + n, 1), :, :].rearrange("p o t k -> p (o t k)").unsqueeze(2).to_broadcast([P, TAPS * 4, C]),
                                            ALU.mult).then_inc(l3["prod_done"], 1)
                    v.wait_ge(l3["o_psum"], i * 16 + (32 * b + n + 2))
                    px = bass.ds(i * (16 * P) + n * P, P)
                    nc.vector.tensor_tensor(xr[:, px], xr[:, px], PS[0:C, 7, 0:P], ALU.add).then_inc(l3["o_read"], 1)

        def gather_tensor(pe, b, i):
            for n in range(16):
                pe.wait_ge(l3["prod_done"], i * 16 + (32 * b + n + 5))
                for r in range(3):
                    pe.wait_ge(l3["t_read"], i * 48 + (3 * (32 * b + n) + r + 1))
                    for t in range(3):
                        last = nc.tensor.transpose(PS[:, 6, t * P:t * P + P], prodg[:, 3 * r + t, :, :].rearrange("p k c -> p (k c)"), ident)
                    last.then_inc(l3["t_psum"], 1)
                pe.wait_ge(l3["t_read"], i * 48 + (3 * (32 * b + n) + 4))
                pe.wait_ge(l3["o_read"], i * 16 + (32 * b + n + 1))
                for tap in range(TAPS):
                    last = nc.tensor.matmul(PS[0:C, 7, 0:P], wt[:, W_L3 + C * tap:W_L3 + C * tap + C], colT[:, tap, :],
                                            start=(tap == 0), stop=(tap == TAPS - 1))
                last.then_inc(l3["o_psum"], 1)

        def gather_scalar(act, b, i):
            for n in range(16):
                act.wait_ge(l3["o_psum"], i * 16 + (32 * b + n + 1))
                for r in range(3):
                    act.wait_ge(l3["t_psum"], i * 48 + (3 * (32 * b + n) + r + 1))
                    nc.scalar.activation(colT[:, 3 * r:3 * r + 3, :], PS[:, 6, 0:3 * P].rearrange("p (t n) -> p t n", t=3),
                                         ACT.Copy).then_inc(l3["t_read"], 1)

        def deform(b):
            xr = G3s[b][0:C, 0:L]
            with nc.Block() as block:
                @block.sync
                def _(sp):
                    for h in range(2):
                        q = 2 * b + h
                        sp.dma_start(xr[:, h * HALF:(h + 1) * HALF], X[32 * q:32 * q + 32, :]).then_inc(l3["resid_in"], 16)
                    sp.wait_ge(l3["o_read"], 32 * (b + 1) + 1)
                    sp.dma_start(out[b].rearrange("c y x -> c (y x)"), xr[:, :]).then_inc(l3["out_dma"], 16)
                    sp.wait_ge(l3["out_dma"], 16 * (b + 1))

                @block.gpsimd
                def _(pool):
                    with nc.gpsimd.Fori(0, 2) as i:
                        gather_pool(pool, b, i)

                @block.tensor
                def _(pe):
                    with nc.tensor.Fori(0, 2) as i:
                        gather_tensor(pe, b, i)

                @block.scalar
                def _(act):
                    with nc.scalar.Fori(0, 2) as i:
                        gather_scalar(act, b, i)

                @block.vector
                def _(v):
                    if b == 0:
                        vchain(v, nc.vector.memset(prodg[:, :, :, :], 0.0))
                        nc.vector.memset(prime[:, 0:1], 0.0).then_inc(l3["prod_done"], 4)
                        nc.vector.memset(prime[:, 1:2], 0.0).then_inc(l3["t_read"], 1)
                        nc.vector.memset(prime[:, 2:3], 0.0).then_inc(l3["o_psum"], 1)
                        nc.vector.memset(prime[:, 3:4], 0.0).then_inc(l3["o_read"], 1)
                    nc.vector.tensor_copy(idx_set[:, 0, :], idx_all[:, 0:SET * TAPS]).then_inc(l3["idx_ready"], 1)
                    v.wait_ge(l3["resid_in"], 32 * (b + 1))
                    with nc.vector.Fori(0, 2) as i:
                        gather_vector(v, b, i)

        for b in range(B):
            project(b)
            scan(b)
            output_projection(b)
        for b in range(B):
            prepare_gather(b)
            deform(b)



def _square_constants():
    m = np.zeros((NMAT, P, P), np.float32)
    i = np.arange(P)
    m[M_IDENT] = np.eye(P)
    same_channel = i[:, None] % C == i[None, :] % C
    m[M_OWN] = 0.5 * (same_channel & (i[:, None] // 64 == i[None, :] // 64))
    m[M_PRE] = 0.5 * (same_channel & (i[:, None] // 64 == 1))
    same_quadrant = i[:, None] // C == i[None, :] // C
    m[M_PAIR] = 0.5 * (same_quadrant & (i[:, None] // 2 == i[None, :] // 2))
    m[M_MEAN] = same_quadrant / C
    m[M_CENTER] = m[M_IDENT] - m[M_MEAN]
    for b in range(B):
        for y in range(H):
            o = H * b + y
            m[M_LAP, o, o] = 4.0
            for s in (y - 1, y + 1):
                if 0 <= s < H:
                    m[M_LAP, H * b + s, o] = -1.0
            m[M_DOWN, H * b + (y + 1 if y < H - 1 else H - 2), o] = 1.0
            m[M_UPR, H * b + (y - 1 if y else 1), o] = 1.0
            if y:
                m[M_UP, o - 1, o] = 1.0
            else:
                m[M_UP0, o, o] = 1.0
        m[M_PICKB, b, H * b:H * b + H] = 1.0
    return np.ascontiguousarray(m.transpose(1, 0, 2))


def _bicubic_weights(out_size, in_size):
    f = np.float32
    src = (np.arange(out_size, dtype=f) + f(0.5)) * f(in_size / out_size) - f(0.5)
    i0 = np.floor(src)
    at = np.abs((src - i0)[:, None] - np.arange(-1, 3).astype(f)[None, :])
    a = f(-0.75)
    near = ((a + f(2)) * at - (a + f(3))) * at * at + f(1)
    far = (((at - f(5)) * at + f(8)) * at - f(4)) * a
    w = np.where(at <= 1, near, np.where(at < 2, far, f(0))).astype(f)
    idx = np.clip(i0[:, None].astype(np.int32) + np.arange(-1, 3)[None, :], 0, in_size - 1)
    m = np.zeros((out_size, in_size), f)
    np.add.at(m, (np.arange(out_size)[:, None], idx), w)
    return m


def _bicubic_rows():
    wy = _bicubic_weights(3 * H, 4)[H // 2:H // 2 + H]
    wx = _bicubic_weights(3 * W, 4)[W // 2:W // 2 + W]
    k = (wy.T[:, None, :, None] * wx.T[None, :, None, :]).reshape(16, L)
    replaced = (5 + 1 - 4) * 4 + (6 + 1 - 5)
    rows = np.zeros((64, HALF), np.float32)
    for h in range(2):
        part = k[:, h * HALF:(h + 1) * HALF]
        rows[h] = part[replaced]
        rows[32 + 16 * h:48 + 16 * h] = part
        rows[32 + 16 * h + replaced] = 0.0
    rows[2] = 1.0
    return rows


def _sample_base():
    p = np.arange(P)[:, None, None]
    g = np.arange(GROUPS)[None, :, None]
    k = np.arange(TAPS)[None, None, :]
    y = 2 * g + p // W - 1 + k // 3
    x = p % W - 1 + k % 3 + 0 * g
    return np.ascontiguousarray(np.stack([y, x], axis=-1).astype(np.float32).reshape(P, GROUPS * TAPS * 2))


def _selectors():
    s = np.zeros((96, 2, PAIRS, 2, DI), np.float32)
    for part in range(3):
        for j in range(PAIRS):
            for h in range(2):
                s[32 * part + 2 * j + h, 0, j, h] = 1.0
                s[32 * part + 16 + 2 * j + h, 1, j, h] = 1.0
    return s.reshape(96, 2 * PAIRS * P)


def kernel(**inputs):
    import concourse.bacc as _bacc
    from concourse.bass_utils import run_bass_kernel_spmd as _run

    a = {k: np.asarray(v) for k, v in inputs.items()}
    rep = lambda v, n: np.tile(np.reshape(v, -1), n)
    vecs = np.zeros((P, NV), np.float32)
    for col, v in ((V_W0, rep(a["L0_conv_weight"], 4)), (V_B0, rep(a["L0_conv_bias"], 4)),
                   (V_GNW, rep(a["L1_conv_gn_weight"], 4)), (V_GNB, rep(a["L1_conv_gn_bias"], 4)),
                   (V_B1, rep(a["L1_conv_b1"], 2)), (V_B2, rep(a["L1_conv_b2"], 4)),
                   (V_LNW, rep(a["L2_conv_ln_w"], 4)), (V_LNB, rep(a["L2_conv_ln_b"], 4)),
                   (V_CB, rep(a["L2_conv_conv_b"], 2)), (V_BDT, rep(a["L2_conv_b_dt"], 2)),
                   (V_D, rep(a["L2_conv_D"], 2))):
        vecs[:, col] = v
    vecs[:, V_A:V_A + PAIRS] = a["L2_conv_A_log"].reshape(DI, PAIRS, 2).transpose(2, 0, 1).reshape(P, PAIRS)
    vecs[0:32, V_M3] = vecs[32:64, V_M3 + 1] = vecs[64:128, V_M3 + 2] = 1.0
    vecs[:, V_EPS] = GN_EPS
    vecs[32:48, V_HALF] = vecs[48:64, V_HALF + 1] = 1.0

    w = np.zeros((P, NW), np.float32)
    for q in range(4):
        r = q % 2
        w[32 * q:32 * q + 32, W_ONE + 64 * r:W_ONE + 64 * r + 64] = a["L1_conv_w1"].T
    for q in range(2):
        w[64 * q:64 * q + 64, W_TWO + 32 * q:W_TWO + 32 * q + 32] = a["L1_conv_w2"].T
    for j in range(4):
        for d in range(2):
            w[32 * j:32 * j + 32, W_INX + 64 * d:W_INX + 64 * d + 64] = a["L2_conv_W_in"][:DI].T
            w[32 * j:32 * j + 32, W_CONV + 64 * d:W_CONV + 64 * d + 64] = a["L2_conv_conv_w"][:, j]
    w[96:128, W_INZ:W_INZ + 64] = a["L2_conv_W_in"][DI:].T
    for part in range(3):
        w[0:64, W_BC + 32 * part:W_BC + 32 * part + 32] = a["L2_conv_W_xproj"][2:].T
    w[0:2, W_DTA:W_DTA + 64] = a["L2_conv_W_xproj"][0:2]
    for d in range(2):
        w[0:2, W_DTB + 64 * d:W_DTB + 64 * d + 64] = a["L2_conv_W_dt"].T
        w[64 * d:64 * d + 64, W_SUM:W_SUM + 64] = np.eye(DI)
    w[0:64, W_OUT:W_OUT + 32] = a["L2_conv_W_out"].T
    taps = np.concatenate([a["L3_conv_offset_w"], a["L3_conv_mask_w"]], axis=0)
    w[0:96, W_OFF:W_OFF + 81] = taps.transpose(3, 1, 2, 0).reshape(96, 81)
    l3 = a["L3_conv_weight"].reshape(C, C, TAPS).transpose(1, 2, 0).reshape(C, TAPS * C)
    for corner in range(4):
        w[32 * corner:32 * corner + 32, W_L3:W_L3 + TAPS * C] = l3

    anchors = np.zeros((32, 2, C), np.float32)
    for s, name in enumerate(("L0_conv_mean_table", "L0_conv_std_table")):
        for h in range(2):
            anchors[16 * h:16 * h + 16, s] = a[name][3:7, 4:8].reshape(16, C)

    arrays = {"x": np.ascontiguousarray(a["x"]), "mats": _square_constants(), "vecs": vecs, "wts": w,
              "bic": _bicubic_rows(), "anchors": anchors, "base": _sample_base(), "sel": _selectors()}
    nc = _bacc.Bacc("TRN2", target_bir_lowering=False, num_devices=1)
    args = [nc.dram_tensor(f"in_{k}", v.shape, F32, kind="ExternalInput").ap() for k, v in arrays.items()]
    args.append(nc.dram_tensor("out_x", (B, C, H, W), F32, kind="ExternalOutput").ap())
    build(nc, *args)
    r = _run(nc, [{f"in_{k}": v for k, v in arrays.items()}], core_ids=[0])
    return r.results[0]["out_x"]
```

```python
import concourse.bass as bass
import numpy as np
from concourse import mybir
from contextlib import ExitStack

F32 = mybir.dt.float32
BF16 = mybir.dt.bfloat16
U32 = mybir.dt.uint32
ALU = mybir.AluOpType
ACT = mybir.ActivationFunctionType
AX = mybir.AxisListType

P = 128
B, C, H, W = 2, 32, 64, 64
L = H * W
HALF = L // 2
BANK = 512
WP = W + 2
DI = 64
DS = 16
PAIRS = DS // 2
CHUNK = 1024
NCHUNK = L // CHUNK
TAPS = 9
SLOTS = 6
GROUPS = L // P
QUARTER = L // 4
GN_EPS = 1e-5
ROUND = 12582912.0

(M_IDENT, M_OWN, M_PRE, M_PAIR, M_CENTER, M_MEAN, M_LAP, M_DOWN, M_UPR, M_UP, M_UP0, M_PICKB) = range(12)
NMAT = 12
(V_W0, V_B0, V_GNW, V_GNB, V_B1, V_B2, V_LNW, V_LNB, V_CB, V_BDT, V_D) = range(11)
V_A = 11
V_M3 = V_A + PAIRS
V_HALF = V_M3 + 3
V_EPS = V_HALF + 2
NV = V_EPS + 1
W_ONE = 0
W_TWO = W_ONE + 2 * 128
W_INX = W_TWO + 64
W_CONV = W_INX + 128
W_INZ = W_CONV + 128
W_BC = W_INZ + 128
W_DTA = W_BC + 96
W_DTB = W_DTA + 64
W_OUT = W_DTB + 128
W_SUM = W_OUT + 32
W_OFF = W_SUM + 128
W_L3 = W_OFF + 3 * 32
NW = W_L3 + 4 * 32


class Chain:

    def __init__(self, sem):
        self.sem, self.n, self.loop = sem, 0, 0

    def __call__(self, engine, ins):
        ins.then_inc(self.sem, 1)
        self.n += 1
        engine.wait_ge(self.sem, self.loop + self.n)

    def enter(self, i, per_turn):
        self.start, self.per_turn, self.loop = self.n, per_turn, i * per_turn

    def leave(self, turns):
        assert self.n == self.start + self.per_turn, (self.n - self.start, self.per_turn)
        self.n, self.loop = self.start + self.per_turn * turns, 0
def build(nc, x, mats, vecs, wts, bic, anchors, base, sel, out):
    ctx = ExitStack()
    with ctx:
        def sb(name, shape, dt=F32):
            return ctx.enter_context(nc.sbuf_tensor(name, shape, dt))

        def sem(name):
            return ctx.enter_context(nc.semaphore(name))

        X = sb("X", [P, HALF])
        mat = sb("mat", [P, NMAT, P])
        vec = sb("vec", [P, NV])
        wt = sb("wt", [P, NW])
        PS = ctx.enter_context(nc.psum_tensor("PS", [P, 8, BANK], F32))

        def M(k, rows=slice(0, P), cols=slice(0, P)):
            return mat[rows, k, cols]

        def V(k, n=1, rows=slice(0, P)):
            return vec[rows, k:k + n]

        ident = M(M_IDENT)
        x_half = x.rearrange("b c (h y) w -> b h c (y w)", h=2)
        out_half = out.rearrange("b c (h y) w -> b h c (y w)", h=2)
        vchain, achain, pchain, gchain = Chain(sem("dve_own")), Chain(sem("act_own")), Chain(sem("pe_own")), Chain(sem("pool_own"))

        def banks(first, n, rows=slice(0, P)):
            return PS[rows, first:first + n, :].rearrange("p b n -> p (b n)")

        def tell(engine, ins, signal, n=1):
            ins.then_inc(signal, 1)
            engine.wait_ge(signal, n)

        st6 = sb("st6", [P, 4, 6])
        mv = sb("mv", [P, 2])
        S2 = sb("S2", [P, 2])
        tot = sb("tot", [P, 4])
        var = sb("var", [P, 2])
        std = sb("std", [P, 2])
        rstd = sb("rstd", [P, 2])
        mrs = sb("mrs", [P, 2])
        nmrs = sb("nmrs", [P, 1])

        def gn_partition_stats(v, rows=slice(0, P)):
            for q in range(4):
                vchain(v, nc.vector.bn_stats(st6[rows, q, :], X[rows, q * BANK:(q + 1) * BANK]))
            vchain(v, nc.vector.bn_aggr(mv[rows, :], st6[rows, :, :].rearrange("p a b -> p (a b)")))
            vchain(v, nc.vector.tensor_copy(S2[rows, 0:1], mv[rows, 0:1]))
            return nc.vector.scalar_tensor_tensor(S2[rows, 1:2], mv[rows, 0:1], mv[rows, 0:1], mv[rows, 1:2],
                                                  ALU.mult, ALU.add)

        def variance(v, n, eps, rows=slice(0, P)):
            pairs = tot[rows, 0:2 * n].rearrange("p (n s) -> p n s", s=2)
            vchain(v, nc.vector.tensor_tensor(var[rows, 0:n], pairs[:, :, 0], pairs[:, :, 0], ALU.mult))
            vchain(v, nc.vector.tensor_tensor(var[rows, 0:n], pairs[:, :, 1], var[rows, 0:n], ALU.subtract))
            return nc.vector.tensor_scalar(std[rows, 0:n], var[rows, 0:n], eps, None, ALU.add)

        with ExitStack() as stage:
            bicubic = stage.enter_context(nc.sbuf_tensor("bicubic", [P, HALF], F32))
            patch = stage.enter_context(nc.sbuf_tensor("patch", [64, 2, 32], F32))
            LMS = stage.enter_context(nc.sbuf_tensor("LMS", [P, 2, P], F32))
            D = stage.enter_context(nc.sbuf_tensor("D", [P, 2, 3], F32))
            t1 = stage.enter_context(nc.sbuf_tensor("t1", [P, HALF], F32))
            xb = stage.enter_context(nc.sbuf_tensor("xb", [P, HALF], F32))
            pv = stage.enter_context(nc.sbuf_tensor("pv", [P, 3], F32))
            x_in, mat_in, vec_in, bic_in, rest_in = (sem(n) for n in ("x_in", "mat_in", "vec_in", "bic_in", "rest_in"))
            bic_zero = sem("bic_zero")
            stats0, totals0, sqrt0_go, sqrt0_done, d_ready, dt_done, l_ready, maps_done, xb_done = (
                sem(n) for n in ("stats0", "totals0", "sqrt0_go", "sqrt0_done", "d_ready", "dt_done", "l_ready",
                                 "maps_done", "xb_done"))
            with nc.Block() as block:
                @block.sync
                def _(sp):
                    for b in range(B):
                        for h in range(2):
                            q = 2 * b + h
                            sp.dma_start(X[32 * q:32 * q + 32, :], x_half[b, h]).then_inc(x_in, 16)
                    sp.dma_start(bicubic[0:64, :], bic).then_inc(bic_in, 16)
                    sp.dma_start(wt[:, :], wts).then_inc(rest_in, 16)
                    sp.wait_ge(rest_in, 16)

                @block.scalar
                def _(act):
                    act.dma_start(vec[:, :], vecs).then_inc(vec_in, 16)
                    act.dma_start(mat[:, :, :], mats).then_inc(mat_in, 16)
                    act.dma_start(patch[32:64, :, :], anchors).then_inc(vec_in, 16)
                    act.wait_ge(x_in, 64)
                    act.wait_ge(vec_in, 32)
                    nc.scalar.activation(xb[:, :], X[:, :], ACT.Identity, bias=V(V_B0)).then_inc(xb_done, 1)
                    act.wait_ge(sqrt0_go, 1)
                    nc.scalar.activation(std[:, :], std[:, :], ACT.Sqrt).then_inc(sqrt0_done, 1)
                    act.wait_ge(sqrt0_go, 2)
                    nc.scalar.activation(pv[:, 1:2], pv[:, 0:1], ACT.Sqrt).then_inc(sqrt0_done, 1)

                @block.gpsimd
                def _(pool):
                    nc.gpsimd.memset(bicubic[64:P, :], 0.0).then_inc(bic_zero, 1)

                @block.tensor
                def _(pe):
                    pe.wait_ge(mat_in, 16)
                    pe.wait_ge(stats0, 1)
                    nc.tensor.matmul(PS[:, 0, 0:2], M(M_OWN), S2[:, :], start=True, stop=True)
                    nc.tensor.matmul(PS[:, 0, 2:4], M(M_PRE), S2[:, :], start=True, stop=True).then_inc(totals0, 1)
                    pe.wait_ge(d_ready, 1)
                    for s in range(2):
                        last = nc.tensor.transpose(PS[0:3, 1, s * P:s * P + P], D[:, s, :], ident)
                    last.then_inc(dt_done, 1)
                    pe.wait_ge(bic_in, 16)
                    pe.wait_ge(bic_zero, 1)
                    pe.wait_ge(l_ready, 1)
                    for s in range(2):
                        for n in range(4):
                            last = nc.tensor.matmul(PS[:, 4 * s + n, :], LMS[:, s, :], bicubic[:, n * BANK:(n + 1) * BANK],
                                                    start=True, stop=True)
                    last.then_inc(maps_done, 1)

                @block.vector
                def _(v):
                    vchain(v, nc.vector.memset(LMS[:, :, :], 0.0))
                    v.wait_ge(vec_in, 32)
                    vchain(v, nc.vector.reciprocal(patch[32:64, 1, :], patch[32:64, 1, :]))
                    for s in range(2):
                        for h in range(2):
                            vchain(v, nc.vector.tensor_scalar(LMS[32:64, s, 32 * h:32 * h + 32], patch[32:64, s, :],
                                                              vec[32:64, V_HALF + h:V_HALF + h + 1], None, ALU.mult))
                    v.wait_ge(x_in, 64)
                    gn_partition_stats(v).then_inc(stats0, 1)
                    v.wait_ge(totals0, 1)
                    vchain(v, nc.vector.tensor_copy(tot[:, :], PS[:, 0, 0:4]))
                    variance(v, 2, GN_EPS).then_inc(sqrt0_go, 1)
                    v.wait_ge(sqrt0_done, 1)
                    vchain(v, nc.vector.reciprocal(rstd[:, :], std[:, :]))
                    vchain(v, nc.vector.tensor_tensor(mrs[:, :], tot[:, 0:4:2], rstd[:, :], ALU.mult))
                    vchain(v, nc.vector.tensor_tensor(pv[:, 0:1], rstd[:, 1:2], rstd[:, 1:2], ALU.mult))
                    tell(v, nc.vector.tensor_scalar(pv[:, 0:1], pv[:, 0:1], var[:, 1:2], float(L) / (L - 1), ALU.mult, ALU.mult), sqrt0_go, 2)
                    vchain(v, nc.vector.tensor_scalar(pv[:, 2:3], tot[:, 2:3], rstd[:, 1:2], mrs[:, 1:2], ALU.mult, ALU.subtract))
                    v.wait_ge(sqrt0_done, 2)
                    vchain(v, nc.vector.reciprocal(pv[:, 1:2], pv[:, 1:2]))
                    vchain(v, nc.vector.tensor_scalar(D[:, 0, :], V(V_M3, 3), pv[:, 2:3], None, ALU.mult))
                    vchain(v, nc.vector.tensor_scalar(D[:, 1, :], V(V_M3, 3), pv[:, 1:2], None, ALU.mult))
                    nc.vector.tensor_tensor(D[:, 0, 2:3], D[:, 0, 2:3], mrs[:, 0:1], ALU.add).then_inc(d_ready, 1)
                    v.wait_ge(dt_done, 1)
                    nc.vector.tensor_copy(LMS[0:3, :, :], PS[0:3, 1, 0:2 * P].rearrange("p (s n) -> p s n", s=2)).then_inc(l_ready, 1)
                    v.wait_ge(maps_done, 1)
                    vchain(v, nc.vector.scalar_tensor_tensor(t1[:, :], X[:, :], rstd[:, 0:1], banks(0, 4), ALU.mult, ALU.subtract))
                    vchain(v, nc.vector.tensor_tensor(t1[:, :], t1[:, :], banks(4, 4), ALU.mult))
                    v.wait_ge(xb_done, 1)
                    vchain(v, nc.vector.scalar_tensor_tensor(X[:, :], t1[:, :], V(V_W0), xb[:, :], ALU.mult, ALU.add))

        with ExitStack() as stage:
            def tile(name, shape, dt=F32):
                return stage.enter_context(nc.sbuf_tensor(name, shape, dt))

            G = tile("G", [P, HALF])
            GR = tile("GR", [P, WP, C])
            GD = tile("GD", [P, WP, C])
            GU = tile("GU", [P, WP, C])
            NPROD = 4
            prod = tile("prod", [P, NPROD, WP, C])
            avg = tile("avg", [P, WP])
            df = tile("df", [P, 2, W])
            mm = tile("mm", [P, 2])
            mmT = tile("mmT", [2, B])
            mmB = tile("mmB", [B, 2])
            rng = tile("rng", [P, 4])
            kval = tile("kval", [P, W])
            n2 = tile("n2", [P, 2, W])
            rn = tile("rn", [P, 3, WP])
            ER = tile("ER", [P, WP])
            VD = tile("VD", [P, 3, WP])
            sim = tile("sim", [P, TAPS, W])
            cmp = tile("cmp", [P, TAPS, W])
            rank = tile("rank", [P, TAPS, W])
            wk = tile("wk", [P, TAPS, W])
            wsum = tile("wsum", [P, 2, W])
            gn2 = tile("gn2", [P, 8])
            enh = tile("enh", [P, HALF])
            hid = tile("hid", [P, 2, HALF])
            names = ("stats1", "totals1", "sqrt1_go", "sqrt1_done", "g_done", "gn_stats", "gn_totals", "gr_ready",
                     "shift_done", "gd_ready", "lap_in", "lap_done", "mm_ready", "mmT_done", "mmT_ready", "mmB_done",
                     "mmB_ready", "rng_done", "norm2_ready", "norm_done", "rn_ready", "rn_shift_done", "vd_ready", "dm_done",
                     "sim_ready", "exp_done", "w_ready", "prod_ready", "prod_free", "agg_done", "enh_ready", "h_psum",
                     "h_ready", "f_psum", "pool_prod")
            S = {n: sem("s1_" + n) for n in names}
            with nc.Block() as block:
                @block.vector
                def _(v):
                    gn_partition_stats(v).then_inc(S["stats1"], 1)
                    v.wait_ge(S["totals1"], 1)
                    vchain(v, nc.vector.tensor_copy(tot[:, 0:2], PS[:, 0, 0:2]))
                    variance(v, 1, GN_EPS).then_inc(S["sqrt1_go"], 1)
                    v.wait_ge(S["sqrt1_done"], 1)
                    vchain(v, nc.vector.reciprocal(rstd[:, 0:1], std[:, 0:1]))
                    vchain(v, nc.vector.scalar_tensor_tensor(nmrs[:, :], tot[:, 0:1], -1.0, rstd[:, 0:1], ALU.mult, ALU.mult))
                    vchain(v, nc.vector.tensor_scalar(G[:, :], X[:, :], rstd[:, 0:1], nmrs[:, :], ALU.mult, ALU.add))
                    vchain(v, nc.vector.tensor_scalar(gn2[:, 0:1], tot[:, 0:1], rstd[:, 0:1], nmrs[:, :], ALU.mult, ALU.add))
                    vchain(v, nc.vector.tensor_tensor(gn2[:, 2:3], rstd[:, 0:1], rstd[:, 0:1], ALU.mult))
                    vchain(v, nc.vector.tensor_scalar(gn2[:, 2:3], gn2[:, 2:3], var[:, 0:1], None, ALU.mult))
                    nc.vector.scalar_tensor_tensor(gn2[:, 1:2], gn2[:, 0:1], gn2[:, 0:1], gn2[:, 2:3],
                                                   ALU.mult, ALU.add).then_inc(S["gn_stats"], 1)
                    vchain(v, nc.vector.transpose(GR[:, 1:W + 1, :], G[:, :].rearrange("p (y x) -> p x y", x=W)))
                    tell(v, nc.vector.tensor_copy(GR[:, 0:WP:W + 1, :], GR[:, 2:W:W - 3, :]), S["gr_ready"])
                    v.wait_ge(S["gn_totals"], 1)
                    vchain(v, nc.vector.tensor_copy(tot[:, 0:2], PS[:, 7, 0:2]))
                    variance(v, 1, GN_EPS).then_inc(S["sqrt1_go"], 1)
                    v.wait_ge(S["sqrt1_done"], 2)
                    vchain(v, nc.vector.reciprocal(gn2[:, 4:5], std[:, 0:1]))
                    vchain(v, nc.vector.tensor_tensor(gn2[:, 4:5], gn2[:, 4:5], V(V_GNW), ALU.mult))
                    vchain(v, nc.vector.tensor_tensor(gn2[:, 5:6], tot[:, 0:1], gn2[:, 4:5], ALU.mult))
                    vchain(v, nc.vector.tensor_tensor(gn2[:, 5:6], V(V_GNB), gn2[:, 5:6], ALU.subtract))
                    vchain(v, nc.vector.memset(avg[:, :], 0.0))
                    vchain(v, nc.vector.tensor_reduce(avg[:, 1:W + 1], GR[:, 1:W + 1, :], AX.X, ALU.add))
                    tell(v, nc.vector.tensor_scalar(avg[:, 1:W + 1], avg[:, 1:W + 1], 1.0 / C, None, ALU.mult), S["lap_in"])
                    vchain(v, nc.vector.tensor_tensor(prod[:, 0, 0:W, :], GR[:, 1:W + 1, :], GR[:, 1:W + 1, :], ALU.mult))
                    tell(v, nc.vector.tensor_reduce(n2[:, 0, :], prod[:, 0, 0:W, :], AX.X, ALU.add), S["norm2_ready"])
                    vchain(v, nc.vector.tensor_tensor(prod[:, 0, 0:W + 1, :], GR[:, 0:W + 1, :], GR[:, 1:W + 2, :], ALU.mult))
                    vchain(v, nc.vector.tensor_reduce(ER[:, 0:W + 1], prod[:, 0, 0:W + 1, :], AX.X, ALU.add))
                    v.wait_ge(S["norm_done"], 1)
                    vchain(v, nc.vector.tensor_scalar(n2[:, 1, :], n2[:, 1, :], 1e-12, None, ALU.max))
                    vchain(v, nc.vector.reciprocal(rn[:, 1, 1:W + 1], n2[:, 1, :]))
                    tell(v, nc.vector.tensor_copy(rn[:, 1, 0:WP:W + 1], rn[:, 1, 2:W:W - 3]), S["rn_ready"])
                    v.wait_ge(S["gd_ready"], 1)
                    for j, (lo, hi, dx) in enumerate(((1, WP, -1), (1, W + 1, 0), (0, W + 1, 1))):
                        vchain(v, nc.vector.tensor_tensor(prod[:, j, lo:hi, :], GR[:, lo:hi, :], GD[:, lo + dx:hi + dx, :], ALU.mult))
                        tell(v, nc.vector.tensor_reduce(VD[:, j, lo:hi], prod[:, j, lo:hi, :], AX.X, ALU.add), S["vd_ready"], j + 1)
                    v.wait_ge(S["lap_done"], 1)
                    vchain(v, nc.vector.tensor_tensor(df[:, 0, :], PS[:, 6, 0:W], avg[:, 0:W], ALU.subtract))
                    vchain(v, nc.vector.tensor_tensor(df[:, 0, :], df[:, 0, :], avg[:, 2:W + 2], ALU.subtract))
                    vchain(v, nc.vector.tensor_scalar(df[:, 1, :], df[:, 0, :], -1.0, None, ALU.mult))
                    vchain(v, nc.vector.tensor_tensor(df[:, 0, :], df[:, 0, :], df[:, 1, :], ALU.max))
                    vchain(v, nc.vector.tensor_scalar(df[:, 1, :], df[:, 0, :], -1.0, None, ALU.mult))
                    tell(v, nc.vector.tensor_reduce(mm[:, :], df[:, :, :], AX.X, ALU.max), S["mm_ready"])
                    v.wait_ge(S["mmT_done"], 1)
                    tell(v, nc.vector.tensor_reduce(mmT[:, :], PS[0:2, 7, 0:P].rearrange("s (b y) -> s b y", b=B), AX.X, ALU.max), S["mmT_ready"])
                    v.wait_ge(S["mmB_done"], 1)
                    tell(v, nc.vector.tensor_copy(mmB[:, :], PS[0:B, 7, 0:2]), S["mmB_ready"])
                    v.wait_ge(S["rng_done"], 1)
                    vchain(v, nc.vector.tensor_copy(rng[:, 0:2], PS[:, 7, 0:2]))
                    vchain(v, nc.vector.tensor_tensor(rng[:, 2:3], rng[:, 0:1], rng[:, 1:2], ALU.add))
                    vchain(v, nc.vector.tensor_scalar(rng[:, 2:3], rng[:, 2:3], 1e-8, None, ALU.add))
                    vchain(v, nc.vector.reciprocal(rng[:, 3:4], rng[:, 2:3]))
                    vchain(v, nc.vector.tensor_scalar(kval[:, :], df[:, 0, :], rng[:, 1:2], rng[:, 3:4], ALU.add, ALU.mult))
                    vchain(v, nc.vector.tensor_scalar(kval[:, :], kval[:, :], 7.0, ROUND, ALU.mult, ALU.add))
                    vchain(v, nc.vector.tensor_scalar(kval[:, :], kval[:, :], ROUND - 1.0, 9.0, ALU.subtract, ALU.min))
                    v.wait_ge(S["rn_shift_done"], 1)
                    vchain(v, nc.vector.tensor_copy(rn[:, 0:3:2, :], PS[:, 6, 0:2 * WP].rearrange("p (s x) -> p s x", s=2)))
                    for dx in (-1, 0, 1):
                        lo, hi = 1 + dx, W + 1 + dx
                        vchain(v, nc.vector.tensor_tensor(sim[:, 7 + dx, :], VD[:, 1 + dx, 1:W + 1], rn[:, 2, lo:hi], ALU.mult))
                    vchain(v, nc.vector.tensor_tensor(sim[:, 3, :], ER[:, 0:W], rn[:, 1, 0:W], ALU.mult))
                    vchain(v, nc.vector.tensor_tensor(sim[:, 4, :], n2[:, 0, :], rn[:, 1, 1:W + 1], ALU.mult))
                    vchain(v, nc.vector.tensor_tensor(sim[:, 5, :], ER[:, 1:W + 1], rn[:, 1, 2:W + 2], ALU.mult))
                    v.wait_ge(S["dm_done"], 1)
                    for dx in (-1, 0, 1):
                        lo, hi = 1 + dx, W + 1 + dx
                        vchain(v, nc.vector.tensor_tensor(sim[:, 1 + dx, :], PS[:, 5, (1 + dx) * W:(2 + dx) * W], rn[:, 0, lo:hi], ALU.mult))
                    tell(v, nc.vector.tensor_tensor(sim[:, :, :], sim[:, :, :],
                                                      rn[:, 1, 1:W + 1].unsqueeze(1).to_broadcast([P, TAPS, W]), ALU.mult), S["sim_ready"])
                    for k in range(TAPS):
                        last = nc.vector.memset(rank[:, k, :], float(TAPS - 1 - k))
                    vchain(v, last)
                    for d in range(1, TAPS):
                        n = TAPS - d
                        vchain(v, nc.vector.tensor_tensor(cmp[:, 0:n, :], sim[:, 0:n, :], sim[:, d:TAPS, :], ALU.is_ge))
                        vchain(v, nc.vector.tensor_tensor(rank[:, d:TAPS, :], rank[:, d:TAPS, :], cmp[:, 0:n, :], ALU.add))
                        vchain(v, nc.vector.tensor_tensor(rank[:, 0:n, :], rank[:, 0:n, :], cmp[:, 0:n, :], ALU.subtract))
                    vchain(v, nc.vector.tensor_tensor(cmp[:, :, :], rank[:, :, :],
                                                      kval[:, :].unsqueeze(1).to_broadcast([P, TAPS, W]), ALU.is_lt))
                    v.wait_ge(S["exp_done"], 1)
                    vchain(v, nc.vector.tensor_tensor(wk[:, :, :], wk[:, :, :], cmp[:, :, :], ALU.mult))
                    vchain(v, nc.vector.tensor_reduce(wsum[:, 0, :], wk[:, :, :].rearrange("p k x -> p x k"), AX.X, ALU.add))
                    vchain(v, nc.vector.reciprocal(wsum[:, 1, :], wsum[:, 0, :]))
                    tell(v, nc.vector.tensor_tensor(wk[:, :, :], wk[:, :, :],
                                                      wsum[:, 1, :].unsqueeze(1).to_broadcast([P, TAPS, W]), ALU.mult), S["w_ready"])
                    for k in range(TAPS):
                        src = (GU, GR, GD)[k // 3]
                        if k >= NPROD:
                            v.wait_ge(S["prod_free"], k - NPROD + 1)
                        nc.vector.tensor_tensor(prod[:, k % NPROD, 0:W, :], src[:, k % 3:k % 3 + W, :],
                                                wk[:, k, :].unsqueeze(2).to_broadcast([P, W, C]),
                                                ALU.mult).then_inc(S["prod_ready"], 1)
                    v.wait_ge(S["agg_done"], 1)
                    vchain(v, nc.vector.transpose(enh[:, :].rearrange("p (y x) -> p x y", x=W),
                                                  banks(0, 4).rearrange("p (x c) -> p x c", c=C)))
                    vchain(v, nc.vector.scalar_tensor_tensor(enh[:, :], G[:, :], gn2[:, 4:5], enh[:, :], ALU.mult, ALU.add))
                    tell(v, nc.vector.tensor_scalar(enh[:, :], enh[:, :], gn2[:, 5:6], None, ALU.add), S["enh_ready"])
                    vchain(v, nc.vector.tensor_tensor(X[:, :], X[:, :], enh[:, :], ALU.add))
                    for n in range(4):
                        v.wait_ge(S["f_psum"], n + 1)
                        vchain(v, nc.vector.scalar_tensor_tensor(X[:, n * BANK:(n + 1) * BANK], PS[:, n, :], V(V_B2),
                                                                 X[:, n * BANK:(n + 1) * BANK], ALU.add, ALU.add))

                @block.scalar
                def _(act):
                    act.wait_ge(S["sqrt1_go"], 1)
                    nc.scalar.activation(std[:, 0:1], std[:, 0:1], ACT.Sqrt).then_inc(S["sqrt1_done"], 1)
                    act.wait_ge(S["sqrt1_go"], 2)
                    nc.scalar.activation(std[:, 0:1], std[:, 0:1], ACT.Sqrt).then_inc(S["sqrt1_done"], 1)
                    act.wait_ge(S["norm2_ready"], 1)
                    nc.scalar.activation(n2[:, 1, :], n2[:, 0, :], ACT.Sqrt).then_inc(S["norm_done"], 1)
                    for j, dst in enumerate((GD, GU)):
                        act.wait_ge(S["shift_done"], j + 1)
                        nc.scalar.activation(dst[:, :, :].rearrange("p x c -> p (x c)"), banks(0, 5)[:, 0:WP * C],
                                             ACT.Copy).then_inc(S["gd_ready"], 1)
                    act.wait_ge(S["sim_ready"], 1)
                    nc.scalar.activation(wk[:, :, :], sim[:, :, :], ACT.Exp).then_inc(S["exp_done"], 1)
                    for m in range(8):
                        act.wait_ge(S["h_psum"], m + 1)
                        nc.scalar.activation(hid[:, m % 2, (m // 2) * BANK:(m // 2 + 1) * BANK], PS[:, 4 + m % 4, :],
                                             ACT.Relu, bias=V(V_B1)).then_inc(S["h_ready"], 1)

                @block.tensor
                def _(pe):
                    pe.wait_ge(S["stats1"], 1)
                    nc.tensor.matmul(PS[:, 0, 0:2], M(M_OWN), S2[:, :], start=True, stop=True).then_inc(S["totals1"], 1)
                    pe.wait_ge(S["gn_stats"], 1)
                    nc.tensor.matmul(PS[:, 7, 0:2], M(M_PAIR), gn2[:, 0:2], start=True, stop=True).then_inc(S["gn_totals"], 1)
                    pe.wait_ge(S["gr_ready"], 1)
                    flat = GR[:, :, :].rearrange("p x c -> p (x c)")

                    def shift_rows(k):
                        for n in range(5):
                            hi = min((n + 1) * BANK, WP * C)
                            last = nc.tensor.matmul(PS[:, n, 0:hi - n * BANK], M(k), flat[:, n * BANK:hi], start=True, stop=True)
                        last.then_inc(S["shift_done"], 1)

                    shift_rows(M_DOWN)
                    pe.wait_ge(S["lap_in"], 1)
                    nc.tensor.matmul(PS[:, 6, 0:W], M(M_LAP), avg[:, 1:W + 1], start=True, stop=True).then_inc(S["lap_done"], 1)
                    pe.wait_ge(S["gd_ready"], 1)
                    shift_rows(M_UPR)
                    pe.wait_ge(S["vd_ready"], 3)
                    for dx in (-1, 0, 1):
                        o = PS[:, 5, (1 + dx) * W:(2 + dx) * W]
                        nc.tensor.matmul(o, M(M_UP), VD[:, 1 - dx, 1 + dx:1 + dx + W], start=True, stop=False)
                        last = nc.tensor.matmul(o, M(M_UP0), VD[:, 1 + dx, 1:W + 1], start=False, stop=True)
                    last.then_inc(S["dm_done"], 1)
                    pe.wait_ge(S["mm_ready"], 1)
                    nc.tensor.transpose(PS[0:2, 7, 0:P], mm[:, :], ident).then_inc(S["mmT_done"], 1)
                    pe.wait_ge(S["rn_ready"], 1)
                    nc.tensor.matmul(PS[:, 6, 0:WP], M(M_UPR), rn[:, 1, :], start=True, stop=True)
                    nc.tensor.matmul(PS[:, 6, WP:2 * WP], M(M_DOWN), rn[:, 1, :], start=True, stop=True).then_inc(S["rn_shift_done"], 1)
                    pe.wait_ge(S["mmT_ready"], 1)
                    nc.tensor.transpose(PS[0:2, 7, 0:2], mmT[:, :], M(M_IDENT, slice(0, 2), slice(0, 2))).then_inc(S["mmB_done"], 1)
                    pe.wait_ge(S["mmB_ready"], 1)
                    nc.tensor.matmul(PS[:, 7, 0:2], M(M_PICKB, slice(0, B)), mmB[:, :], start=True, stop=True).then_inc(S["rng_done"], 1)
                    pe.wait_ge(S["gd_ready"], 2)
                    for k in range(TAPS):
                        pe.wait_ge(S["prod_ready"], k + 1)
                        for n in range(4):
                            last = nc.tensor.matmul(PS[:, n, :], ident,
                                                    prod[:, k % NPROD, 0:W, :].rearrange("p x c -> p (x c)")[:, n * BANK:(n + 1) * BANK],
                                                    start=(k == 0), stop=(k == TAPS - 1))
                        last.then_inc(S["prod_free"] if k < TAPS - 1 else S["agg_done"], 1)
                    pe.wait_ge(S["enh_ready"], 1)

                    def ffn_out(m):
                        n, r = m // 2, m % 2
                        pe.wait_ge(S["h_ready"], m + 1)
                        last = nc.tensor.matmul(PS[64 * r:64 * r + 64, n, :], wt[:, W_TWO:W_TWO + 64],
                                                hid[:, r, n * BANK:(n + 1) * BANK], start=True, stop=True)
                        if r == 1:
                            last.then_inc(S["f_psum"], 1)

                    for m in range(8):
                        n, r = m // 2, m % 2
                        if m >= 4:
                            pe.wait_ge(S["h_ready"], m - 3)
                        nc.tensor.matmul(PS[:, 4 + m % 4, :], wt[:, W_ONE + P * r:W_ONE + P * r + P], enh[:, n * BANK:(n + 1) * BANK],
                                         start=True, stop=True).then_inc(S["h_psum"], 1)
                        if m:
                            ffn_out(m - 1)
                    ffn_out(7)

        XN = sb("XN", [P, B, L])
        UZ = sb("UZ", [P, 2 * L])
        u = UZ[:, 0:L]
        zy = UZ[:, L:2 * L]
        wx = sb("wx", [P, P])
        wdt = sb("wdt", [P, P])
        negA = sb("negA", [P, PAIRS])
        selb = sb("selb", [96, 2, PAIRS, P], BF16)

        with ExitStack() as stage:
            g = stage.enter_context(nc.sbuf_tensor("ln_g", [P, HALF], F32))
            sq = stage.enter_context(nc.sbuf_tensor("ln_sq", [P, HALF], F32))
            selw = stage.enter_context(nc.sbuf_tensor("selw", [96, 2 * PAIRS * P], F32))
            names = ("sel_in", "stats", "totals", "sqrt_go", "sqrt_done", "g_ready", "centered", "squared", "var_done",
                     "std_done", "xn_ready", "zeroed", "xn_in", "dt_psum", "expA_done", "w_done")
            S = {n: sem("s2_" + n) for n in names}
            with nc.Block() as block:
                @block.sync
                def _(sp):
                    sp.dma_start(selw[:, :], sel).then_inc(S["sel_in"], 16)
                    sp.wait_ge(S["zeroed"], 1)
                    sp.wait_ge(S["xn_ready"], 1)
                    for b in range(B):
                        for h in range(2):
                            q = 2 * b + h
                            for j in range(4):
                                first = h * HALF + 3 - j
                                n = min(HALF, L - first)
                                sp.dma_start(XN[32 * j:32 * j + 32, b, first:first + n],
                                             g[32 * q:32 * q + 32, 0:n]).then_inc(S["xn_in"], 16)
                    sp.wait_ge(S["xn_in"], 16 * 16)

                @block.tensor
                def _(pe):
                    nc.tensor.matmul(PS[0:DI, 4, 0:P], wt[0:2, W_DTA:W_DTA + DI], wt[0:2, W_DTB:W_DTB + P],
                                     start=True, stop=True).then_inc(S["dt_psum"], 1)
                    pe.wait_ge(S["stats"], 1)
                    nc.tensor.matmul(PS[:, 0, 0:2], M(M_OWN), S2[:, :], start=True, stop=True).then_inc(S["totals"], 1)
                    pe.wait_ge(S["g_ready"], 1)
                    for n in range(4):
                        last = nc.tensor.matmul(PS[:, n, :], M(M_CENTER), g[:, n * BANK:(n + 1) * BANK], start=True, stop=True)
                    last.then_inc(S["centered"], 1)
                    pe.wait_ge(S["squared"], 1)
                    pe.wait_ge(S["w_done"], 1)
                    for n in range(4):
                        last = nc.tensor.matmul(PS[:, 4 + n, :], M(M_MEAN), sq[:, n * BANK:(n + 1) * BANK], start=True, stop=True)
                    last.then_inc(S["var_done"], 1)

                @block.scalar
                def _(act):
                    nc.scalar.activation(negA[:, :], V(V_A, PAIRS), ACT.Exp).then_inc(S["expA_done"], 1)
                    act.wait_ge(S["sqrt_go"], 1)
                    nc.scalar.activation(std[:, 0:1], std[:, 0:1], ACT.Sqrt).then_inc(S["sqrt_done"], 1)
                    act.wait_ge(S["centered"], 1)
                    nc.scalar.activation(sq[:, :], banks(0, 4), ACT.Square).then_inc(S["squared"], 1)
                    act.wait_ge(S["var_done"], 1)
                    nc.scalar.activation(sq[:, :], banks(4, 4), ACT.Sqrt, bias=V(V_EPS)).then_inc(S["std_done"], 1)

                @block.vector
                def _(v):
                    gn_partition_stats(v).then_inc(S["stats"], 1)
                    v.wait_ge(S["totals"], 1)
                    vchain(v, nc.vector.tensor_copy(tot[:, 0:2], PS[:, 0, 0:2]))
                    variance(v, 1, GN_EPS).then_inc(S["sqrt_go"], 1)
                    v.wait_ge(S["sqrt_done"], 1)
                    vchain(v, nc.vector.reciprocal(rstd[:, 0:1], std[:, 0:1]))
                    vchain(v, nc.vector.scalar_tensor_tensor(nmrs[:, :], tot[:, 0:1], -1.0, rstd[:, 0:1], ALU.mult, ALU.mult))
                    tell(v, nc.vector.tensor_scalar(g[:, :], X[:, :], rstd[:, 0:1], nmrs[:, :], ALU.mult, ALU.add), S["g_ready"])
                    tell(v, nc.vector.memset(XN[0:96, :, 0:3], 0.0), S["zeroed"])
                    vchain(v, nc.vector.tensor_tensor(wx[:, :], wt[:, W_INX:W_INX + P], wt[:, W_CONV:W_CONV + P], ALU.mult))
                    v.wait_ge(S["expA_done"], 1)
                    vchain(v, nc.vector.tensor_scalar(negA[:, :], negA[:, :], -1.0, None, ALU.mult))
                    v.wait_ge(S["sel_in"], 16)
                    vchain(v, nc.vector.tensor_copy(selb[:, :, :, :].rearrange("p a b c -> p (a b c)"), selw[:, :]))
                    v.wait_ge(S["dt_psum"], 1)
                    vchain(v, nc.vector.memset(wdt[DI:P, :], 0.0))
                    tell(v, nc.vector.tensor_copy(wdt[0:DI, :], PS[0:DI, 4, 0:P]), S["w_done"])
                    v.wait_ge(S["std_done"], 1)
                    vchain(v, nc.vector.reciprocal(sq[:, :], sq[:, :]))
                    vchain(v, nc.vector.tensor_tensor(g[:, :], banks(0, 4), sq[:, :], ALU.mult))
                    tell(v, nc.vector.tensor_scalar(g[:, :], g[:, :], V(V_LNW), V(V_LNB), ALU.mult, ALU.add), S["xn_ready"])


        scratch = sb("scratch", [P, 9 * CHUNK])

        def chunk_buffer(k, n=1):
            return scratch[:, k * CHUNK:(k + n) * CHUNK]

        dl = XN[:, 0, :]
        du = chunk_buffer(0)
        gate_tmp = chunk_buffer(1)
        resid = chunk_buffer(2)
        hs = chunk_buffer(3)
        dA = chunk_buffer(4, 2).rearrange("p (s n) -> p s n", s=2)
        dBC = chunk_buffer(6, 2).rearrange("p (s n) -> p s n", s=2)
        log_tmp = chunk_buffer(4, 4)
        parts = sb("parts", [96, L], BF16)
        prime = sb("prime", [P, 16])
        carry = sb("carry", [P, PAIRS])

        pr = {n: sem("proj_" + n) for n in ("xc_psum", "z_psum", "u_done", "z_done", "dt_psum", "v_ready", "bc_psum",
                                            "hi_done", "r_read", "abs_done", "exp_done", "log_done", "parts_ready", "delta_ready")}
        sc = {n: sem("scan_" + n) for n in ("b_psum", "c_psum", "b_used", "exp_done", "h_done", "hc_done", "y_done", "y_used", "zy_done",
                                            "dbu_done", "du_done",
                                            "o_psum")}
        l3 = {n: sem("l3_" + n) for n in (
            "stats", "totals", "sqrt_go", "sqrt_done", "g_ready", "corner_ready", "shift_done", "below_ready", "table_in",
            "zeroed", "g3_in", "g3_ready", "off_psum", "mask_in", "mask_exp", "base_in", "resid_in", "prepared",
            "idx_ready", "prod_done", "rows_done", "sum_done", "t_psum", "t_read", "o_psum", "o_read", "out_dma")}
        gathered = [sem(f"gathered{k}") for k in range(SLOTS)]

        GLEN = (H + 2) * W
        G3s = [sb("G3", [96, GLEN])[:, :], UZ[0:96, 0:GLEN]]
        tabs = [t.rearrange("p (x k c) -> p x k c", k=4, c=C)
                for t in (chunk_buffer(0, 8), XN[:, :, :].rearrange("p b n -> p (b n)"))]
        temps = [UZ, scratch]
        tables = [nc.dram_tensor(f"corner_table_{b}", (L, 4 * C), F32, kind="Internal").ap() for b in range(B)]
        idx_all = sb("idx_all", [P, (B * GROUPS + SLOTS) * TAPS], U32)
        idx_slot = sb("idx_slot", [P, SLOTS, TAPS], U32)
        coef = sb("coef", [P, B * GROUPS, TAPS, 4])
        got = sb("got", [P, SLOTS, TAPS, 4, C])
        Bs, dBu = (got[:, :, :, :, :].rearrange("p s t k c -> p (s t k c)")[:, 2 * k * CHUNK:2 * (k + 1) * CHUNK].rearrange(
            "p (s n) -> p s n", s=2) for k in range(2))
        prodg = sb("prodg", [P, TAPS, 4, C])
        colg = sb("colg", [P, 4 * P])
        colT = sb("colT", [P, 4 * P])


        def group_gather(pool, b, G, slot, index):
            pool.wait_ge(l3["prod_done"], G + 1)
            pool.nop(nofuse=True)
            for tap in range(TAPS):
                pool.indirect_dma_start(got[:, slot, tap, :, :].rearrange("p k c -> p (k c)"), None, tables[b],
                                        bass.IndirectOffsetOnAxis(ap=index[:, tap:tap + 1], axis=0)
                                        ).then_inc(gathered[slot], 16)

        def group_weigh(v, G, slot, uses):
            v.wait_ge(gathered[slot], uses * (16 * TAPS) + 16 * TAPS)
            v.nop(nofuse=True)
            nc.vector.tensor_copy(idx_slot[:, slot, :], idx_all[:, bass.ds((G + SLOTS) * TAPS, TAPS)])
            if not isinstance(G, int) or G:
                v.wait_ge(l3["sum_done"], G)
            tell(v, nc.vector.tensor_tensor(prodg[:, :, :, :].rearrange("p t k c -> p (t k) c"),
                                            got[:, slot, :, :, :].rearrange("p t k c -> p (t k) c"),
                                            coef[:, bass.ds(G, 1), :, :].rearrange("p o t k -> p (o t k)").unsqueeze(2).to_broadcast([P, TAPS * 4, C]),
                                            ALU.mult), l3["prod_done"], G + (SLOTS + 1))
            tell(v, nc.vector.tensor_tensor(prodg[:, 6:9, 0:2, :], prodg[:, 6:9, 0:2, :], prodg[:, 6:9, 2:4, :], ALU.add),
                 l3["rows_done"], G + 1)
            v.wait_ge(l3["t_psum"], G + 1)
            nc.vector.tensor_tensor(colg[:, 0:3 * P].rearrange("p (t k c) -> p t (k c)", k=2, c=C),
                                    prodg[:, 0:6, 0:2, :].rearrange("p t k c -> p t (k c)"),
                                    prodg[:, 0:6, 2:4, :].rearrange("p t k c -> p t (k c)"), ALU.add)
            nc.vector.tensor_tensor(colg[:, 3 * P:3 * P + 3 * C].rearrange("p (t c) -> p t c", c=C),
                                    prodg[:, 6:9, 0, :], prodg[:, 6:9, 1, :], ALU.add).then_inc(l3["sum_done"], 1)

        def group_transpose(pe, G):
            pe.wait_ge(l3["sum_done"], G + 1)
            pe.wait_ge(l3["t_read"], G + 1)
            for r in range(4):
                last = nc.tensor.transpose(PS[:, 6, r * P:r * P + P], colg[:, r * P:r * P + P], ident)
            last.then_inc(l3["t_psum"], 1)

        def group_copy(act, G):
            act.wait_ge(l3["t_psum"], G + 2)
            act.wait_ge(l3["o_psum"], G + 1)
            nc.scalar.activation(colT[:, :], PS[:, 6, :], ACT.Copy).then_inc(l3["t_read"], 1)

        def group_multiply(pe, G):
            pe.wait_ge(l3["t_read"], G + 2)
            pe.wait_ge(l3["o_read"], G + 1)
            for r in range(4):
                last = nc.tensor.matmul(PS[0:C, 7, 0:P], wt[:, W_L3 + C * r:W_L3 + C * r + C], colT[:, r * P:r * P + P],
                                        start=(r == 0), stop=(r == 3))
            last.then_inc(l3["o_psum"], 1)

        def group_add(v, b, G, g):
            xr = G3s[b][0:C, 0:L]
            v.wait_ge(l3["o_psum"], G + 2)
            px = xr.rearrange("c (q n) -> c q n", q=4)[:, :, bass.ds(g * 32, 32)]
            nc.vector.tensor_tensor(px, px, PS[0:C, 7, 0:P].rearrange("c (q n) -> c q n", q=4), ALU.add).then_inc(l3["o_read"], 1)

        def tensor_turn(pe, G):
            if not isinstance(G, int) or 2 <= G:
                group_multiply(pe, G - 2)
            if not isinstance(G, int) or 1 <= G < B * GROUPS + 1:
                group_transpose(pe, G - 1)

        def scalar_turn(act, G):
            if not isinstance(G, int) or 1 <= G < B * GROUPS + 1:
                group_copy(act, G - 1)

        def vector_turn(v, G):
            if G >= 2:
                b = (G - 2) // GROUPS
                if (G - 2) % GROUPS == 0:
                    v.wait_ge(l3["resid_in"], 32 * (b + 1))
                group_add(v, b, G - 2, G - 2 - b * GROUPS)
            if G < B * GROUPS:
                group_weigh(v, G, G % SLOTS, G // SLOTS)

        def nothing(k):
            pass


        def project_tensor(pe, b, between=nothing):
            if b == 1:
                pe.wait_ge(l3["below_ready"], 1)
                pe.wait_ge(l3["mask_in"], 1)

            def tokens(n):
                cols = slice(n * BANK, (n + 1) * BANK)
                if n >= 2:
                    pe.wait_ge(pr["z_done"], 8 * b + n - 1)
                nc.tensor.matmul(PS[:, n % 2, :], wx[:, :], XN[:, b, cols], start=True, stop=True).then_inc(pr["xc_psum"], 1)
                nc.tensor.matmul(PS[:, 2 + n % 2, :], wt[:, W_INZ:W_INZ + P], XN[:, b, cols],
                                 start=True, stop=True).then_inc(pr["z_psum"], 1)

            def delta(c):
                pe.wait_ge(pr["u_done"], 8 * b + 2 * c + 2)
                if c:
                    pe.wait_ge(pr["v_ready"], 4 * b + c)
                for n in range(2):
                    last = nc.tensor.matmul(PS[:, 4 + n, :], wdt[:, :], u[:, (2 * c + n) * BANK:(2 * c + n + 1) * BANK],
                                            start=True, stop=True)
                last.then_inc(pr["dt_psum"], 1)

            def b_and_c(c):
                if c == 0:
                    pe.wait_ge(pr["z_done"], 8 * b + 8)
                if c >= 2:
                    pe.wait_ge(pr["r_read"], 4 * b + c - 1)
                for n in range(2):
                    last = nc.tensor.matmul(PS[0:96, 2 * (c % 2) + n, :], wt[:, W_BC:W_BC + 96],
                                            u[:, (2 * c + n) * BANK:(2 * c + n + 1) * BANK], start=True, stop=True)
                last.then_inc(pr["bc_psum"], 1)

            for n in range(4):
                tokens(n)
            delta(0)
            between(0)
            tokens(4), tokens(5), delta(1), tokens(6), tokens(7), delta(2), delta(3)
            between(1)
            b_and_c(0), b_and_c(1)
            between(2)
            b_and_c(2), b_and_c(3)
            between(3)

        def project_scalar(act, b, between=nothing):
            if b == 1:
                act.wait_ge(l3["prepared"], 1)

            def gated(n):
                k = 8 * b + n
                cols = slice(n * BANK, (n + 1) * BANK)
                act.wait_ge(pr["xc_psum"], k + 1)
                nc.scalar.activation(u[:, cols], PS[:, n % 2, :], ACT.Silu, bias=V(V_CB)).then_inc(pr["u_done"], 1)
                act.wait_ge(pr["z_psum"], k + 1)
                nc.scalar.activation(zy[:, cols], PS[:, 2 + n % 2, :], ACT.Silu).then_inc(pr["z_done"], 1)

            def high(c):
                act.wait_ge(pr["bc_psum"], 4 * b + c + 1)
                nc.scalar.activation(parts[:, c * CHUNK:(c + 1) * CHUNK], banks(2 * (c % 2), 2, slice(0, 96)),
                                     ACT.Copy).then_inc(pr["hi_done"], 1)

            def magnitude(c):
                act.wait_ge(pr["v_ready"], 4 * b + c + 1)
                cols = slice(c * CHUNK, (c + 1) * CHUNK)
                nc.scalar.activation(log_tmp[:, cols], dl[:, cols], ACT.Abs).then_inc(pr["abs_done"], 1)

            for n in range(4):
                gated(n)
            between(0)
            for n in range(4, 8):
                gated(n)
            if b == 1:
                act.wait_ge(l3["table_in"], 16)
            for c in range(4):
                magnitude(c)
            between(1)
            high(0), high(1)
            between(2)
            act.wait_ge(pr["abs_done"], 4 * b + 4)
            nc.scalar.activation(log_tmp, log_tmp, ACT.Exp, scale=-1.0).then_inc(pr["exp_done"], 1)
            high(2), high(3)
            act.wait_ge(pr["exp_done"], b + 1)
            nc.scalar.activation(log_tmp, log_tmp, ACT.Ln, bias=1.0).then_inc(pr["log_done"], 1)
            between(3)

        def project_vector(v, b, between=nothing):
            def preactivation(c):
                v.wait_ge(pr["dt_psum"], 4 * b + c + 1)
                nc.vector.tensor_scalar(dl[:, c * CHUNK:(c + 1) * CHUNK], banks(4, 2), V(V_BDT), None,
                                        ALU.add).then_inc(pr["v_ready"], 1)

            def split(c):
                cols = slice(c * CHUNK, (c + 1) * CHUNK)
                v.wait_ge(pr["hi_done"], 4 * b + c + 1)
                tell(v, nc.vector.tensor_tensor(resid[0:DI, :], banks(2 * (c % 2), 2, slice(0, DI)), parts[0:DI, cols],
                                                ALU.subtract), pr["r_read"], 4 * b + c + 1)
                vchain(v, nc.vector.tensor_copy(parts[0:DI, cols], resid[0:DI, :]))
                tell(v, nc.vector.tensor_tensor(parts[0:32, cols], resid[0:32, :], parts[0:32, cols], ALU.subtract),
                     pr["parts_ready"], 4 * b + c + 1)

            preactivation(0)
            between(0)
            for c in range(1, 4):
                preactivation(c)
            between(1)
            if b == 1:
                v.wait_ge(l3["table_in"], 16)
            split(0), split(1)
            between(2)
            split(2), split(3)
            between(3)
            v.wait_ge(pr["v_ready"], 4 * b + 4)
            v.wait_ge(pr["log_done"], b + 1)
            tell(v, nc.vector.scalar_tensor_tensor(dl, dl, 0.0, log_tmp, ALU.max, ALU.add), pr["delta_ready"], b + 1)


        def scan_tensor(pe, i, c, between=nothing):
            tok = lambda n: bass.ds(i * CHUNK + n * BANK, BANK)

            def add_states(j):
                s = c * PAIRS + j
                pe.wait_ge(sc["hc_done"], s + 2)
                if j == 0:
                    pe.wait_ge(sc["y_used"], c + 2)
                for n in range(2):
                    last = nc.tensor.matmul(PS[:, 4 + n, :], wt[:, W_SUM:W_SUM + P], dBC[:, j % 2, n * BANK:(n + 1) * BANK],
                                            start=(j == 0), stop=(j == PAIRS - 1))
                last.then_inc(sc["y_done"], 1)

            for j in range(PAIRS):
                s = c * PAIRS + j
                pe.wait_ge(sc["b_used"], s + 1)
                for n in range(2):
                    last = nc.tensor.matmul(PS[:, n, :], selb[:, 0, j, :], parts[:, tok(n)], start=True, stop=True)
                last.then_inc(sc["b_psum"], 1)
                pe.wait_ge(sc["hc_done"], s + 1)
                for n in range(2):
                    last = nc.tensor.matmul(PS[:, 2 + n, :], selb[:, 1, j, :], parts[:, tok(n)], start=True, stop=True)
                last.then_inc(sc["c_psum"], 1)
                if j:
                    add_states(j - 1)
                if j in TURN_AFTER:
                    between(TURN_AFTER.index(j))
            add_states(PAIRS - 1)

        def scan_scalar(act, i, c, between=nothing):
            for j in range(PAIRS):
                s = c * PAIRS + j
                act.wait_ge(sc["h_done"], s + 1)
                act.nop(nofuse=True)
                nc.scalar.activation(dA[:, j % 2, :], dl[:, bass.ds(i * CHUNK, CHUNK)], ACT.Exp,
                                     scale=negA[:, j:j + 1]).then_inc(sc["exp_done"], 1)
                if j in TURN_AFTER:
                    between(TURN_AFTER.index(j))

        def scan_vector(v, i, c, between=nothing):
            tok = bass.ds(i * CHUNK, CHUNK)
            vchain(v, nc.vector.tensor_tensor(du, dl[:, tok], u[:, tok], ALU.mult))
            for j in range(PAIRS):
                s = c * PAIRS + j
                slot = dBC[:, j % 2, :]
                v.wait_ge(sc["b_psum"], s + 1)
                v.wait_ge(sc["y_done"], s + 1)
                tell(v, nc.vector.tensor_tensor(slot, du, banks(0, 2), ALU.mult), sc["b_used"], s + 2)
                v.wait_ge(sc["exp_done"], s + 1)
                v.wait_ge(sc["hc_done"], s + 1)
                tell(v, nc.vector.tensor_tensor_scan(hs, dA[:, j % 2, :], slot, carry[:, j:j + 1], ALU.mult, ALU.add),
                     sc["h_done"], s + 3)
                nc.vector.tensor_copy(carry[:, j:j + 1], hs[:, CHUNK - 1:CHUNK])
                v.wait_ge(sc["c_psum"], s + 1)
                nc.vector.tensor_tensor(slot, hs, banks(2, 2), ALU.mult).then_inc(sc["hc_done"], 1)
                if j in TURN_AFTER:
                    between(TURN_AFTER.index(j))
            v.wait_ge(sc["y_done"], c * PAIRS + PAIRS + 2)
            tell(v, nc.vector.scalar_tensor_tensor(gate_tmp, u[:, tok], V(V_D), banks(4, 2), ALU.mult, ALU.add),
                 sc["y_used"], c + 3)
            tell(v, nc.vector.tensor_tensor(zy[:, tok], gate_tmp, zy[:, tok], ALU.mult), sc["zy_done"], c + 2)


        def helped_broadcast(pe, c, j, which):
            c, j = c + j // PAIRS, j % PAIRS
            s = c * PAIRS + j
            first = 0 if which == 0 else (2, 6)[j % 2]
            if which == 0:
                pe.wait_ge(sc["b_used"], s + 1)
            elif not isinstance(s, int) or s:
                pe.wait_ge(sc["hc_done"], s)
            for n in range(2):
                last = nc.tensor.matmul(PS[:, first + n, :], selb[:, which, j, :],
                                        parts[:, bass.ds(c * CHUNK + n * BANK, BANK)], start=True, stop=True)
            last.then_inc(sc["c_psum" if which else "b_psum"], 1)

        def helped_tensor(pe, c, ends=False):
            for j in range(PAIRS):
                if not ends or j + 2 < PAIRS:
                    helped_broadcast(pe, c, j + 2, 0)
                if not ends or j + 1 < PAIRS:
                    helped_broadcast(pe, c, j + 1, 1)
                pe.wait_ge(sc["hc_done"], c * PAIRS + (j + 2))
                if j == 0:
                    pe.wait_ge(sc["y_used"], c + 2)
                for n in range(2):
                    last = nc.tensor.matmul(PS[:, 4 + n, :], wt[:, W_SUM:W_SUM + P], dBC[:, j % 2, n * BANK:(n + 1) * BANK],
                                            start=(j == 0), stop=(j == PAIRS - 1))
                last.then_inc(sc["y_done"], 1)

        def helped_scalar(act, c):
            for j in range(PAIRS):
                s = c * PAIRS + j
                act.wait_ge(sc["dbu_done"], s + 1)
                act.wait_ge(sc["b_psum"], s + 1)
                nc.scalar.activation(Bs[:, j % 2, :], banks(0, 2), ACT.Copy).then_inc(sc["b_used"], 1)
                act.wait_ge(sc["h_done"], s + 1)
                act.nop(nofuse=True)
                nc.scalar.activation(dA[:, j % 2, :], dl[:, bass.ds(c * CHUNK, CHUNK)], ACT.Exp,
                                     scale=negA[:, j:j + 1]).then_inc(sc["exp_done"], 1)

        def helped_gate(pool, c):
            pool.wait_ge(sc["y_used"], c + 3)
            pool.nop(nofuse=True)
            tok = bass.ds(c * CHUNK, CHUNK)
            nc.gpsimd.tensor_tensor(zy[:, tok], gate_tmp, zy[:, tok], ALU.mult).then_inc(sc["zy_done"], 1)

        def helped_gpsimd(pool, c, between=nothing):
            pool.wait_ge(sc["du_done"], c + 1)
            for j in range(PAIRS):
                s = c * PAIRS + j
                pool.wait_ge(sc["b_used"], s + 2)
                pool.wait_ge(sc["h_done"], s + 1)
                nc.gpsimd.tensor_tensor(dBu[:, j % 2, :], du, Bs[:, j % 2, :], ALU.mult).then_inc(sc["dbu_done"], 1)
                between(j)

        def helped_du(v, c):
            nc.vector.tensor_tensor(du, dl[:, bass.ds(c * CHUNK, CHUNK)], u[:, bass.ds(c * CHUNK, CHUNK)],
                                    ALU.mult).then_inc(sc["du_done"], 1)

        def helped_vector(v, c, ends=False):
            for j in range(PAIRS):
                s = c * PAIRS + j
                v.wait_ge(sc["dbu_done"], s + 3)
                v.wait_ge(sc["exp_done"], s + 1)
                v.wait_ge(sc["hc_done"], s + 1)
                tell(v, nc.vector.tensor_tensor_scan(hs, dA[:, j % 2, :], dBu[:, j % 2, :], carry[:, j:j + 1], ALU.mult, ALU.add),
                     sc["h_done"], s + 3)
                nc.vector.tensor_copy(carry[:, j:j + 1], hs[:, CHUNK - 1:CHUNK])
                v.wait_ge(sc["c_psum"], s + 1)
                v.wait_ge(sc["y_done"], s + 1)
                nc.vector.tensor_tensor(dBC[:, j % 2, :], hs, banks((2, 6)[j % 2], 2), ALU.mult).then_inc(sc["hc_done"], 1)
            if not ends:
                helped_du(v, c + 1)
            v.wait_ge(sc["y_done"], c * PAIRS + (PAIRS + 2))
            v.wait_ge(sc["zy_done"], c + 1)
            tell(v, nc.vector.scalar_tensor_tensor(gate_tmp, u[:, bass.ds(c * CHUNK, CHUNK)], V(V_D), banks(4, 2),
                                                   ALU.mult, ALU.add), sc["y_used"], c + 3)


        def output_tensor(pe, b):
            pe.wait_ge(sc["zy_done"], NCHUNK * (b + 1) + 1)
            for n in range(4):
                for h in range(2):
                    q = 2 * b + h
                    last = nc.tensor.matmul(PS[32 * q:32 * q + 32, n, :], wt[:, W_OUT:W_OUT + C],
                                            zy[:, h * HALF + n * BANK:h * HALF + (n + 1) * BANK], start=True, stop=True)
            last.then_inc(sc["o_psum"], 1)

        def output_vector(v, b):
            rows = slice(64 * b, 64 * b + 64)
            v.wait_ge(sc["o_psum"], b + 1)
            vchain(v, nc.vector.tensor_tensor(X[rows, :], X[rows, :], banks(0, 4, rows), ALU.add))


        def prepare(b):
            rows = slice(64 * b, 64 * b + 64)
            n = GROUPS * TAPS
            G3, tab = G3s[b], tabs[b]

            def temp(first, count):
                return temps[b][:, first:first + count]

            g4 = temp(0, HALF)
            bases, yx, corner0 = (temp(HALF + 2 * n * k, 2 * n).rearrange("p (g k) -> p g k", k=2 * TAPS) for k in range(3))
            hat = temp(HALF + 6 * n, 4 * n).rearrange("p (r g k) -> p r g k", r=2, k=2 * TAPS)
            msk = temp(HALF + 10 * n, n).rearrange("p (g k) -> p g k", k=TAPS)
            om = temp(HALF + 13 * n, 32 * GROUPS).rearrange("p (g k) -> p g k", k=32)
            cm = temp(HALF + 11 * n, 2 * n).rearrange("p (r g k) -> p r g k", r=2, k=TAPS)

            def sync(sp):
                sp.wait_ge(l3["zeroed"], b + 1)
                sp.dma_start(bases.rearrange("p g k -> p (g k)"), base).then_inc(l3["base_in"], 16)
                sp.wait_ge(l3["g_ready"], b + 1)
                for h in range(2):
                    for j in range(3):
                        first = W + h * HALF - (j - 1)
                        sp.dma_start(G3[32 * j:32 * j + 32, first:first + HALF],
                                     g4[64 * b + 32 * h:64 * b + 32 * h + 32, :]).then_inc(l3["g3_in"], 16)
                sp.wait_ge(l3["corner_ready"], b + 1)
                sp.wait_ge(l3["below_ready"], b + 1)
                sp.dma_start(tables[b].rearrange("(y x) n -> y (x n)", y=H),
                             tab[rows, :, :, :].rearrange("p x k c -> p (x k c)")).then_inc(l3["table_in"], 16)
                sp.wait_ge(l3["off_psum"], b + 1)
                for h in range(2):
                    q = 2 * b + h
                    sp.dma_start(G3[0:C, h * HALF:(h + 1) * HALF], X[32 * q:32 * q + 32, :]).then_inc(l3["resid_in"], 16)
                sp.wait_ge(l3["table_in"], 16 * (b + 1))

            def tensor(pe, between=nothing):
                pe.wait_ge(l3["stats"], b + 1)
                nc.tensor.matmul(PS[rows, 0, 0:2], M(M_OWN, rows, rows), S2[rows, :], start=True, stop=True).then_inc(l3["totals"], 1)
                pe.wait_ge(l3["corner_ready"], b + 1)
                for n in range(4):
                    last = nc.tensor.matmul(PS[rows, n, :], M(M_DOWN, cols=rows), tab[:, 16 * n:16 * n + 16, 0, :],
                                            start=True, stop=True)
                last.then_inc(l3["shift_done"], 1)
                between(0)
                pe.wait_ge(l3["g3_ready"], b + 1)
                for n in range(2):
                    for q in range(4):
                        for dy in range(3):
                            first = q * QUARTER + n * BANK + dy * W
                            last = nc.tensor.matmul(PS[32 * q:32 * q + 32, 4 + n, :], wt[0:96, W_OFF + 32 * dy:W_OFF + 32 * dy + 32],
                                                    G3[:, first:first + BANK], start=(dy == 0), stop=(dy == 2))
                last.then_inc(l3["off_psum"], 1)
                between(1)
                between(2)

            def scalar(act, between=nothing):
                act.wait_ge(l3["sqrt_go"], b + 1)
                nc.scalar.activation(std[rows, 0:1], std[rows, 0:1], ACT.Sqrt).then_inc(l3["sqrt_done"], 1)
                act.wait_ge(l3["shift_done"], b + 1)
                below = banks(0, 4, rows).rearrange("p (x c) -> p x c", c=C)
                nc.scalar.activation(tab[rows, :, 2, :], below, ACT.Copy)
                nc.scalar.activation(tab[rows, 0:W - 1, 3, :], below[:, 1:W, :], ACT.Copy).then_inc(l3["below_ready"], 1)
                between(0)
                between(1)
                act.wait_ge(l3["mask_in"], b + 1)
                nc.scalar.activation(msk, msk, ACT.Exp, scale=-1.0).then_inc(l3["mask_exp"], 1)
                between(2)

            def vector(v, between=nothing):
                vchain(v, nc.vector.memset(G3[:, 0:W], 0.0))
                tell(v, nc.vector.memset(G3[:, GLEN - W:GLEN], 0.0), l3["zeroed"], b + 1)
                gn_partition_stats(v, rows).then_inc(l3["stats"], 1)
                v.wait_ge(l3["totals"], b + 1)
                vchain(v, nc.vector.tensor_copy(tot[rows, 0:2], PS[rows, 0, 0:2]))
                variance(v, 1, GN_EPS, rows).then_inc(l3["sqrt_go"], 1)
                v.wait_ge(l3["sqrt_done"], b + 1)
                vchain(v, nc.vector.reciprocal(rstd[rows, 0:1], std[rows, 0:1]))
                vchain(v, nc.vector.scalar_tensor_tensor(nmrs[rows, :], tot[rows, 0:1], -1.0, rstd[rows, 0:1], ALU.mult, ALU.mult))
                tell(v, nc.vector.tensor_scalar(g4[rows, :], X[rows, :], rstd[rows, 0:1], nmrs[rows, :], ALU.mult, ALU.add),
                     l3["g_ready"], b + 1)
                vchain(v, nc.vector.memset(tab[rows, W - 1, 1::2, :], 0.0))
                vchain(v, nc.vector.memset(tab[64 - 64 * b:P - 64 * b, :, 0, :], 0.0))
                vchain(v, nc.vector.transpose(tab[rows, :, 0, :], g4[rows, :].rearrange("p (y x) -> p x y", x=W)))
                tell(v, nc.vector.tensor_copy(tab[rows, 0:W - 1, 1, :], tab[rows, 1:W, 0, :]), l3["corner_ready"], b + 1)
                between(0)
                cols = G3.rearrange("p (y x) -> p y x", x=W)
                v.wait_ge(l3["g3_in"], 96 * (b + 1))
                vchain(v, nc.vector.memset(cols[0:32, :, 0], 0.0))
                tell(v, nc.vector.memset(cols[64:96, :, W - 1], 0.0), l3["g3_ready"], b + 1)
                v.wait_ge(l3["base_in"], 16 * (b + 1))
                v.wait_ge(l3["off_psum"], b + 1)
                vchain(v, nc.vector.transpose(om.rearrange("p g k -> p (g k)"), banks(4, 2)))
                vchain(v, nc.vector.tensor_tensor(yx, om[:, :, 0:18], bases, ALU.add))
                tell(v, nc.vector.tensor_copy(msk, om[:, :, 18:27]), l3["mask_in"], b + 1)
                between(1)
                vchain(v, nc.vector.tensor_scalar(corner0, yx, 0.5, 0.0, ALU.subtract, ALU.max))
                vchain(v, nc.vector.tensor_scalar(corner0, corner0, float(H - 2), ROUND, ALU.min, ALU.add))
                vchain(v, nc.vector.tensor_scalar(corner0, corner0, ROUND, None, ALU.subtract))
                gs = slice(b * GROUPS, (b + 1) * GROUPS)
                vchain(v, nc.vector.scalar_tensor_tensor(
                    idx_all[:, b * n:(b + 1) * n].rearrange("p (g k) -> p g k", k=TAPS),
                    corner0[:, :, 0::2], float(W), corner0[:, :, 1::2], ALU.mult, ALU.add))
                nc.vector.memset(prime[:, 12 + b:13 + b], 0.0).then_inc(l3["idx_ready"], 1)
                vchain(v, nc.vector.tensor_tensor(hat[:, 0, :, :], yx, corner0, ALU.subtract))
                vchain(v, nc.vector.tensor_scalar(hat[:, 1, :, :], hat[:, 0, :, :], 1.0, None, ALU.subtract))
                flat = hat.rearrange("p r g k -> p (r g k)")
                vchain(v, nc.vector.scalar_tensor_tensor(flat, flat, -1.0, flat, ALU.mult, ALU.min))
                vchain(v, nc.vector.tensor_scalar(flat, flat, 1.0, 0.0, ALU.add, ALU.max))
                v.wait_ge(l3["mask_exp"], b + 1)
                vchain(v, nc.vector.tensor_scalar(msk, msk, 1.0, None, ALU.add))
                vchain(v, nc.vector.reciprocal(msk, msk))
                for r in range(2):
                    vchain(v, nc.vector.tensor_tensor(cm[:, r, :, :], hat[:, r, :, 0::2], msk, ALU.mult))
                    for s in range(2):
                        vchain(v, nc.vector.tensor_tensor(coef[:, gs, :, 2 * r + s], cm[:, r, :, :], hat[:, s, :, 1::2], ALU.mult))
                nc.vector.memset(prime[:, 14 + b:15 + b], 0.0).then_inc(l3["prepared"], 1)
                between(2)

            return sync, tensor, scalar, vector

        prep = [prepare(b) for b in range(B)]
        IN_SCAN, IN_PREPARE, REST = 4, 28, 34
        TURNS = 6
        TURN_AFTER = (0, 1, 3, 4, 5, 7)
        assert TURNS == SLOTS and IN_PREPARE == IN_SCAN + NCHUNK * TURNS

        with nc.Block() as block:
            @block.sync
            def _(sp):
                for b in range(B):
                    prep[b][0](sp)
                for b in range(B):
                    sp.wait_ge(l3["o_read"], GROUPS * (b + 1) + 1)
                    sp.dma_start(out[b].rearrange("c y x -> c (y x)"), G3s[b][0:C, 0:L]).then_inc(l3["out_dma"], 16)
                sp.wait_ge(l3["out_dma"], 16 * B)

            @block.gpsimd
            def _(pool):
                pool.wait_ge(pr["delta_ready"], 1)
                helped_gpsimd(pool, 0)
                with nc.gpsimd.Fori(0, NCHUNK - 1) as i:
                    helped_gpsimd(pool, i + 1, lambda j: helped_gate(pool, i) if j == 2 else None)
                helped_gate(pool, NCHUNK - 1)
                for b in range(B):
                    first = b * GROUPS
                    pool.wait_ge(l3["table_in"], 16 * (b + 1))
                    pool.wait_ge(l3["idx_ready"], b + 1)
                    for G in range(first, first + SLOTS):
                        group_gather(pool, b, G, G % SLOTS, idx_all[:, G * TAPS:(G + 1) * TAPS])
                    turns = GROUPS // SLOTS - 1
                    with nc.gpsimd.Fori(0, turns) as i:
                        for k in range(SLOTS):
                            slot = (first + k) % SLOTS
                            group_gather(pool, b, i * SLOTS + (first + SLOTS + k), slot, idx_slot[:, slot, :])
                    for G in range(first + SLOTS * (turns + 1), first + GROUPS):
                        group_gather(pool, b, G, G % SLOTS, idx_slot[:, G % SLOTS, :])

            @block.tensor
            def _(pe):
                project_tensor(pe, 0)
                pe.wait_ge(pr["delta_ready"], 1)
                for j, which in ((0, 0), (1, 0), (0, 1)):
                    helped_broadcast(pe, 0, j, which)
                with nc.tensor.Fori(0, NCHUNK - 1) as i:
                    helped_tensor(pe, i)
                helped_tensor(pe, NCHUNK - 1, ends=True)
                output_tensor(pe, 0)
                prep[0][1](pe)
                project_tensor(pe, 1, lambda k: tensor_turn(pe, k))
                pe.wait_ge(pr["delta_ready"], 2)
                with nc.tensor.Fori(0, NCHUNK) as i:
                    scan_tensor(pe, i, i + NCHUNK, lambda k: tensor_turn(pe, i * TURNS + (IN_SCAN + k)))
                output_tensor(pe, 1)
                tensor_turn(pe, IN_PREPARE)
                prep[1][1](pe, lambda k: tensor_turn(pe, IN_PREPARE + 1 + k))
                for G in range(IN_PREPARE + 4, REST):
                    tensor_turn(pe, G)
                with nc.tensor.Fori(0, (B * GROUPS - REST) // SLOTS) as i:
                    for k in range(SLOTS):
                        tensor_turn(pe, i * SLOTS + (REST + k))
                for G in range(B * GROUPS, B * GROUPS + 2):
                    tensor_turn(pe, G)

            @block.scalar
            def _(act):
                project_scalar(act, 0)
                act.wait_ge(pr["delta_ready"], 1)
                with nc.scalar.Fori(0, NCHUNK) as i:
                    helped_scalar(act, i)
                prep[0][2](act)
                project_scalar(act, 1, lambda k: scalar_turn(act, k))
                act.wait_ge(pr["delta_ready"], 2)
                with nc.scalar.Fori(0, NCHUNK) as i:
                    scan_scalar(act, i, i + NCHUNK, lambda k: scalar_turn(act, i * TURNS + (IN_SCAN + k)))
                scalar_turn(act, IN_PREPARE)
                prep[1][2](act, lambda k: scalar_turn(act, IN_PREPARE + 1 + k))
                for G in range(IN_PREPARE + 4, REST):
                    scalar_turn(act, G)
                with nc.scalar.Fori(0, (B * GROUPS - REST) // SLOTS) as i:
                    for k in range(SLOTS):
                        scalar_turn(act, i * SLOTS + (REST + k))
                scalar_turn(act, B * GROUPS)

            @block.vector
            def _(v):
                nc.vector.memset(idx_all[:, GROUPS * TAPS:], 0)
                nc.vector.memset(colg[:, :], 0.0)
                for k, (signal, n) in enumerate((
                        (sc["h_done"], 2), (sc["hc_done"], 1), (sc["y_done"], 2), (sc["y_used"], 2), (sc["b_used"], 1),
                        (sc["zy_done"], 1), (sc["dbu_done"], 2),
                        (l3["prod_done"], SLOTS), (l3["t_psum"], 1), (l3["t_read"], 1), (l3["o_psum"], 1), (l3["o_read"], 1))):
                    nc.vector.memset(prime[:, k:k + 1], 0.0).then_inc(signal, n)
                vchain(v, nc.vector.memset(carry[:, :], 0.0))
                project_vector(v, 0)
                helped_du(v, 0)
                with nc.vector.Fori(0, NCHUNK - 1) as i:
                    helped_vector(v, i)
                helped_vector(v, NCHUNK - 1, ends=True)
                output_vector(v, 0)
                prep[0][3](v)
                project_vector(v, 1, lambda k: vector_turn(v, k))
                vchain(v, nc.vector.memset(carry[:, :], 0.0))
                with nc.vector.Fori(0, NCHUNK) as i:
                    vchain.enter(i, 1)

                    def turn(k):
                        G = i * TURNS + (IN_SCAN + k)
                        group_add(v, 0, G - 2, G - 2)
                        group_weigh(v, G, (IN_SCAN + k) % SLOTS, i + (IN_SCAN + k) // SLOTS)

                    scan_vector(v, i, i + NCHUNK, turn)
                vchain.leave(NCHUNK)
                output_vector(v, 1)
                vector_turn(v, IN_PREPARE)
                prep[1][3](v, lambda k: vector_turn(v, IN_PREPARE + 1 + k))
                for G in range(IN_PREPARE + 4, REST):
                    vector_turn(v, G)
                v.wait_ge(l3["resid_in"], 32 * B)
                with nc.vector.Fori(0, (B * GROUPS - REST) // SLOTS) as i:
                    for k in range(SLOTS):
                        G = i * SLOTS + (REST + k)
                        group_add(v, 1, G - 2, i * SLOTS + (REST - 2 - GROUPS + k))
                        group_weigh(v, G, (REST + k) % SLOTS, i + (REST + k) // SLOTS)
                for G in range(B * GROUPS, B * GROUPS + 2):
                    vector_turn(v, G)



def _square_constants():
    m = np.zeros((NMAT, P, P), np.float32)
    i = np.arange(P)
    m[M_IDENT] = np.eye(P)
    same_channel = i[:, None] % C == i[None, :] % C
    m[M_OWN] = 0.5 * (same_channel & (i[:, None] // 64 == i[None, :] // 64))
    m[M_PRE] = 0.5 * (same_channel & (i[:, None] // 64 == 1))
    same_quadrant = i[:, None] // C == i[None, :] // C
    m[M_PAIR] = 0.5 * (same_quadrant & (i[:, None] // 2 == i[None, :] // 2))
    m[M_MEAN] = same_quadrant / C
    m[M_CENTER] = m[M_IDENT] - m[M_MEAN]
    for b in range(B):
        for y in range(H):
            o = H * b + y
            m[M_LAP, o, o] = 4.0
            for s in (y - 1, y + 1):
                if 0 <= s < H:
                    m[M_LAP, H * b + s, o] = -1.0
            m[M_DOWN, H * b + (y + 1 if y < H - 1 else H - 2), o] = 1.0
            m[M_UPR, H * b + (y - 1 if y else 1), o] = 1.0
            if y:
                m[M_UP, o - 1, o] = 1.0
            else:
                m[M_UP0, o, o] = 1.0
        m[M_PICKB, b, H * b:H * b + H] = 1.0
    return np.ascontiguousarray(m.transpose(1, 0, 2))


def _bicubic_weights(out_size, in_size):
    f = np.float32
    src = (np.arange(out_size, dtype=f) + f(0.5)) * f(in_size / out_size) - f(0.5)
    i0 = np.floor(src)
    at = np.abs((src - i0)[:, None] - np.arange(-1, 3).astype(f)[None, :])
    a = f(-0.75)
    near = ((a + f(2)) * at - (a + f(3))) * at * at + f(1)
    far = (((at - f(5)) * at + f(8)) * at - f(4)) * a
    w = np.where(at <= 1, near, np.where(at < 2, far, f(0))).astype(f)
    idx = np.clip(i0[:, None].astype(np.int32) + np.arange(-1, 3)[None, :], 0, in_size - 1)
    m = np.zeros((out_size, in_size), f)
    np.add.at(m, (np.arange(out_size)[:, None], idx), w)
    return m


def _bicubic_rows():
    wy = _bicubic_weights(3 * H, 4)[H // 2:H // 2 + H]
    wx = _bicubic_weights(3 * W, 4)[W // 2:W // 2 + W]
    k = (wy.T[:, None, :, None] * wx.T[None, :, None, :]).reshape(16, L)
    replaced = (5 + 1 - 4) * 4 + (6 + 1 - 5)
    rows = np.zeros((64, HALF), np.float32)
    for h in range(2):
        part = k[:, h * HALF:(h + 1) * HALF]
        rows[h] = part[replaced]
        rows[32 + 16 * h:48 + 16 * h] = part
        rows[32 + 16 * h + replaced] = 0.0
    rows[2] = 1.0
    return rows


def _sample_base():
    p = np.arange(P)[:, None, None]
    g = np.arange(GROUPS)[None, :, None]
    k = np.arange(TAPS)[None, None, :]
    pixel = p // 32 * QUARTER + 32 * g + p % 32
    y = pixel // W - 1 + k // 3
    x = pixel % W - 1 + k % 3
    return np.ascontiguousarray(np.stack([y, x], axis=-1).astype(np.float32).reshape(P, GROUPS * TAPS * 2))


def _selectors():
    s = np.zeros((96, 2, PAIRS, 2, DI), np.float32)
    for part in range(3):
        for j in range(PAIRS):
            for h in range(2):
                s[32 * part + 2 * j + h, 0, j, h] = 1.0
                s[32 * part + 16 + 2 * j + h, 1, j, h] = 1.0
    return s.reshape(96, 2 * PAIRS * P)


def kernel(**inputs):
    import concourse.bacc as _bacc
    from concourse.bass_utils import run_bass_kernel_spmd as _run

    a = {k: np.asarray(v) for k, v in inputs.items()}
    rep = lambda v, n: np.tile(np.reshape(v, -1), n)
    vecs = np.zeros((P, NV), np.float32)
    for col, v in ((V_W0, rep(a["L0_conv_weight"], 4)), (V_B0, rep(a["L0_conv_bias"], 4)),
                   (V_GNW, rep(a["L1_conv_gn_weight"], 4)), (V_GNB, rep(a["L1_conv_gn_bias"], 4)),
                   (V_B1, rep(a["L1_conv_b1"], 2)), (V_B2, rep(a["L1_conv_b2"], 4)),
                   (V_LNW, rep(a["L2_conv_ln_w"], 4)), (V_LNB, rep(a["L2_conv_ln_b"], 4)),
                   (V_CB, rep(a["L2_conv_conv_b"], 2)), (V_BDT, rep(a["L2_conv_b_dt"], 2)),
                   (V_D, rep(a["L2_conv_D"], 2))):
        vecs[:, col] = v
    vecs[:, V_A:V_A + PAIRS] = a["L2_conv_A_log"].reshape(DI, PAIRS, 2).transpose(2, 0, 1).reshape(P, PAIRS)
    vecs[0:32, V_M3] = vecs[32:64, V_M3 + 1] = vecs[64:128, V_M3 + 2] = 1.0
    vecs[:, V_EPS] = GN_EPS
    vecs[32:48, V_HALF] = vecs[48:64, V_HALF + 1] = 1.0

    w = np.zeros((P, NW), np.float32)
    for q in range(4):
        r = q % 2
        first = W_ONE + 128 * (q // 2) + 64 * r
        w[32 * q:32 * q + 32, first:first + 64] = a["L1_conv_w1"].T
    for q in range(2):
        w[64 * q:64 * q + 64, W_TWO + 32 * q:W_TWO + 32 * q + 32] = a["L1_conv_w2"].T
    for j in range(4):
        for d in range(2):
            w[32 * j:32 * j + 32, W_INX + 64 * d:W_INX + 64 * d + 64] = a["L2_conv_W_in"][:DI].T
            w[32 * j:32 * j + 32, W_CONV + 64 * d:W_CONV + 64 * d + 64] = a["L2_conv_conv_w"][:, j]
    for d in range(2):
        w[96:128, W_INZ + 64 * d:W_INZ + 64 * d + 64] = a["L2_conv_W_in"][DI:].T
    for part in range(3):
        w[0:64, W_BC + 32 * part:W_BC + 32 * part + 32] = a["L2_conv_W_xproj"][2:].T
    w[0:2, W_DTA:W_DTA + 64] = a["L2_conv_W_xproj"][0:2]
    for d in range(2):
        w[0:2, W_DTB + 64 * d:W_DTB + 64 * d + 64] = a["L2_conv_W_dt"].T
        for m in range(2):
            w[64 * d:64 * d + 64, W_SUM + 64 * m:W_SUM + 64 * m + 64] = np.eye(DI)
    w[0:64, W_OUT:W_OUT + 32] = a["L2_conv_W_out"].T
    taps = np.concatenate([a["L3_conv_offset_w"], a["L3_conv_mask_w"]], axis=0)
    for dy in range(3):
        w[0:96, W_OFF + 32 * dy:W_OFF + 32 * dy + 27] = taps[:, :, dy].transpose(2, 1, 0).reshape(96, 27)
    l3 = a["L3_conv_weight"].reshape(C, C, TAPS).transpose(2, 1, 0)
    for r in range(3):
        w[:, W_L3 + C * r:W_L3 + C * r + C] = np.repeat(l3[2 * r:2 * r + 2, None], 2, axis=1).reshape(P, C)
    w[0:96, W_L3 + 3 * C:W_L3 + 4 * C] = l3[6:9].reshape(96, C)

    anchors = np.zeros((32, 2, C), np.float32)
    for s, name in enumerate(("L0_conv_mean_table", "L0_conv_std_table")):
        for h in range(2):
            anchors[16 * h:16 * h + 16, s] = a[name][3:7, 4:8].reshape(16, C)

    arrays = {"x": np.ascontiguousarray(a["x"]), "mats": _square_constants(), "vecs": vecs, "wts": w,
              "bic": _bicubic_rows(), "anchors": anchors, "base": _sample_base(), "sel": _selectors()}
    nc = _bacc.Bacc("TRN2", target_bir_lowering=False, num_devices=1)
    args = [nc.dram_tensor(f"in_{k}", v.shape, F32, kind="ExternalInput").ap() for k, v in arrays.items()]
    args.append(nc.dram_tensor("out_x", (B, C, H, W), F32, kind="ExternalOutput").ap())
    build(nc, *args)
    r = _run(nc, [{f"in_{k}": v for k, v in arrays.items()}], core_ids=[0])
    return r.results[0]["out_x"]
```

```python
import concourse.bass as bass
import numpy as np
from concourse import mybir
from contextlib import ExitStack

F32 = mybir.dt.float32
BF16 = mybir.dt.bfloat16
U32 = mybir.dt.uint32
ALU = mybir.AluOpType
ACT = mybir.ActivationFunctionType
AX = mybir.AxisListType

P = 128
B, C, H, W = 2, 32, 64, 64
L = H * W
HALF = L // 2
BANK = 512
WP = W + 2
DI = 64
DS = 16
PAIRS = DS // 2
CHUNK = 1024
NCHUNK = L // CHUNK
TAPS = 9
SLOTS = 5
GROUPS = L // P
QUARTER = L // 4
GN_EPS = 1e-5
ROUND = 12582912.0

(M_IDENT, M_OWN, M_PRE, M_PAIR, M_CENTER, M_MEAN, M_LAP, M_DOWN, M_UPR, M_UP, M_UP0, M_PICKB) = range(12)
NMAT = 12
(V_W0, V_B0, V_GNW, V_GNB, V_B1, V_B2, V_LNW, V_LNB, V_CB, V_BDT, V_D) = range(11)
V_A = 11
V_M3 = V_A + PAIRS
V_HALF = V_M3 + 3
V_EPS = V_HALF + 2
NV = V_EPS + 1
W_ONE = 0
W_TWO = W_ONE + 2 * 128
W_INX = W_TWO + 64
W_CONV = W_INX + 128
W_INZ = W_CONV + 128
W_BC = W_INZ + 128
W_DTA = W_BC + 96
W_DTB = W_DTA + 64
W_OUT = W_DTB + 128
W_SUM = W_OUT + 32
W_OFF = W_SUM + 128
W_L3 = W_OFF + 3 * 32
NW = W_L3 + 4 * 32


class Chain:

    def __init__(self, sem):
        self.sem, self.n, self.loop = sem, 0, 0

    def __call__(self, engine, ins):
        ins.then_inc(self.sem, 1)
        self.n += 1
        engine.wait_ge(self.sem, self.loop + self.n)

    def enter(self, i, per_turn):
        self.start, self.per_turn, self.loop = self.n, per_turn, i * per_turn

    def leave(self, turns):
        assert self.n == self.start + self.per_turn, (self.n - self.start, self.per_turn)
        self.n, self.loop = self.start + self.per_turn * turns, 0


def build(nc, x, mats, vecs, wts, bic, anchors, base, sel, out):
    ctx = ExitStack()
    with ctx:
        def sb(name, shape, dt=F32):
            return ctx.enter_context(nc.sbuf_tensor(name, shape, dt))

        def sem(name):
            return ctx.enter_context(nc.semaphore(name))

        X = sb("X", [P, HALF])
        mat = sb("mat", [P, NMAT, P])
        vec = sb("vec", [P, NV])
        wt = sb("wt", [P, NW])
        PS = ctx.enter_context(nc.psum_tensor("PS", [P, 8, BANK], F32))

        def M(k, rows=slice(0, P), cols=slice(0, P)):
            return mat[rows, k, cols]

        def V(k, n=1, rows=slice(0, P)):
            return vec[rows, k:k + n]

        ident = M(M_IDENT)
        x_half = x.rearrange("b c (h y) w -> b h c (y w)", h=2)
        vchain = Chain(sem("dve_own"))

        def banks(first, n, rows=slice(0, P)):
            return PS[rows, first:first + n, :].rearrange("p b n -> p (b n)")

        def tell(engine, ins, signal, n=1):
            ins.then_inc(signal, 1)
            engine.wait_ge(signal, n)

        st6 = sb("st6", [P, 4, 6])
        mv = sb("mv", [P, 2])
        S2 = sb("S2", [P, 2])
        tot = sb("tot", [P, 4])
        var = sb("var", [P, 2])
        std = sb("std", [P, 2])
        rstd = sb("rstd", [P, 2])
        mrs = sb("mrs", [P, 2])
        nmrs = sb("nmrs", [P, 1])

        def gn_bank_stats(v, q, rows=slice(0, P)):
            vchain(v, nc.vector.bn_stats(st6[rows, q, :], X[rows, q * BANK:(q + 1) * BANK]))

        def gn_partition_stats(v, rows=slice(0, P), banks_done=False):
            if not banks_done:
                for q in range(4):
                    gn_bank_stats(v, q, rows)
            vchain(v, nc.vector.bn_aggr(mv[rows, :], st6[rows, :, :].rearrange("p a b -> p (a b)")))
            vchain(v, nc.vector.tensor_copy(S2[rows, 0:1], mv[rows, 0:1]))
            return nc.vector.scalar_tensor_tensor(S2[rows, 1:2], mv[rows, 0:1], mv[rows, 0:1], mv[rows, 1:2],
                                                  ALU.mult, ALU.add)

        def variance(v, n, eps, rows=slice(0, P)):
            pairs = tot[rows, 0:2 * n].rearrange("p (n s) -> p n s", s=2)
            vchain(v, nc.vector.tensor_tensor(var[rows, 0:n], pairs[:, :, 0], pairs[:, :, 0], ALU.mult))
            vchain(v, nc.vector.tensor_tensor(var[rows, 0:n], pairs[:, :, 1], var[rows, 0:n], ALU.subtract))
            return nc.vector.tensor_scalar(std[rows, 0:n], var[rows, 0:n], eps, None, ALU.add)

        with ExitStack() as stage:
            bicubic = stage.enter_context(nc.sbuf_tensor("bicubic", [P, HALF], F32))
            patch = stage.enter_context(nc.sbuf_tensor("patch", [64, 2, 32], F32))
            LMS = stage.enter_context(nc.sbuf_tensor("LMS", [P, 2, P], F32))
            D = stage.enter_context(nc.sbuf_tensor("D", [P, 2, 3], F32))
            t1 = stage.enter_context(nc.sbuf_tensor("t1", [P, HALF], F32))
            xb = stage.enter_context(nc.sbuf_tensor("xb", [P, HALF], F32))
            pv = stage.enter_context(nc.sbuf_tensor("pv", [P, 3], F32))
            x_in, mat_in, vec_in, bic_in, rest_in = (sem(n) for n in ("x_in", "mat_in", "vec_in", "bic_in", "rest_in"))
            bic_zero = sem("bic_zero")
            stats0, totals0, sqrt0_go, sqrt0_done, d_ready, dt_done, l_ready, maps_done, xb_done = (
                sem(n) for n in ("stats0", "totals0", "sqrt0_go", "sqrt0_done", "d_ready", "dt_done", "l_ready",
                                 "maps_done", "xb_done"))
            with nc.Block() as block:
                @block.sync
                def _(sp):
                    for b in range(B):
                        for h in range(2):
                            q = 2 * b + h
                            sp.dma_start(X[32 * q:32 * q + 32, :], x_half[b, h]).then_inc(x_in, 16)
                    sp.dma_start(bicubic[0:64, :], bic).then_inc(bic_in, 16)
                    sp.dma_start(wt[:, :], wts).then_inc(rest_in, 16)
                    sp.wait_ge(rest_in, 16)

                @block.scalar
                def _(act):
                    act.dma_start(vec[:, :], vecs).then_inc(vec_in, 16)
                    act.dma_start(mat[:, :, :], mats).then_inc(mat_in, 16)
                    act.dma_start(patch[32:64, :, :], anchors).then_inc(vec_in, 16)
                    act.wait_ge(x_in, 64)
                    act.wait_ge(vec_in, 32)
                    nc.scalar.activation(xb[:, :], X[:, :], ACT.Identity, bias=V(V_B0)).then_inc(xb_done, 1)
                    act.wait_ge(sqrt0_go, 1)
                    nc.scalar.activation(std[:, :], std[:, :], ACT.Sqrt).then_inc(sqrt0_done, 1)
                    act.wait_ge(sqrt0_go, 2)
                    nc.scalar.activation(pv[:, 1:2], pv[:, 0:1], ACT.Sqrt).then_inc(sqrt0_done, 1)

                @block.gpsimd
                def _(pool):
                    nc.gpsimd.memset(bicubic[64:P, :], 0.0).then_inc(bic_zero, 1)

                @block.tensor
                def _(pe):
                    pe.wait_ge(mat_in, 16)
                    pe.wait_ge(stats0, 1)
                    nc.tensor.matmul(PS[:, 0, 0:2], M(M_OWN), S2[:, :], start=True, stop=True)
                    nc.tensor.matmul(PS[:, 0, 2:4], M(M_PRE), S2[:, :], start=True, stop=True).then_inc(totals0, 1)
                    pe.wait_ge(d_ready, 1)
                    for s in range(2):
                        last = nc.tensor.transpose(PS[0:3, 1, s * P:s * P + P], D[:, s, :], ident)
                    last.then_inc(dt_done, 1)
                    pe.wait_ge(bic_in, 16)
                    pe.wait_ge(bic_zero, 1)
                    pe.wait_ge(l_ready, 1)
                    for n in range(4):
                        for s in range(2):
                            last = nc.tensor.matmul(PS[:, 4 * s + n, :], LMS[:, s, :], bicubic[:, n * BANK:(n + 1) * BANK],
                                                    start=True, stop=True)
                        last.then_inc(maps_done, 1)

                @block.vector
                def _(v):
                    vchain(v, nc.vector.memset(LMS[:, :, :], 0.0))
                    v.wait_ge(vec_in, 32)
                    vchain(v, nc.vector.reciprocal(patch[32:64, 1, :], patch[32:64, 1, :]))
                    for s in range(2):
                        for h in range(2):
                            vchain(v, nc.vector.tensor_scalar(LMS[32:64, s, 32 * h:32 * h + 32], patch[32:64, s, :],
                                                              vec[32:64, V_HALF + h:V_HALF + h + 1], None, ALU.mult))
                    v.wait_ge(x_in, 64)
                    gn_partition_stats(v).then_inc(stats0, 1)
                    v.wait_ge(totals0, 1)
                    vchain(v, nc.vector.tensor_copy(tot[:, :], PS[:, 0, 0:4]))
                    variance(v, 2, GN_EPS).then_inc(sqrt0_go, 1)
                    v.wait_ge(sqrt0_done, 1)
                    vchain(v, nc.vector.reciprocal(rstd[:, :], std[:, :]))
                    vchain(v, nc.vector.tensor_tensor(mrs[:, :], tot[:, 0:4:2], rstd[:, :], ALU.mult))
                    vchain(v, nc.vector.tensor_tensor(pv[:, 0:1], rstd[:, 1:2], rstd[:, 1:2], ALU.mult))
                    tell(v, nc.vector.tensor_scalar(pv[:, 0:1], pv[:, 0:1], var[:, 1:2], float(L) / (L - 1), ALU.mult, ALU.mult), sqrt0_go, 2)
                    vchain(v, nc.vector.tensor_scalar(pv[:, 2:3], tot[:, 2:3], rstd[:, 1:2], mrs[:, 1:2], ALU.mult, ALU.subtract))
                    v.wait_ge(sqrt0_done, 2)
                    vchain(v, nc.vector.reciprocal(pv[:, 1:2], pv[:, 1:2]))
                    vchain(v, nc.vector.tensor_scalar(D[:, 0, :], V(V_M3, 3), pv[:, 2:3], None, ALU.mult))
                    vchain(v, nc.vector.tensor_scalar(D[:, 1, :], V(V_M3, 3), pv[:, 1:2], None, ALU.mult))
                    nc.vector.tensor_tensor(D[:, 0, 2:3], D[:, 0, 2:3], mrs[:, 0:1], ALU.add).then_inc(d_ready, 1)
                    v.wait_ge(dt_done, 1)
                    nc.vector.tensor_copy(LMS[0:3, :, :], PS[0:3, 1, 0:2 * P].rearrange("p (s n) -> p s n", s=2)).then_inc(l_ready, 1)
                    v.wait_ge(xb_done, 1)
                    for n in range(4):
                        cols = slice(n * BANK, (n + 1) * BANK)
                        v.wait_ge(maps_done, n + 1)
                        vchain(v, nc.vector.scalar_tensor_tensor(t1[:, cols], X[:, cols], rstd[:, 0:1], PS[:, n, :], ALU.mult, ALU.subtract))
                        vchain(v, nc.vector.tensor_tensor(t1[:, cols], t1[:, cols], PS[:, 4 + n, :], ALU.mult))
                        vchain(v, nc.vector.scalar_tensor_tensor(X[:, cols], t1[:, cols], V(V_W0), xb[:, cols], ALU.mult, ALU.add))
                        gn_bank_stats(v, n)

        with ExitStack() as stage:
            def tile(name, shape, dt=F32):
                return stage.enter_context(nc.sbuf_tensor(name, shape, dt))

            G = tile("G", [P, HALF])
            GR = tile("GR", [P, WP, C])
            GD = tile("GD", [P, WP, C])
            GU = tile("GU", [P, WP, C])
            NPROD = 8
            prod = tile("prod", [P, NPROD, WP, C])
            avg = tile("avg", [P, WP])
            df = tile("df", [P, 2, W])
            mm = tile("mm", [P, 2])
            mmT = tile("mmT", [2, B])
            mmB = tile("mmB", [B, 2])
            rng = tile("rng", [P, 4])
            kval = tile("kval", [P, W])
            n2 = tile("n2", [P, 2, W])
            rn = tile("rn", [P, 3, WP])
            ER = tile("ER", [P, WP])
            VD = tile("VD", [P, 3, WP])
            sim = tile("sim", [P, TAPS, W])
            cmp = tile("cmp", [P, TAPS, W])
            rank = tile("rank", [P, TAPS, W])
            rankB = tile("rankB", [P, TAPS, W])
            cmps = tile("cmps", [P, TAPS * (TAPS - 1) // 2, W])
            CMP_FIRST = [0] + [sum(TAPS - e for e in range(1, d)) for d in range(1, TAPS)]
            wk = tile("wk", [P, TAPS, W])
            wsum = tile("wsum", [P, 2, W])
            gn2 = tile("gn2", [P, 8])
            enh = tile("enh", [P, HALF])
            hid = tile("hid", [P, 2, HALF])
            names = ("stats1", "totals1", "sqrt1_go", "sqrt1_done", "g_done", "gn_stats", "gn_totals", "gr_ready",
                     "shift_done", "gd_ready", "lap_in", "lap_done", "mm_ready", "mmT_done", "mmT_ready", "mmB_done",
                     "mmB_ready", "rng_done", "norm2_ready", "norm_done", "rn_ready", "rn_shift_done", "vd_ready", "dm_done",
                     "sim_ready", "exp_done", "w_ready", "prod_ready", "prod_free", "agg_done", "enh_ready", "h_psum",
                     "h_ready", "f_psum", "pool_prod", "squared", "cmp_ready", "gain_done", "pool_sum", "affine_ready", "affine_done")
            S = {n: sem("s1_" + n) for n in names}
            BELOW = ((1, WP, -1), (1, W + 1, 0), (0, W + 1, 1))

            def below_product(engine, j):
                lo, hi, dx = BELOW[j]
                return engine.tensor_tensor(prod[:, j, lo:hi, :], GR[:, lo:hi, :], GD[:, lo + dx:hi + dx, :], ALU.mult)

            def weighted(engine, k, slot):
                return engine.tensor_tensor(prod[:, slot, 0:W, :], (GU, GR, GD)[k // 3][:, k % 3:k % 3 + W, :],
                                            wk[:, k, :].unsqueeze(2).to_broadcast([P, W, C]), ALU.mult)

            def pair_sum(engine, slot, other):
                return engine.tensor_tensor(prod[:, slot, 0:W, :], prod[:, slot, 0:W, :], prod[:, other, 0:W, :], ALU.add)

            SUMS = (((0,), (0,)), ((1,), (1,)), ((2, 3), (2, 3)), ((4,), (4,)), ((5, 8), (5, 0)))
            POOL_SUM = 6

            with nc.Block() as block:
                @block.gpsimd
                def _(pool):
                    pool.wait_ge(S["gr_ready"], 1)
                    nc.gpsimd.tensor_tensor(prod[:, 3, 0:W + 1, :], GR[:, 0:W + 1, :], GR[:, 1:W + 2, :],
                                            ALU.mult).then_inc(S["pool_prod"], 1)
                    pool.wait_ge(S["norm2_ready"], 1)
                    pool.wait_ge(S["gd_ready"], 1)
                    for j in (0, 2):
                        below_product(nc.gpsimd, j).then_inc(S["pool_prod"], 1)
                    for d in range(1, TAPS):
                        n = TAPS - d
                        pool.wait_ge(S["cmp_ready"], d)
                        gain = cmps[:, CMP_FIRST[d]:CMP_FIRST[d] + n, :]
                        if d == 1:
                            op = nc.gpsimd.tensor_copy(rankB[:, 0:n, :], gain)
                        else:
                            op = nc.gpsimd.tensor_tensor(rankB[:, 0:n, :], rankB[:, 0:n, :], gain, ALU.add)
                        op.then_inc(S["gain_done"], 1)
                        pool.wait_ge(S["gain_done"], d)
                    pool.wait_ge(S["w_ready"], 1)
                    weighted(nc.gpsimd, 6, 6)
                    weighted(nc.gpsimd, 7, 7).then_inc(S["pool_prod"], 1)
                    pool.wait_ge(S["pool_prod"], 4)
                    pair_sum(nc.gpsimd, 6, 7).then_inc(S["pool_sum"], 1)

                @block.vector
                def _(v):
                    gn_partition_stats(v, banks_done=True).then_inc(S["stats1"], 1)
                    v.wait_ge(S["totals1"], 1)
                    vchain(v, nc.vector.tensor_copy(tot[:, 0:2], PS[:, 0, 0:2]))
                    variance(v, 1, GN_EPS).then_inc(S["sqrt1_go"], 1)
                    v.wait_ge(S["sqrt1_done"], 1)
                    vchain(v, nc.vector.reciprocal(rstd[:, 0:1], std[:, 0:1]))
                    vchain(v, nc.vector.scalar_tensor_tensor(nmrs[:, :], tot[:, 0:1], -1.0, rstd[:, 0:1], ALU.mult, ALU.mult))
                    vchain(v, nc.vector.tensor_scalar(G[:, :], X[:, :], rstd[:, 0:1], nmrs[:, :], ALU.mult, ALU.add))
                    vchain(v, nc.vector.tensor_scalar(gn2[:, 0:1], tot[:, 0:1], rstd[:, 0:1], nmrs[:, :], ALU.mult, ALU.add))
                    vchain(v, nc.vector.tensor_tensor(gn2[:, 2:3], rstd[:, 0:1], rstd[:, 0:1], ALU.mult))
                    vchain(v, nc.vector.tensor_scalar(gn2[:, 2:3], gn2[:, 2:3], var[:, 0:1], None, ALU.mult))
                    nc.vector.scalar_tensor_tensor(gn2[:, 1:2], gn2[:, 0:1], gn2[:, 0:1], gn2[:, 2:3],
                                                   ALU.mult, ALU.add).then_inc(S["gn_stats"], 1)
                    vchain(v, nc.vector.transpose(GR[:, 1:W + 1, :], G[:, :].rearrange("p (y x) -> p x y", x=W)))
                    tell(v, nc.vector.tensor_copy(GR[:, 0:WP:W + 1, :], GR[:, 2:W:W - 3, :]), S["gr_ready"])
                    v.wait_ge(S["gn_totals"], 1)
                    vchain(v, nc.vector.tensor_copy(tot[:, 0:2], PS[:, 7, 0:2]))
                    variance(v, 1, GN_EPS).then_inc(S["sqrt1_go"], 1)
                    v.wait_ge(S["sqrt1_done"], 2)
                    vchain(v, nc.vector.reciprocal(gn2[:, 4:5], std[:, 0:1]))
                    vchain(v, nc.vector.tensor_tensor(gn2[:, 4:5], gn2[:, 4:5], V(V_GNW), ALU.mult))
                    vchain(v, nc.vector.tensor_tensor(gn2[:, 5:6], tot[:, 0:1], gn2[:, 4:5], ALU.mult))
                    tell(v, nc.vector.tensor_tensor(gn2[:, 5:6], V(V_GNB), gn2[:, 5:6], ALU.subtract), S["affine_ready"])
                    vchain(v, nc.vector.memset(avg[:, :], 0.0))
                    vchain(v, nc.vector.tensor_reduce(avg[:, 1:W + 1], GR[:, 1:W + 1, :], AX.X, ALU.add))
                    tell(v, nc.vector.tensor_scalar(avg[:, 1:W + 1], avg[:, 1:W + 1], 1.0 / C, None, ALU.mult), S["lap_in"])
                    v.wait_ge(S["squared"], 1)
                    tell(v, nc.vector.tensor_reduce(n2[:, 0, :], prod[:, 0, 0:W, :], AX.X, ALU.add), S["norm2_ready"])
                    v.wait_ge(S["pool_prod"], 1)
                    vchain(v, nc.vector.tensor_reduce(ER[:, 0:W + 1], prod[:, 3, 0:W + 1, :], AX.X, ALU.add))
                    v.wait_ge(S["norm_done"], 1)
                    vchain(v, nc.vector.tensor_scalar(n2[:, 1, :], n2[:, 1, :], 1e-12, None, ALU.max))
                    vchain(v, nc.vector.reciprocal(rn[:, 1, 1:W + 1], n2[:, 1, :]))
                    tell(v, nc.vector.tensor_copy(rn[:, 1, 0:WP:W + 1], rn[:, 1, 2:W:W - 3]), S["rn_ready"])
                    v.wait_ge(S["gd_ready"], 1)
                    vchain(v, below_product(nc.vector, 1))
                    for n, j in enumerate((1, 0, 2)):
                        lo, hi, dx = BELOW[j]
                        if n:
                            v.wait_ge(S["pool_prod"], n + 1)
                        tell(v, nc.vector.tensor_reduce(VD[:, j, lo:hi], prod[:, j, lo:hi, :], AX.X, ALU.add), S["vd_ready"], n + 1)
                    v.wait_ge(S["lap_done"], 1)
                    vchain(v, nc.vector.tensor_tensor(df[:, 0, :], PS[:, 6, 0:W], avg[:, 0:W], ALU.subtract))
                    vchain(v, nc.vector.tensor_tensor(df[:, 0, :], df[:, 0, :], avg[:, 2:W + 2], ALU.subtract))
                    vchain(v, nc.vector.tensor_scalar(df[:, 1, :], df[:, 0, :], -1.0, None, ALU.mult))
                    vchain(v, nc.vector.tensor_tensor(df[:, 0, :], df[:, 0, :], df[:, 1, :], ALU.max))
                    vchain(v, nc.vector.tensor_scalar(df[:, 1, :], df[:, 0, :], -1.0, None, ALU.mult))
                    tell(v, nc.vector.tensor_reduce(mm[:, :], df[:, :, :], AX.X, ALU.max), S["mm_ready"])
                    v.wait_ge(S["mmT_done"], 1)
                    tell(v, nc.vector.tensor_reduce(mmT[:, :], PS[0:2, 7, 0:P].rearrange("s (b y) -> s b y", b=B), AX.X, ALU.max), S["mmT_ready"])
                    v.wait_ge(S["mmB_done"], 1)
                    tell(v, nc.vector.tensor_copy(mmB[:, :], PS[0:B, 7, 0:2]), S["mmB_ready"])
                    v.wait_ge(S["rng_done"], 1)
                    vchain(v, nc.vector.tensor_copy(rng[:, 0:2], PS[:, 7, 0:2]))
                    vchain(v, nc.vector.tensor_tensor(rng[:, 2:3], rng[:, 0:1], rng[:, 1:2], ALU.add))
                    vchain(v, nc.vector.tensor_scalar(rng[:, 2:3], rng[:, 2:3], 1e-8, None, ALU.add))
                    vchain(v, nc.vector.reciprocal(rng[:, 3:4], rng[:, 2:3]))
                    vchain(v, nc.vector.tensor_scalar(kval[:, :], df[:, 0, :], rng[:, 1:2], rng[:, 3:4], ALU.add, ALU.mult))
                    vchain(v, nc.vector.tensor_scalar(kval[:, :], kval[:, :], 7.0, ROUND, ALU.mult, ALU.add))
                    vchain(v, nc.vector.tensor_scalar(kval[:, :], kval[:, :], ROUND - 1.0, 9.0, ALU.subtract, ALU.min))
                    v.wait_ge(S["rn_shift_done"], 1)
                    vchain(v, nc.vector.tensor_copy(rn[:, 0:3:2, :], PS[:, 6, 0:2 * WP].rearrange("p (s x) -> p s x", s=2)))
                    for dx in (-1, 0, 1):
                        lo, hi = 1 + dx, W + 1 + dx
                        vchain(v, nc.vector.tensor_tensor(sim[:, 7 + dx, :], VD[:, 1 + dx, 1:W + 1], rn[:, 2, lo:hi], ALU.mult))
                    vchain(v, nc.vector.tensor_tensor(sim[:, 3, :], ER[:, 0:W], rn[:, 1, 0:W], ALU.mult))
                    vchain(v, nc.vector.tensor_tensor(sim[:, 4, :], n2[:, 0, :], rn[:, 1, 1:W + 1], ALU.mult))
                    vchain(v, nc.vector.tensor_tensor(sim[:, 5, :], ER[:, 1:W + 1], rn[:, 1, 2:W + 2], ALU.mult))
                    v.wait_ge(S["dm_done"], 1)
                    for dx in (-1, 0, 1):
                        lo, hi = 1 + dx, W + 1 + dx
                        vchain(v, nc.vector.tensor_tensor(sim[:, 1 + dx, :], PS[:, 5, (1 + dx) * W:(2 + dx) * W], rn[:, 0, lo:hi], ALU.mult))
                    tell(v, nc.vector.tensor_tensor(sim[:, :, :], sim[:, :, :],
                                                      rn[:, 1, 1:W + 1].unsqueeze(1).to_broadcast([P, TAPS, W]), ALU.mult), S["sim_ready"])
                    for k in range(TAPS):
                        last = nc.vector.memset(rank[:, k, :], float(TAPS - 1 - k))
                    vchain(v, last)
                    for d in range(1, TAPS):
                        n = TAPS - d
                        gain = cmps[:, CMP_FIRST[d]:CMP_FIRST[d] + n, :]
                        tell(v, nc.vector.tensor_tensor(gain, sim[:, 0:n, :], sim[:, d:TAPS, :], ALU.is_ge), S["cmp_ready"], d)
                        vchain(v, nc.vector.tensor_tensor(rank[:, d:TAPS, :], rank[:, d:TAPS, :], gain, ALU.add))
                    v.wait_ge(S["gain_done"], TAPS - 1)
                    vchain(v, nc.vector.tensor_tensor(rank[:, 0:TAPS - 1, :], rank[:, 0:TAPS - 1, :], rankB[:, 0:TAPS - 1, :], ALU.subtract))
                    vchain(v, nc.vector.tensor_tensor(cmp[:, :, :], rank[:, :, :],
                                                      kval[:, :].unsqueeze(1).to_broadcast([P, TAPS, W]), ALU.is_lt))
                    v.wait_ge(S["exp_done"], 1)
                    vchain(v, nc.vector.tensor_tensor(wk[:, :, :], wk[:, :, :], cmp[:, :, :], ALU.mult))
                    vchain(v, nc.vector.tensor_reduce(wsum[:, 0, :], wk[:, :, :].rearrange("p k x -> p x k"), AX.X, ALU.add))
                    vchain(v, nc.vector.reciprocal(wsum[:, 1, :], wsum[:, 0, :]))
                    tell(v, nc.vector.tensor_tensor(wk[:, :, :], wk[:, :, :],
                                                      wsum[:, 1, :].unsqueeze(1).to_broadcast([P, TAPS, W]), ALU.mult), S["w_ready"])
                    for n, (neighbours, slots) in enumerate(SUMS):
                        if 0 in slots and n:
                            v.wait_ge(S["prod_free"], 1)
                        for k, slot in zip(neighbours, slots):
                            last = weighted(nc.vector, k, slot)
                        if len(slots) > 1:
                            vchain(v, last)
                            last = pair_sum(nc.vector, *slots)
                        last.then_inc(S["prod_ready"], 1)
                    v.wait_ge(S["agg_done"], 1)
                    vchain(v, nc.vector.transpose(enh[:, :].rearrange("p (y x) -> p x y", x=W),
                                                  banks(0, 4).rearrange("p (x c) -> p x c", c=C)))
                    v.wait_ge(S["affine_done"], 1)
                    for n in range(4):
                        cols = slice(n * BANK, (n + 1) * BANK)
                        tell(v, nc.vector.tensor_tensor(enh[:, cols], G[:, cols], enh[:, cols], ALU.add), S["enh_ready"], n + 1)
                    vchain(v, nc.vector.tensor_tensor(X[:, :], X[:, :], enh[:, :], ALU.add))
                    for n in range(4):
                        v.wait_ge(S["f_psum"], n + 1)
                        vchain(v, nc.vector.scalar_tensor_tensor(X[:, n * BANK:(n + 1) * BANK], PS[:, n, :], V(V_B2),
                                                                 X[:, n * BANK:(n + 1) * BANK], ALU.add, ALU.add))
                        gn_bank_stats(v, n)

                @block.scalar
                def _(act):
                    act.wait_ge(S["sqrt1_go"], 1)
                    nc.scalar.activation(std[:, 0:1], std[:, 0:1], ACT.Sqrt).then_inc(S["sqrt1_done"], 1)
                    act.wait_ge(S["sqrt1_go"], 2)
                    nc.scalar.activation(std[:, 0:1], std[:, 0:1], ACT.Sqrt).then_inc(S["sqrt1_done"], 1)
                    act.wait_ge(S["gr_ready"], 1)
                    nc.scalar.activation(prod[:, 0, 0:W, :], GR[:, 1:W + 1, :], ACT.Square).then_inc(S["squared"], 1)
                    act.wait_ge(S["norm2_ready"], 1)
                    nc.scalar.activation(n2[:, 1, :], n2[:, 0, :], ACT.Sqrt).then_inc(S["norm_done"], 1)
                    for j, dst in enumerate((GD, GU)):
                        act.wait_ge(S["shift_done"], j + 1)
                        nc.scalar.activation(dst[:, :, :].rearrange("p x c -> p (x c)"), banks(0, 5)[:, 0:WP * C],
                                             ACT.Copy).then_inc(S["gd_ready"], 1)
                    act.wait_ge(S["affine_ready"], 1)
                    nc.scalar.activation(G[:, :], G[:, :], ACT.Identity, bias=gn2[:, 5:6], scale=gn2[:, 4:5]).then_inc(S["affine_done"], 1)
                    act.wait_ge(S["sim_ready"], 1)
                    nc.scalar.activation(wk[:, :, :], sim[:, :, :], ACT.Exp).then_inc(S["exp_done"], 1)
                    for m in range(8):
                        act.wait_ge(S["h_psum"], m + 1)
                        nc.scalar.activation(hid[:, m % 2, (m // 2) * BANK:(m // 2 + 1) * BANK], PS[:, 4 + m % 4, :],
                                             ACT.Relu, bias=V(V_B1)).then_inc(S["h_ready"], 1)

                @block.tensor
                def _(pe):
                    pe.wait_ge(S["stats1"], 1)
                    nc.tensor.matmul(PS[:, 0, 0:2], M(M_OWN), S2[:, :], start=True, stop=True).then_inc(S["totals1"], 1)
                    pe.wait_ge(S["gn_stats"], 1)
                    nc.tensor.matmul(PS[:, 7, 0:2], M(M_PAIR), gn2[:, 0:2], start=True, stop=True).then_inc(S["gn_totals"], 1)
                    pe.wait_ge(S["gr_ready"], 1)
                    flat = GR[:, :, :].rearrange("p x c -> p (x c)")

                    def shift_rows(k):
                        for n in range(5):
                            hi = min((n + 1) * BANK, WP * C)
                            last = nc.tensor.matmul(PS[:, n, 0:hi - n * BANK], M(k), flat[:, n * BANK:hi], start=True, stop=True)
                        last.then_inc(S["shift_done"], 1)

                    shift_rows(M_DOWN)
                    pe.wait_ge(S["lap_in"], 1)
                    nc.tensor.matmul(PS[:, 6, 0:W], M(M_LAP), avg[:, 1:W + 1], start=True, stop=True).then_inc(S["lap_done"], 1)
                    pe.wait_ge(S["gd_ready"], 1)
                    shift_rows(M_UPR)
                    pe.wait_ge(S["vd_ready"], 3)
                    for dx in (-1, 0, 1):
                        o = PS[:, 5, (1 + dx) * W:(2 + dx) * W]
                        nc.tensor.matmul(o, M(M_UP), VD[:, 1 - dx, 1 + dx:1 + dx + W], start=True, stop=False)
                        last = nc.tensor.matmul(o, M(M_UP0), VD[:, 1 + dx, 1:W + 1], start=False, stop=True)
                    last.then_inc(S["dm_done"], 1)
                    pe.wait_ge(S["mm_ready"], 1)
                    nc.tensor.transpose(PS[0:2, 7, 0:P], mm[:, :], ident).then_inc(S["mmT_done"], 1)
                    pe.wait_ge(S["rn_ready"], 1)
                    nc.tensor.matmul(PS[:, 6, 0:WP], M(M_UPR), rn[:, 1, :], start=True, stop=True)
                    nc.tensor.matmul(PS[:, 6, WP:2 * WP], M(M_DOWN), rn[:, 1, :], start=True, stop=True).then_inc(S["rn_shift_done"], 1)
                    pe.wait_ge(S["mmT_ready"], 1)
                    nc.tensor.transpose(PS[0:2, 7, 0:2], mmT[:, :], M(M_IDENT, slice(0, 2), slice(0, 2))).then_inc(S["mmB_done"], 1)
                    pe.wait_ge(S["mmB_ready"], 1)
                    nc.tensor.matmul(PS[:, 7, 0:2], M(M_PICKB, slice(0, B)), mmB[:, :], start=True, stop=True).then_inc(S["rng_done"], 1)
                    pe.wait_ge(S["gd_ready"], 2)
                    order = [slots[0] for _, slots in SUMS]
                    order.insert(len(order) - 1, POOL_SUM)
                    for t, slot in enumerate(order):
                        if slot == POOL_SUM:
                            pe.wait_ge(S["pool_sum"], 1)
                        else:
                            pe.wait_ge(S["prod_ready"], min(t + 1, len(SUMS)))
                        for n in range(4):
                            last = nc.tensor.matmul(PS[:, n, :], ident,
                                                    prod[:, slot, 0:W, :].rearrange("p x c -> p (x c)")[:, n * BANK:(n + 1) * BANK],
                                                    start=(t == 0), stop=(t == len(order) - 1))
                        last.then_inc(S["prod_free"] if t < len(order) - 1 else S["agg_done"], 1)

                    def ffn_out(m):
                        n, r = m // 2, m % 2
                        pe.wait_ge(S["h_ready"], m + 1)
                        last = nc.tensor.matmul(PS[64 * r:64 * r + 64, n, :], wt[:, W_TWO:W_TWO + 64],
                                                hid[:, r, n * BANK:(n + 1) * BANK], start=True, stop=True)
                        if r == 1:
                            last.then_inc(S["f_psum"], 1)

                    for m in range(8):
                        n, r = m // 2, m % 2
                        if r == 0:
                            pe.wait_ge(S["enh_ready"], n + 1)
                        if m >= 4:
                            pe.wait_ge(S["h_ready"], m - 3)
                        nc.tensor.matmul(PS[:, 4 + m % 4, :], wt[:, W_ONE + P * r:W_ONE + P * r + P], enh[:, n * BANK:(n + 1) * BANK],
                                         start=True, stop=True).then_inc(S["h_psum"], 1)
                        if m:
                            ffn_out(m - 1)
                    ffn_out(7)

        XN = sb("XN", [P, B, L])
        UZ = sb("UZ", [P, 2 * L])
        u = UZ[:, 0:L]
        zy = UZ[:, L:2 * L]
        wx = sb("wx", [P, P])
        wdt = sb("wdt", [P, P])
        diagD = sb("diagD", [P, P])
        bdt20 = sb("bdt20", [P, 1])
        negA = sb("negA", [P, PAIRS])
        selb = sb("selb", [96, 2, PAIRS, P], BF16)

        g = sb("ln_g", [P, HALF])
        xn_in = [[sem(f"xn_in{b}{h}") for h in range(2)] for b in range(B)]

        def load_tokens(engine, b, h, shifts):
            q = 2 * b + h
            for j in shifts:
                first = h * HALF + 3 - j
                n = min(HALF, L - first)
                engine.dma_start(XN[32 * j:32 * j + 32, b, first:first + n], g[32 * q:32 * q + 32, 0:n]).then_inc(xn_in[b][h], 16)

        with ExitStack() as stage:
            sq = stage.enter_context(nc.sbuf_tensor("ln_sq", [P, HALF], F32))
            selw = stage.enter_context(nc.sbuf_tensor("selw", [96, 2 * PAIRS * P], F32))
            names = ("sel_in", "stats", "totals", "sqrt_go", "sqrt_done", "g_ready", "centered", "squared", "var_done",
                     "std_done", "xn_ready", "zeroed", "rstd_done", "dt_psum", "expA_done", "w_done")
            S = {n: sem("s2_" + n) for n in names}
            with nc.Block() as block:
                @block.sync
                def _(sp):
                    sp.dma_start(selw[:, :], sel).then_inc(S["sel_in"], 16)
                    sp.wait_ge(S["zeroed"], 1)
                    sp.wait_ge(S["xn_ready"], 4)
                    load_tokens(sp, 0, 0, (0, 1))

                @block.tensor
                def _(pe):
                    nc.tensor.matmul(PS[0:DI, 4, 0:P], wt[0:2, W_DTA:W_DTA + DI], wt[0:2, W_DTB:W_DTB + P],
                                     start=True, stop=True).then_inc(S["dt_psum"], 1)
                    pe.wait_ge(S["stats"], 1)
                    nc.tensor.matmul(PS[:, 0, 0:2], M(M_OWN), S2[:, :], start=True, stop=True).then_inc(S["totals"], 1)
                    pe.wait_ge(S["g_ready"], 1)
                    for n in range(4):
                        nc.tensor.matmul(PS[:, n, :], M(M_CENTER), g[:, n * BANK:(n + 1) * BANK], start=True,
                                         stop=True).then_inc(S["centered"], 1)
                    pe.wait_ge(S["w_done"], 1)
                    for n in range(4):
                        pe.wait_ge(S["squared"], n + 1)
                        nc.tensor.matmul(PS[:, 4 + n, :], M(M_MEAN), sq[:, n * BANK:(n + 1) * BANK], start=True,
                                         stop=True).then_inc(S["var_done"], 1)

                @block.scalar
                def _(act):
                    nc.scalar.activation(negA[:, :], V(V_A, PAIRS), ACT.Exp).then_inc(S["expA_done"], 1)
                    act.wait_ge(S["sqrt_go"], 1)
                    nc.scalar.activation(std[:, 0:1], std[:, 0:1], ACT.Sqrt).then_inc(S["sqrt_done"], 1)
                    part = lambda n: sq[:, n * BANK:(n + 1) * BANK]
                    for n in range(4):
                        act.wait_ge(S["centered"], n + 1)
                        nc.scalar.activation(part(n), PS[:, n, :], ACT.Square).then_inc(S["squared"], 1)
                    for n in range(4):
                        act.wait_ge(S["var_done"], n + 1)
                        nc.scalar.activation(part(n), PS[:, 4 + n, :], ACT.Ln, bias=V(V_EPS)).then_inc(S["std_done"], 1)
                    for n in range(4):
                        act.wait_ge(S["std_done"], n + 1)
                        nc.scalar.activation(part(n), part(n), ACT.Exp, scale=-0.5).then_inc(S["rstd_done"], 1)
                    act.wait_ge(S["zeroed"], 1)
                    act.wait_ge(S["xn_ready"], 4)
                    load_tokens(act, 0, 0, (2, 3))

                @block.vector
                def _(v):
                    gn_partition_stats(v, banks_done=True).then_inc(S["stats"], 1)
                    v.wait_ge(S["totals"], 1)
                    vchain(v, nc.vector.tensor_copy(tot[:, 0:2], PS[:, 0, 0:2]))
                    variance(v, 1, GN_EPS).then_inc(S["sqrt_go"], 1)
                    v.wait_ge(S["sqrt_done"], 1)
                    vchain(v, nc.vector.reciprocal(rstd[:, 0:1], std[:, 0:1]))
                    vchain(v, nc.vector.scalar_tensor_tensor(nmrs[:, :], tot[:, 0:1], -1.0, rstd[:, 0:1], ALU.mult, ALU.mult))
                    tell(v, nc.vector.tensor_scalar(g[:, :], X[:, :], rstd[:, 0:1], nmrs[:, :], ALU.mult, ALU.add), S["g_ready"])
                    tell(v, nc.vector.memset(XN[0:96, :, 0:3], 0.0), S["zeroed"])
                    vchain(v, nc.vector.tensor_tensor(wx[:, :], wt[:, W_INX:W_INX + P], wt[:, W_CONV:W_CONV + P], ALU.mult))
                    vchain(v, nc.vector.tensor_scalar(bdt20[:, :], V(V_BDT), 20.0, None, ALU.subtract))
                    vchain(v, nc.vector.tensor_scalar(diagD[:, :], ident, V(V_D), None, ALU.mult))
                    v.wait_ge(S["expA_done"], 1)
                    vchain(v, nc.vector.tensor_scalar(negA[:, :], negA[:, :], -1.0, None, ALU.mult))
                    v.wait_ge(S["sel_in"], 16)
                    vchain(v, nc.vector.tensor_copy(selb[:, :, :, :].rearrange("p a b c -> p (a b c)"), selw[:, :]))
                    v.wait_ge(S["dt_psum"], 1)
                    vchain(v, nc.vector.memset(wdt[DI:P, :], 0.0))
                    tell(v, nc.vector.tensor_copy(wdt[0:DI, :], PS[0:DI, 4, 0:P]), S["w_done"])
                    for n in range(4):
                        cols = slice(n * BANK, (n + 1) * BANK)
                        v.wait_ge(S["rstd_done"], n + 1)
                        vchain(v, nc.vector.tensor_tensor(g[:, cols], PS[:, n, :], sq[:, cols], ALU.mult))
                        tell(v, nc.vector.tensor_scalar(g[:, cols], g[:, cols], V(V_LNW), V(V_LNB), ALU.mult, ALU.add), S["xn_ready"], n + 1)

        scratch = sb("scratch", [P, 9 * CHUNK])

        def chunk_buffer(k, n=1):
            return scratch[:, k * CHUNK:(k + n) * CHUNK]

        dl = XN[:, 0, :]
        du = chunk_buffer(0)

        def resid(c):
            return chunk_buffer(2 + c % 2)

        hs = chunk_buffer(3)
        dA = chunk_buffer(4, 2).rearrange("p (s n) -> p s n", s=2)
        dBC = chunk_buffer(6, 2).rearrange("p (s n) -> p s n", s=2)
        parts = sb("parts", [96, L], BF16)
        prime = sb("prime", [P, 16])
        carry = sb("carry", [P, PAIRS])

        pr = {n: sem("proj_" + n) for n in ("xc_psum", "z_psum", "u_done", "z_done", "dt_psum", "v_ready", "bc_psum",
                                            "hi_done", "r_read", "clamp_done", "exp_done", "log_done", "mid_done", "parts_ready", "delta_ready")}
        sc = {n: sem("scan_" + n) for n in ("b_psum", "c_psum", "b_used", "exp_done", "h_done", "hc_done", "y_done", "y_used",
                                            "dbu_done", "du_done",
                                            "o_psum")}
        l3 = {n: sem("l3_" + n) for n in (
            "stats", "totals", "sqrt_go", "sqrt_done", "g_ready", "corner_ready", "shift_done", "below_in", "below_ready", "table_in",
            "zeroed", "g3_in", "g3_ready", "off_psum", "mask_in", "mask_exp", "base_in", "resid_in",
            "idx_ready", "prod_done", "rows_done", "sum_done", "t_psum", "t_read", "o_psum", "o_read", "out_dma")}
        gathered = [sem(f"gathered{k}") for k in range(SLOTS)]

        GLEN = (H + 2) * W
        G3s = [sb("G3", [96, GLEN])[:, :], UZ[0:96, 0:GLEN]]
        tabs = [t.rearrange("p (x k c) -> p x k c", k=4, c=C)
                for t in (chunk_buffer(0, 8), XN[:, :, :].rearrange("p b n -> p (b n)"))]
        temps = [XN[:, 0, :], scratch]
        tables = [nc.dram_tensor(f"corner_table_{b}", (L, 4 * C), F32, kind="Internal").ap() for b in range(B)]
        idx_all = sb("idx_all", [P, (B * GROUPS + SLOTS) * TAPS], U32)
        idx_slot = sb("idx_slot", [P, SLOTS, TAPS], U32)
        coef = sb("coef", [P, B * GROUPS, TAPS, 4])
        got = sb("got", [P, SLOTS, TAPS, 4, C])
        got_flat = got[:, :, :, :, :].rearrange("p s t k c -> p (s t k c)")
        log_tmps = [got_flat[:, 0:L], chunk_buffer(4, 4)]
        Bs = [chunk_buffer(1), chunk_buffer(2)]
        dBu = [chunk_buffer(8), got_flat[:, L:L + CHUNK]]
        prodg = sb("prodg", [P, TAPS, 4, C])
        colg = sb("colg", [P, 4 * P])
        colT = sb("colT", [P, 4 * P])


        def group_gather(pool, b, G, slot, index):
            pool.wait_ge(l3["prod_done"], G + 1)
            pool.nop(nofuse=True)
            for tap in range(TAPS):
                pool.indirect_dma_start(got[:, slot, tap, :, :].rearrange("p k c -> p (k c)"), None, tables[b],
                                        bass.IndirectOffsetOnAxis(ap=index[:, tap:tap + 1], axis=0)
                                        ).then_inc(gathered[slot], 16)

        def group_weigh(v, G, slot, uses):
            v.wait_ge(gathered[slot], uses * (16 * TAPS) + 16 * TAPS)
            v.nop(nofuse=True)
            nc.vector.tensor_copy(idx_slot[:, slot, :], idx_all[:, bass.ds((G + SLOTS) * TAPS, TAPS)])
            if not isinstance(G, int) or G:
                v.wait_ge(l3["sum_done"], G)
            tell(v, nc.vector.tensor_tensor(prodg[:, :, :, :].rearrange("p t k c -> p (t k) c"),
                                            got[:, slot, :, :, :].rearrange("p t k c -> p (t k) c"),
                                            coef[:, bass.ds(G, 1), :, :].rearrange("p o t k -> p (o t k)").unsqueeze(2).to_broadcast([P, TAPS * 4, C]),
                                            ALU.mult), l3["prod_done"], G + (SLOTS + 1))
            tell(v, nc.vector.tensor_tensor(prodg[:, 6:9, 0:2, :], prodg[:, 6:9, 0:2, :], prodg[:, 6:9, 2:4, :], ALU.add),
                 l3["rows_done"], G + 1)
            v.wait_ge(l3["t_psum"], G + 1)
            nc.vector.tensor_tensor(colg[:, 0:3 * P].rearrange("p (t k c) -> p t (k c)", k=2, c=C),
                                    prodg[:, 0:6, 0:2, :].rearrange("p t k c -> p t (k c)"),
                                    prodg[:, 0:6, 2:4, :].rearrange("p t k c -> p t (k c)"), ALU.add)
            nc.vector.tensor_tensor(colg[:, 3 * P:3 * P + 3 * C].rearrange("p (t c) -> p t c", c=C),
                                    prodg[:, 6:9, 0, :], prodg[:, 6:9, 1, :], ALU.add).then_inc(l3["sum_done"], 1)

        def group_transpose(pe, G):
            pe.wait_ge(l3["sum_done"], G + 1)
            pe.wait_ge(l3["t_read"], G + 1)
            for r in range(4):
                last = nc.tensor.transpose(PS[:, 6, r * P:r * P + P], colg[:, r * P:r * P + P], ident)
            last.then_inc(l3["t_psum"], 1)

        def group_copy(act, G):
            act.wait_ge(l3["t_psum"], G + 2)
            act.wait_ge(l3["o_psum"], G + 1)
            nc.scalar.activation(colT[:, :], PS[:, 6, :], ACT.Copy).then_inc(l3["t_read"], 1)

        def group_pixels(t, g):
            return t[:, 0:L].rearrange("c (q n) -> c q n", q=4)[:, :, bass.ds(g * 32, 32)]

        def group_multiply(pe, b, G, g):
            pe.wait_ge(l3["t_read"], G + 2)
            pe.wait_ge(l3["o_read"], G + 1)
            for r in range(4):
                nc.tensor.matmul(PS[0:C, 7, 0:P], wt[:, W_L3 + C * r:W_L3 + C * r + C], colT[:, r * P:r * P + P],
                                 start=(r == 0), stop=False)
            nc.tensor.matmul(PS[0:C, 7, 0:P], M(M_IDENT, slice(0, 96), slice(0, C)), group_pixels(G3s[b], g),
                             start=False, stop=True).then_inc(l3["o_psum"], 1)

        def group_out(act, b, G, g):
            act.wait_ge(l3["o_psum"], G + 2)
            act.nop(nofuse=True)
            nc.scalar.activation(group_pixels(G3s[b][0:C, :], g), PS[0:C, 7, 0:P].rearrange("c (q n) -> c q n", q=4),
                                 ACT.Copy).then_inc(l3["o_read"], 1)

        def tensor_turn(pe, G):
            if G >= 2:
                b = (G - 2) // GROUPS
                if (G - 2) % GROUPS == 0:
                    pe.wait_ge(l3["resid_in"], 32 * (b + 1))
                group_multiply(pe, b, G - 2, G - 2 - b * GROUPS)
            if 1 <= G < B * GROUPS + 1:
                group_transpose(pe, G - 1)

        def tensor_turn_in_loop(pe, b, G, g):
            group_multiply(pe, b, G - 2, g - 2)
            group_transpose(pe, G - 1)

        def scalar_turn(act, G):
            if G >= 2:
                b = (G - 2) // GROUPS
                group_out(act, b, G - 2, G - 2 - b * GROUPS)
            if 1 <= G < B * GROUPS + 1:
                group_copy(act, G - 1)

        def scalar_turn_in_loop(act, b, G, g):
            group_out(act, b, G - 2, g - 2)
            group_copy(act, G - 1)

        def vector_turn(v, G):
            if G < B * GROUPS:
                group_weigh(v, G, G % SLOTS, G // SLOTS)

        def nothing(k):
            pass


        def project_delta(v, b, c):
            cols = bass.ds(c * CHUNK, CHUNK)
            v.wait_ge(pr["v_ready"], c + (4 * b + 1))
            v.wait_ge(pr["log_done"], c + (4 * b + 1))
            nc.vector.tensor_tensor(dl[:, cols], dl[:, cols], log_tmps[b][:, cols], ALU.add).then_inc(pr["delta_ready"], 1)

        def project_tensor(pe, b, between=nothing):
            if b == 1:
                pe.wait_ge(l3["below_ready"], 1)
                pe.wait_ge(l3["mask_in"], 1)

            def tokens(n):
                cols = slice(n * BANK, (n + 1) * BANK)
                if n % 4 == 0:
                    pe.wait_ge(xn_in[b][n // 4], 16 * 4)
                if n >= 2:
                    pe.wait_ge(pr["z_done"], 8 * b + n - 1)
                nc.tensor.matmul(PS[:, n % 2, :], wx[:, :], XN[:, b, cols], start=True, stop=True).then_inc(pr["xc_psum"], 1)
                nc.tensor.matmul(PS[:, 2 + n % 2, :], wt[:, W_INZ:W_INZ + P], XN[:, b, cols],
                                 start=True, stop=True).then_inc(pr["z_psum"], 1)

            def delta(c):
                pe.wait_ge(pr["u_done"], 8 * b + 2 * c + 2)
                if c:
                    pe.wait_ge(pr["v_ready"], 4 * b + c)
                for n in range(2):
                    last = nc.tensor.matmul(PS[:, 4 + n, :], wdt[:, :], u[:, (2 * c + n) * BANK:(2 * c + n + 1) * BANK],
                                            start=True, stop=True)
                last.then_inc(pr["dt_psum"], 1)

            def b_and_c(c):
                if c == 0:
                    pe.wait_ge(pr["z_done"], 8 * b + 8)
                if c >= 2:
                    pe.wait_ge(pr["r_read"], 4 * b + c - 1)
                for n in range(2):
                    last = nc.tensor.matmul(PS[0:96, 2 * (c % 2) + n, :], wt[:, W_BC:W_BC + 96],
                                            u[:, (2 * c + n) * BANK:(2 * c + n + 1) * BANK], start=True, stop=True)
                last.then_inc(pr["bc_psum"], 1)

            for n in range(4):
                tokens(n)
            delta(0)
            between(0)
            tokens(4), tokens(5), delta(1), tokens(6), tokens(7), delta(2)
            b_and_c(0), b_and_c(1)
            delta(3)
            between(1)
            b_and_c(2)
            between(2)
            b_and_c(3)
            between(3)

        def project_scalar(act, b, between=nothing):
            def gated(n):
                k = 8 * b + n
                cols = slice(n * BANK, (n + 1) * BANK)
                act.wait_ge(pr["xc_psum"], k + 1)
                nc.scalar.activation(u[:, cols], PS[:, n % 2, :], ACT.Silu, bias=V(V_CB)).then_inc(pr["u_done"], 1)
                act.wait_ge(pr["z_psum"], k + 1)
                nc.scalar.activation(zy[:, cols], PS[:, 2 + n % 2, :], ACT.Silu).then_inc(pr["z_done"], 1)

            def high(c):
                act.wait_ge(pr["bc_psum"], 4 * b + c + 1)
                nc.scalar.activation(parts[:, c * CHUNK:(c + 1) * CHUNK], banks(2 * (c % 2), 2, slice(0, 96)),
                                     ACT.Copy).then_inc(pr["hi_done"], 1)

            def middle(c):
                act.wait_ge(pr["r_read"], 4 * b + c + 1)
                nc.scalar.activation(parts[0:DI, c * CHUNK:(c + 1) * CHUNK], resid(c)[0:DI, :], ACT.Copy).then_inc(pr["mid_done"], 1)

            def exp(c):
                act.wait_ge(pr["clamp_done"], 4 * b + c + 1)
                cols = slice(c * CHUNK, (c + 1) * CHUNK)
                nc.scalar.activation(log_tmps[b][:, cols], log_tmps[b][:, cols], ACT.Exp).then_inc(pr["exp_done"], 1)

            def log(c):
                act.wait_ge(pr["exp_done"], 4 * b + c + 1)
                cols = slice(c * CHUNK, (c + 1) * CHUNK)
                nc.scalar.activation(log_tmps[b][:, cols], log_tmps[b][:, cols], ACT.Ln, bias=1.0).then_inc(pr["log_done"], 1)

            for n in range(4):
                gated(n)
            between(0)
            for n in range(4, 8):
                gated(n)
            exp(0), exp(1), high(0), exp(2), high(1)
            between(1)
            middle(0), high(2), exp(3), middle(1), log(0)
            between(2)
            high(3), middle(2), log(1), log(2), middle(3), log(3)
            between(3)

        def project_vector(v, b, between=nothing):
            def preactivation(c):
                cols = slice(c * CHUNK, (c + 1) * CHUNK)
                v.wait_ge(pr["dt_psum"], 4 * b + c + 1)
                if b == 1 and c == 0:
                    v.wait_ge(l3["table_in"], 16)
                nc.vector.tensor_scalar(log_tmps[b][:, cols], banks(4, 2), V(V_BDT), 20.0, ALU.add, ALU.min).then_inc(pr["clamp_done"], 1)
                nc.vector.tensor_scalar(dl[:, cols], banks(4, 2), bdt20[:, :], 0.0, ALU.add, ALU.max).then_inc(pr["v_ready"], 1)

            def left(c):
                v.wait_ge(pr["hi_done"], 4 * b + c + 1)
                if c >= 2:
                    v.wait_ge(pr["mid_done"], 4 * b + c - 1)
                    v.wait_ge(pr["parts_ready"], 4 * b + c - 1)
                nc.vector.tensor_tensor(resid(c)[0:DI, :], banks(2 * (c % 2), 2, slice(0, DI)),
                                        parts[0:DI, c * CHUNK:(c + 1) * CHUNK], ALU.subtract).then_inc(pr["r_read"], 1)

            def low(c):
                rows = parts[0:32, c * CHUNK:(c + 1) * CHUNK]
                v.wait_ge(pr["mid_done"], 4 * b + c + 1)
                nc.vector.tensor_tensor(rows, resid(c)[0:32, :], rows, ALU.subtract).then_inc(pr["parts_ready"], 1)

            preactivation(0)
            between(0)
            preactivation(1), preactivation(2), left(0), preactivation(3), left(1)
            between(1)
            low(0), left(2), low(1)
            between(2)
            if b == 0:
                project_delta(v, 0, 0)
                left(3), low(2)
                helped_du(v, 0)
                low(3)
            else:
                left(3), low(2), low(3)
                for c in range(NCHUNK):
                    project_delta(v, 1, c)
            between(3)


        def broadcast(pe, i, j, which, first, waited):
            i, j = i + j // PAIRS, j % PAIRS
            if waited:
                pe.wait_ge(*waited)
            for n in range(2):
                last = nc.tensor.matmul(PS[:, first + n, :], selb[:, which, j, :],
                                        parts[:, bass.ds(i * CHUNK + n * BANK, BANK)], start=True, stop=True)
            last.then_inc(sc["c_psum" if which else "b_psum"], 1)

        def start_y(pe, i, c):
            pe.wait_ge(sc["y_used"], c + 1)
            for n in range(2):
                nc.tensor.matmul(PS[:, 4 + n, :], diagD[:, :], u[:, bass.ds(i * CHUNK + n * BANK, BANK)],
                                 start=True, stop=False)

        def add_states(pe, c, j):
            pe.wait_ge(sc["hc_done"], c * PAIRS + (j + 2))
            for n in range(2):
                last = nc.tensor.matmul(PS[:, 4 + n, :], wt[:, W_SUM:W_SUM + P], dBC[:, j % 2, n * BANK:(n + 1) * BANK],
                                        start=False, stop=(j == PAIRS - 1))
            last.then_inc(sc["y_done"], 1)

        def scan_tensor(pe, i, c, between=nothing, ends=False):
            for j in range(PAIRS):
                s = c * PAIRS + j
                if j in TURN_AFTER:
                    between(TURN_AFTER.index(j))
                broadcast(pe, i, j, 1, 2, (sc["hc_done"], s + 1))
                if not ends or j + 1 < PAIRS:
                    broadcast(pe, i, j + 1, 0, 0, (sc["b_used"], s + 2))
                if j:
                    add_states(pe, c, j - 1)
                else:
                    start_y(pe, i, c)
            add_states(pe, c, PAIRS - 1)

        def scan_scalar(act, i, c, between=nothing):
            for j in range(PAIRS):
                s = c * PAIRS + j
                act.wait_ge(sc["h_done"], s + 1)
                act.nop(nofuse=True)
                nc.scalar.activation(dA[:, j % 2, :], dl[:, bass.ds(i * CHUNK, CHUNK)], ACT.Exp,
                                     scale=negA[:, j:j + 1]).then_inc(sc["exp_done"], 1)
                if j in TURN_AFTER:
                    between(TURN_AFTER.index(j))

        def gate(v, tok, c):
            v.wait_ge(sc["y_done"], c * PAIRS + (PAIRS + 2))
            nc.vector.tensor_tensor(zy[:, tok], banks(4, 2), zy[:, tok], ALU.mult).then_inc(sc["y_used"], 1)

        def scan_vector(v, i, c, between=nothing):
            tok = bass.ds(i * CHUNK, CHUNK)
            vchain(v, nc.vector.tensor_tensor(du, dl[:, tok], u[:, tok], ALU.mult))
            for j in range(PAIRS):
                s = c * PAIRS + j
                slot = dBC[:, j % 2, :]
                v.wait_ge(sc["b_psum"], s + 1)
                v.wait_ge(sc["y_done"], s + 1)
                tell(v, nc.vector.tensor_tensor(slot, du, banks(0, 2), ALU.mult), sc["b_used"], s + 2)
                v.wait_ge(sc["exp_done"], s + 1)
                v.wait_ge(sc["hc_done"], s + 1)
                tell(v, nc.vector.tensor_tensor_scan(hs, dA[:, j % 2, :], slot, carry[:, j:j + 1], ALU.mult, ALU.add),
                     sc["h_done"], s + 3)
                nc.vector.tensor_copy(carry[:, j:j + 1], hs[:, CHUNK - 1:CHUNK])
                v.wait_ge(sc["c_psum"], s + 1)
                nc.vector.tensor_tensor(slot, hs, banks(2, 2), ALU.mult).then_inc(sc["hc_done"], 1)
                if j in TURN_AFTER:
                    between(TURN_AFTER.index(j))
            gate(v, tok, c)


        def helped_tensor(pe, c, ends=False):
            for j in range(PAIRS):
                s = c * PAIRS + j
                if not ends or j + 1 < PAIRS:
                    broadcast(pe, c, j + 1, 1, (6, 2)[j % 2], (sc["hc_done"], s + 1))
                if j == 0:
                    start_y(pe, c, c)
                if not ends or j + 2 < PAIRS:
                    broadcast(pe, c, j + 2, 0, 0, (sc["b_used"], s + 3))
                add_states(pe, c, j)

        def helped_scalar(act, c):
            act.wait_ge(pr["delta_ready"], c + 1)
            for j in range(PAIRS):
                s = c * PAIRS + j
                act.wait_ge(sc["dbu_done"], s + 1)
                act.wait_ge(sc["b_psum"], s + 1)
                nc.scalar.activation(Bs[j % 2], banks(0, 2), ACT.Copy).then_inc(sc["b_used"], 1)
                act.wait_ge(sc["h_done"], s + 1)
                act.nop(nofuse=True)
                nc.scalar.activation(dA[:, j % 2, :], dl[:, bass.ds(c * CHUNK, CHUNK)], ACT.Exp,
                                     scale=negA[:, j:j + 1]).then_inc(sc["exp_done"], 1)

        def helped_gpsimd(pool, c):
            pool.wait_ge(sc["du_done"], c + 1)
            for j in range(PAIRS):
                s = c * PAIRS + j
                pool.wait_ge(sc["b_used"], s + 2)
                pool.wait_ge(sc["h_done"], s + 1)
                nc.gpsimd.tensor_tensor(dBu[j % 2], du, Bs[j % 2], ALU.mult).then_inc(sc["dbu_done"], 1)

        def helped_du(v, c):
            v.wait_ge(pr["delta_ready"], c + 1)
            v.nop(nofuse=True)
            nc.vector.tensor_tensor(du, dl[:, bass.ds(c * CHUNK, CHUNK)], u[:, bass.ds(c * CHUNK, CHUNK)],
                                    ALU.mult).then_inc(sc["du_done"], 1)

        def helped_vector(v, c, ends=False):
            for j in range(PAIRS):
                s = c * PAIRS + j
                v.wait_ge(sc["dbu_done"], s + 3)
                v.wait_ge(sc["exp_done"], s + 1)
                v.wait_ge(sc["hc_done"], s + 1)
                tell(v, nc.vector.tensor_tensor_scan(hs, dA[:, j % 2, :], dBu[j % 2], carry[:, j:j + 1], ALU.mult, ALU.add),
                     sc["h_done"], s + 3)
                nc.vector.tensor_copy(carry[:, j:j + 1], hs[:, CHUNK - 1:CHUNK])
                v.wait_ge(sc["c_psum"], s + 1)
                v.wait_ge(sc["y_done"], s + 1)
                nc.vector.tensor_tensor(dBC[:, j % 2, :], hs, banks((2, 6)[j % 2], 2), ALU.mult).then_inc(sc["hc_done"], 1)
                if j == 3 and not ends:
                    project_delta(v, 0, c + 1)
            if not ends:
                helped_du(v, c + 1)
            gate(v, bass.ds(c * CHUNK, CHUNK), c)


        def output_tensor(pe, b):
            for h, n in ((0, 0), (0, 1), (0, 2), (0, 3), (1, 0), (1, 1), (1, 2), (1, 3)):
                if (h, n) == (0, 0):
                    pe.wait_ge(sc["hc_done"], NCHUNK * PAIRS * (b + 1) + 1)
                if (h, n) == (1, 2):
                    pe.wait_ge(sc["y_used"], NCHUNK * (b + 1) + 1)
                q = 2 * b + h
                last = nc.tensor.matmul(PS[32 * q:32 * q + 32, n, :], wt[:, W_OUT:W_OUT + C],
                                        zy[:, h * HALF + n * BANK:h * HALF + (n + 1) * BANK], start=True, stop=True)
                if h == 1:
                    last.then_inc(sc["o_psum"], 1)

        def output_vector(v, b):
            rows = slice(64 * b, 64 * b + 64)
            for n in range(4):
                cols = slice(n * BANK, (n + 1) * BANK)
                v.wait_ge(sc["o_psum"], 4 * b + n + 1)
                vchain(v, nc.vector.tensor_tensor(X[rows, cols], X[rows, cols], PS[rows, n, :], ALU.add))
                gn_bank_stats(v, n, rows)


        def prepare(b):
            rows = slice(64 * b, 64 * b + 64)
            n = GROUPS * TAPS
            G3, tab = G3s[b], tabs[b]

            def temp(first, count):
                return temps[b][:, first:first + count]

            g4 = temp(0, HALF)
            bases, yx, corner0 = (temp(HALF + 2 * n * k, 2 * n).rearrange("p (g k) -> p g k", k=2 * TAPS) for k in range(3))
            msk = temp(HALF + 6 * n, n).rearrange("p (g k) -> p g k", k=TAPS)
            om = scratch[:, 8 * CHUNK:9 * CHUNK].rearrange("p (g k) -> p g k", k=32)
            hat = temp(0, 4 * n).rearrange("p (r g k) -> p r g k", r=2, k=2 * TAPS)
            cm = temp(4 * n, 2 * n).rearrange("p (r g k) -> p r g k", r=2, k=TAPS)

            def sync(sp):
                sp.wait_ge(l3["zeroed"], b + 1)
                sp.dma_start(bases.rearrange("p g k -> p (g k)"), base).then_inc(l3["base_in"], 16)
                sp.wait_ge(l3["g_ready"], b + 1)
                for h in range(2):
                    for j in range(3):
                        first = W + h * HALF - (j - 1)
                        sp.dma_start(G3[32 * j:32 * j + 32, first:first + HALF],
                                     g4[64 * b + 32 * h:64 * b + 32 * h + 32, :]).then_inc(l3["g3_in"], 16)
                sp.wait_ge(l3["corner_ready"], b + 1)
                sp.wait_ge(l3["below_ready"], b + 1)
                sp.dma_start(tables[b].rearrange("(y x) n -> y (x n)", y=H),
                             tab[rows, :, :, :].rearrange("p x k c -> p (x k c)")).then_inc(l3["table_in"], 16)
                sp.wait_ge(l3["off_psum"], b + 1)
                for h in range(2):
                    q = 2 * b + h
                    sp.dma_start(G3[0:C, h * HALF:(h + 1) * HALF], X[32 * q:32 * q + 32, :]).then_inc(l3["resid_in"], 16)
                sp.wait_ge(l3["table_in"], 16 * (b + 1))

            def tensor(pe, between=nothing):
                pe.wait_ge(l3["stats"], b + 1)
                nc.tensor.matmul(PS[rows, 0, 0:2], M(M_OWN, rows, rows), S2[rows, :], start=True, stop=True).then_inc(l3["totals"], 1)
                pe.wait_ge(l3["corner_ready"], b + 1)
                for n in range(4):
                    nc.tensor.matmul(PS[rows, n, :], M(M_DOWN, cols=rows), tab[:, 16 * n:16 * n + 16, 0, :],
                                     start=True, stop=True).then_inc(l3["shift_done"], 1)
                between(0)
                pe.wait_ge(l3["g3_ready"], b + 1)
                for n in range(2):
                    for q in range(4):
                        for dy in range(3):
                            first = q * QUARTER + n * BANK + dy * W
                            last = nc.tensor.matmul(PS[32 * q:32 * q + 32, 4 + n, :], wt[0:96, W_OFF + 32 * dy:W_OFF + 32 * dy + 32],
                                                    G3[:, first:first + BANK], start=(dy == 0), stop=(dy == 2))
                last.then_inc(l3["off_psum"], 1)
                between(1)
                between(2)

            def scalar(act, between=nothing):
                act.wait_ge(l3["sqrt_go"], b + 1)
                nc.scalar.activation(std[rows, 0:1], std[rows, 0:1], ACT.Sqrt).then_inc(l3["sqrt_done"], 1)
                for n in range(4):
                    act.wait_ge(l3["shift_done"], 4 * b + n + 1)
                    nc.scalar.activation(tab[rows, 16 * n:16 * n + 16, 2, :], PS[rows, n, :].rearrange("p (x c) -> p x c", c=C),
                                         ACT.Copy).then_inc(l3["below_in"], 1)
                between(0)
                between(1)
                act.wait_ge(l3["mask_in"], b + 1)
                nc.scalar.activation(msk, msk, ACT.Exp, scale=-1.0).then_inc(l3["mask_exp"], 1)
                between(2)

            def vector(v, between=nothing):
                vchain(v, nc.vector.memset(G3[:, 0:W], 0.0))
                tell(v, nc.vector.memset(G3[:, GLEN - W:GLEN], 0.0), l3["zeroed"], b + 1)
                gn_partition_stats(v, rows, banks_done=True).then_inc(l3["stats"], 1)
                v.wait_ge(l3["totals"], b + 1)
                vchain(v, nc.vector.tensor_copy(tot[rows, 0:2], PS[rows, 0, 0:2]))
                variance(v, 1, GN_EPS, rows).then_inc(l3["sqrt_go"], 1)
                v.wait_ge(l3["sqrt_done"], b + 1)
                vchain(v, nc.vector.reciprocal(rstd[rows, 0:1], std[rows, 0:1]))
                vchain(v, nc.vector.scalar_tensor_tensor(nmrs[rows, :], tot[rows, 0:1], -1.0, rstd[rows, 0:1], ALU.mult, ALU.mult))
                tell(v, nc.vector.tensor_scalar(g4[rows, :], X[rows, :], rstd[rows, 0:1], nmrs[rows, :], ALU.mult, ALU.add),
                     l3["g_ready"], b + 1)
                vchain(v, nc.vector.memset(tab[rows, W - 1, 1::2, :], 0.0))
                vchain(v, nc.vector.memset(tab[64 - 64 * b:P - 64 * b, :, 0, :], 0.0))
                vchain(v, nc.vector.transpose(tab[rows, :, 0, :], g4[rows, :].rearrange("p (y x) -> p x y", x=W)))
                tell(v, nc.vector.tensor_copy(tab[rows, 0:W - 1, 1, :], tab[rows, 1:W, 0, :]), l3["corner_ready"], b + 1)
                between(0)
                cols = G3.rearrange("p (y x) -> p y x", x=W)
                v.wait_ge(l3["g3_in"], 96 * (b + 1))
                vchain(v, nc.vector.memset(cols[0:32, :, 0], 0.0))
                tell(v, nc.vector.memset(cols[64:96, :, W - 1], 0.0), l3["g3_ready"], b + 1)
                v.wait_ge(l3["below_in"], 4 * b + 4)
                nc.vector.tensor_copy(tab[rows, 0:W - 1, 3, :], tab[rows, 1:W, 2, :]).then_inc(l3["below_ready"], 1)
                v.wait_ge(l3["base_in"], 16 * (b + 1))
                v.wait_ge(l3["off_psum"], b + 1)
                vchain(v, nc.vector.transpose(om.rearrange("p g k -> p (g k)"), banks(4, 2)))
                vchain(v, nc.vector.tensor_tensor(yx, om[:, :, 0:18], bases, ALU.add))
                tell(v, nc.vector.tensor_copy(msk, om[:, :, 18:27]), l3["mask_in"], b + 1)
                between(1)
                vchain(v, nc.vector.tensor_scalar(corner0, yx, 0.5, 0.0, ALU.subtract, ALU.max))
                vchain(v, nc.vector.tensor_scalar(corner0, corner0, float(H - 2), ROUND, ALU.min, ALU.add))
                vchain(v, nc.vector.tensor_scalar(corner0, corner0, ROUND, None, ALU.subtract))
                gs = slice(b * GROUPS, (b + 1) * GROUPS)
                vchain(v, nc.vector.scalar_tensor_tensor(
                    idx_all[:, b * n:(b + 1) * n].rearrange("p (g k) -> p g k", k=TAPS),
                    corner0[:, :, 0::2], float(W), corner0[:, :, 1::2], ALU.mult, ALU.add))
                nc.vector.memset(prime[:, 12 + b:13 + b], 0.0).then_inc(l3["idx_ready"], 1)
                vchain(v, nc.vector.tensor_tensor(hat[:, 0, :, :], yx, corner0, ALU.subtract))
                vchain(v, nc.vector.tensor_scalar(hat[:, 1, :, :], hat[:, 0, :, :], 1.0, None, ALU.subtract))
                flat = hat.rearrange("p r g k -> p (r g k)")
                vchain(v, nc.vector.scalar_tensor_tensor(flat, flat, -1.0, flat, ALU.mult, ALU.min))
                vchain(v, nc.vector.tensor_scalar(flat, flat, 1.0, 0.0, ALU.add, ALU.max))
                v.wait_ge(l3["mask_exp"], b + 1)
                vchain(v, nc.vector.tensor_scalar(msk, msk, 1.0, None, ALU.add))
                vchain(v, nc.vector.reciprocal(msk, msk))
                for r in range(2):
                    vchain(v, nc.vector.tensor_tensor(cm[:, r, :, :], hat[:, r, :, 0::2], msk, ALU.mult))
                    for s in range(2):
                        vchain(v, nc.vector.tensor_tensor(coef[:, gs, :, 2 * r + s], cm[:, r, :, :], hat[:, s, :, 1::2], ALU.mult))
                between(2)

            return sync, tensor, scalar, vector

        prep = [prepare(b) for b in range(B)]
        TURN_AFTER = (0, 2, 3, 5, 7)
        TURNS = len(TURN_AFTER)
        IN_SCAN = 4
        IN_PREPARE = IN_SCAN + NCHUNK * TURNS
        REST = GROUPS + 2
        assert TURNS == SLOTS and (B * GROUPS - REST) % SLOTS == 0
        EARLY = 28

        with nc.Block() as block:
            @block.sync
            def _(sp):
                load_tokens(sp, 0, 1, range(4))
                for h in range(2):
                    load_tokens(sp, 1, h, range(4))
                for b in range(B):
                    prep[b][0](sp)
                for b in range(B):
                    for first, last in ((0, EARLY), (EARLY, GROUPS)):
                        sp.wait_ge(l3["o_read"], GROUPS * b + last + 1)
                        to, source = (t.rearrange("c (q n) -> c q n", q=4)[:, :, 32 * first:32 * last]
                                      for t in (out[b].rearrange("c y x -> c (y x)"), G3s[b][0:C, 0:L]))
                        sp.dma_start(to, source).then_inc(l3["out_dma"], 16)
                sp.wait_ge(l3["out_dma"], 16 * 2 * B)

            @block.gpsimd
            def _(pool):
                with nc.gpsimd.Fori(0, NCHUNK) as i:
                    helped_gpsimd(pool, i)
                for b in range(B):
                    first = b * GROUPS
                    pool.wait_ge(l3["table_in"], 16 * (b + 1))
                    pool.wait_ge(l3["idx_ready"], b + 1)
                    for G in range(first, first + SLOTS):
                        group_gather(pool, b, G, G % SLOTS, idx_all[:, G * TAPS:(G + 1) * TAPS])
                    turns = GROUPS // SLOTS - 1
                    with nc.gpsimd.Fori(0, turns) as i:
                        for k in range(SLOTS):
                            slot = (first + k) % SLOTS
                            group_gather(pool, b, i * SLOTS + (first + SLOTS + k), slot, idx_slot[:, slot, :])
                    for G in range(first + SLOTS * (turns + 1), first + GROUPS):
                        group_gather(pool, b, G, G % SLOTS, idx_slot[:, G % SLOTS, :])

            @block.tensor
            def _(pe):
                project_tensor(pe, 0)
                pe.wait_ge(pr["parts_ready"], 1)
                broadcast(pe, 0, 0, 0, 0, (pr["r_read"], 3))
                pe.wait_ge(pr["parts_ready"], 4)
                broadcast(pe, 0, 1, 0, 0, (sc["b_used"], 2))
                broadcast(pe, 0, 0, 1, 2, None)
                with nc.tensor.Fori(0, NCHUNK - 1) as i:
                    helped_tensor(pe, i)
                helped_tensor(pe, NCHUNK - 1, ends=True)
                output_tensor(pe, 0)
                prep[0][1](pe)
                project_tensor(pe, 1, lambda k: tensor_turn(pe, k))
                pe.wait_ge(pr["parts_ready"], 8)
                broadcast(pe, 0, 0, 0, 0, (sc["b_used"], NCHUNK * PAIRS + 1))
                with nc.tensor.Fori(0, NCHUNK - 1) as i:
                    scan_tensor(pe, i, i + NCHUNK, lambda k: tensor_turn_in_loop(
                        pe, 0, i * TURNS + (IN_SCAN + k), i * TURNS + (IN_SCAN + k)))
                scan_tensor(pe, NCHUNK - 1, 2 * NCHUNK - 1, lambda k: tensor_turn(pe, IN_PREPARE - TURNS + k), ends=True)
                output_tensor(pe, 1)
                prep[1][1](pe, lambda k: tensor_turn(pe, IN_PREPARE + k))
                for G in range(IN_PREPARE + 3, REST):
                    tensor_turn(pe, G)
                pe.wait_ge(l3["resid_in"], 32 * B)
                with nc.tensor.Fori(0, (B * GROUPS - REST) // SLOTS) as i:
                    for k in range(SLOTS):
                        tensor_turn_in_loop(pe, 1, i * SLOTS + (REST + k), i * SLOTS + (REST - GROUPS + k))
                for G in range(B * GROUPS, B * GROUPS + 2):
                    tensor_turn(pe, G)

            @block.scalar
            def _(act):
                project_scalar(act, 0)
                with nc.scalar.Fori(0, NCHUNK) as i:
                    helped_scalar(act, i)
                prep[0][2](act)
                project_scalar(act, 1, lambda k: scalar_turn(act, k))
                act.wait_ge(pr["delta_ready"], 8)
                with nc.scalar.Fori(0, NCHUNK) as i:
                    scan_scalar(act, i, i + NCHUNK, lambda k: scalar_turn_in_loop(
                        act, 0, i * TURNS + (IN_SCAN + k), i * TURNS + (IN_SCAN + k)))
                prep[1][2](act, lambda k: scalar_turn(act, IN_PREPARE + k))
                for G in range(IN_PREPARE + 3, REST):
                    scalar_turn(act, G)
                with nc.scalar.Fori(0, (B * GROUPS - REST) // SLOTS) as i:
                    for k in range(SLOTS):
                        scalar_turn_in_loop(act, 1, i * SLOTS + (REST + k), i * SLOTS + (REST - GROUPS + k))
                scalar_turn(act, B * GROUPS)
                scalar_turn(act, B * GROUPS + 1)

            @block.vector
            def _(v):
                nc.vector.memset(idx_all[:, GROUPS * TAPS:], 0)
                nc.vector.memset(colg[:, :], 0.0)
                for k, (signal, n) in enumerate((
                        (sc["h_done"], 2), (sc["hc_done"], 1), (sc["y_done"], 2), (sc["y_used"], 1), (sc["b_used"], 1),
                        (sc["dbu_done"], 2),
                        (l3["prod_done"], SLOTS), (l3["t_psum"], 1), (l3["t_read"], 1), (l3["o_psum"], 1), (l3["o_read"], 1))):
                    nc.vector.memset(prime[:, k:k + 1], 0.0).then_inc(signal, n)
                vchain(v, nc.vector.memset(carry[:, :], 0.0))
                project_vector(v, 0)
                v.wait_ge(pr["parts_ready"], 4)
                with nc.vector.Fori(0, NCHUNK - 1) as i:
                    helped_vector(v, i)
                helped_vector(v, NCHUNK - 1, ends=True)
                output_vector(v, 0)
                prep[0][3](v)
                project_vector(v, 1, lambda k: vector_turn(v, k))
                vchain(v, nc.vector.memset(carry[:, :], 0.0))
                v.wait_ge(pr["delta_ready"], 8)
                v.wait_ge(pr["parts_ready"], 8)
                with nc.vector.Fori(0, NCHUNK) as i:
                    vchain.enter(i, 1)

                    def turn(k):
                        G = i * TURNS + (IN_SCAN + k)
                        group_weigh(v, G, (IN_SCAN + k) % SLOTS, i + (IN_SCAN + k) // SLOTS)

                    scan_vector(v, i, i + NCHUNK, turn)
                vchain.leave(NCHUNK)
                output_vector(v, 1)
                prep[1][3](v, lambda k: vector_turn(v, IN_PREPARE + k))
                for G in range(IN_PREPARE + 3, REST):
                    vector_turn(v, G)
                with nc.vector.Fori(0, (B * GROUPS - REST) // SLOTS) as i:
                    for k in range(SLOTS):
                        G = i * SLOTS + (REST + k)
                        group_weigh(v, G, (REST + k) % SLOTS, i + (REST + k) // SLOTS)



def _square_constants():
    m = np.zeros((NMAT, P, P), np.float32)
    i = np.arange(P)
    m[M_IDENT] = np.eye(P)
    same_channel = i[:, None] % C == i[None, :] % C
    m[M_OWN] = 0.5 * (same_channel & (i[:, None] // 64 == i[None, :] // 64))
    m[M_PRE] = 0.5 * (same_channel & (i[:, None] // 64 == 1))
    same_quadrant = i[:, None] // C == i[None, :] // C
    m[M_PAIR] = 0.5 * (same_quadrant & (i[:, None] // 2 == i[None, :] // 2))
    m[M_MEAN] = same_quadrant / C
    m[M_CENTER] = m[M_IDENT] - m[M_MEAN]
    for b in range(B):
        for y in range(H):
            o = H * b + y
            m[M_LAP, o, o] = 4.0
            for s in (y - 1, y + 1):
                if 0 <= s < H:
                    m[M_LAP, H * b + s, o] = -1.0
            m[M_DOWN, H * b + (y + 1 if y < H - 1 else H - 2), o] = 1.0
            m[M_UPR, H * b + (y - 1 if y else 1), o] = 1.0
            if y:
                m[M_UP, o - 1, o] = 1.0
            else:
                m[M_UP0, o, o] = 1.0
        m[M_PICKB, b, H * b:H * b + H] = 1.0
    return np.ascontiguousarray(m.transpose(1, 0, 2))


def _bicubic_weights(out_size, in_size):
    f = np.float32
    src = (np.arange(out_size, dtype=f) + f(0.5)) * f(in_size / out_size) - f(0.5)
    i0 = np.floor(src)
    at = np.abs((src - i0)[:, None] - np.arange(-1, 3).astype(f)[None, :])
    a = f(-0.75)
    near = ((a + f(2)) * at - (a + f(3))) * at * at + f(1)
    far = (((at - f(5)) * at + f(8)) * at - f(4)) * a
    w = np.where(at <= 1, near, np.where(at < 2, far, f(0))).astype(f)
    idx = np.clip(i0[:, None].astype(np.int32) + np.arange(-1, 3)[None, :], 0, in_size - 1)
    m = np.zeros((out_size, in_size), f)
    np.add.at(m, (np.arange(out_size)[:, None], idx), w)
    return m


def _bicubic_rows():
    wy = _bicubic_weights(3 * H, 4)[H // 2:H // 2 + H]
    wx = _bicubic_weights(3 * W, 4)[W // 2:W // 2 + W]
    k = (wy.T[:, None, :, None] * wx.T[None, :, None, :]).reshape(16, L)
    replaced = (5 + 1 - 4) * 4 + (6 + 1 - 5)
    rows = np.zeros((64, HALF), np.float32)
    for h in range(2):
        part = k[:, h * HALF:(h + 1) * HALF]
        rows[h] = part[replaced]
        rows[32 + 16 * h:48 + 16 * h] = part
        rows[32 + 16 * h + replaced] = 0.0
    rows[2] = 1.0
    return rows


def _sample_base():
    p = np.arange(P)[:, None, None]
    g = np.arange(GROUPS)[None, :, None]
    k = np.arange(TAPS)[None, None, :]
    pixel = p // 32 * QUARTER + 32 * g + p % 32
    y = pixel // W - 1 + k // 3
    x = pixel % W - 1 + k % 3
    return np.ascontiguousarray(np.stack([y, x], axis=-1).astype(np.float32).reshape(P, GROUPS * TAPS * 2))


def _selectors():
    s = np.zeros((96, 2, PAIRS, 2, DI), np.float32)
    for part in range(3):
        for j in range(PAIRS):
            for h in range(2):
                s[32 * part + 2 * j + h, 0, j, h] = 1.0
                s[32 * part + 16 + 2 * j + h, 1, j, h] = 1.0
    return s.reshape(96, 2 * PAIRS * P)


def kernel(**inputs):
    import concourse.bacc as _bacc
    from concourse.bass_utils import run_bass_kernel_spmd as _run

    a = {k: np.asarray(v) for k, v in inputs.items()}
    rep = lambda v, n: np.tile(np.reshape(v, -1), n)
    vecs = np.zeros((P, NV), np.float32)
    for col, v in ((V_W0, rep(a["L0_conv_weight"], 4)), (V_B0, rep(a["L0_conv_bias"], 4)),
                   (V_GNW, rep(a["L1_conv_gn_weight"], 4)), (V_GNB, rep(a["L1_conv_gn_bias"], 4)),
                   (V_B1, rep(a["L1_conv_b1"], 2)), (V_B2, rep(a["L1_conv_b2"], 4)),
                   (V_LNW, rep(a["L2_conv_ln_w"], 4)), (V_LNB, rep(a["L2_conv_ln_b"], 4)),
                   (V_CB, rep(a["L2_conv_conv_b"], 2)), (V_BDT, rep(a["L2_conv_b_dt"], 2)),
                   (V_D, rep(a["L2_conv_D"], 2))):
        vecs[:, col] = v
    vecs[:, V_A:V_A + PAIRS] = a["L2_conv_A_log"].reshape(DI, PAIRS, 2).transpose(2, 0, 1).reshape(P, PAIRS)
    vecs[0:32, V_M3] = vecs[32:64, V_M3 + 1] = vecs[64:128, V_M3 + 2] = 1.0
    vecs[:, V_EPS] = GN_EPS
    vecs[32:48, V_HALF] = vecs[48:64, V_HALF + 1] = 1.0

    w = np.zeros((P, NW), np.float32)
    for q in range(4):
        r = q % 2
        first = W_ONE + 128 * (q // 2) + 64 * r
        w[32 * q:32 * q + 32, first:first + 64] = a["L1_conv_w1"].T
    for q in range(2):
        w[64 * q:64 * q + 64, W_TWO + 32 * q:W_TWO + 32 * q + 32] = a["L1_conv_w2"].T
    for j in range(4):
        for d in range(2):
            w[32 * j:32 * j + 32, W_INX + 64 * d:W_INX + 64 * d + 64] = a["L2_conv_W_in"][:DI].T
            w[32 * j:32 * j + 32, W_CONV + 64 * d:W_CONV + 64 * d + 64] = a["L2_conv_conv_w"][:, j]
    for d in range(2):
        w[96:128, W_INZ + 64 * d:W_INZ + 64 * d + 64] = a["L2_conv_W_in"][DI:].T
    for part in range(3):
        w[0:64, W_BC + 32 * part:W_BC + 32 * part + 32] = a["L2_conv_W_xproj"][2:].T
    w[0:2, W_DTA:W_DTA + 64] = a["L2_conv_W_xproj"][0:2]
    for d in range(2):
        w[0:2, W_DTB + 64 * d:W_DTB + 64 * d + 64] = a["L2_conv_W_dt"].T
        for m in range(2):
            w[64 * d:64 * d + 64, W_SUM + 64 * m:W_SUM + 64 * m + 64] = np.eye(DI)
    w[0:64, W_OUT:W_OUT + 32] = a["L2_conv_W_out"].T
    taps = np.concatenate([a["L3_conv_offset_w"], a["L3_conv_mask_w"]], axis=0)
    for dy in range(3):
        w[0:96, W_OFF + 32 * dy:W_OFF + 32 * dy + 27] = taps[:, :, dy].transpose(2, 1, 0).reshape(96, 27)
    l3 = a["L3_conv_weight"].reshape(C, C, TAPS).transpose(2, 1, 0)
    for r in range(3):
        w[:, W_L3 + C * r:W_L3 + C * r + C] = np.repeat(l3[2 * r:2 * r + 2, None], 2, axis=1).reshape(P, C)
    w[0:96, W_L3 + 3 * C:W_L3 + 4 * C] = l3[6:9].reshape(96, C)

    anchors = np.zeros((32, 2, C), np.float32)
    for s, name in enumerate(("L0_conv_mean_table", "L0_conv_std_table")):
        for h in range(2):
            anchors[16 * h:16 * h + 16, s] = a[name][3:7, 4:8].reshape(16, C)

    arrays = {"x": np.ascontiguousarray(a["x"]), "mats": _square_constants(), "vecs": vecs, "wts": w,
              "bic": _bicubic_rows(), "anchors": anchors, "base": _sample_base(), "sel": _selectors()}
    nc = _bacc.Bacc("TRN2", target_bir_lowering=False, num_devices=1)
    args = [nc.dram_tensor(f"in_{k}", v.shape, F32, kind="ExternalInput").ap() for k, v in arrays.items()]
    args.append(nc.dram_tensor("out_x", (B, C, H, W), F32, kind="ExternalOutput").ap())
    build(nc, *args)
    r = _run(nc, [{f"in_{k}": v for k, v in arrays.items()}], core_ids=[0])
    return r.results[0]["out_x"]
```
